# Optimizing a Trainium2 kernel written in Bass

```python
import numpy as np
import jax
import jax.numpy as jnp

def _softmax(x, axis=-1):
    return jax.nn.softmax(x, axis=axis)

def _gelu(x):
    return jax.nn.gelu(x, approximate=True)

def _silu(x):
    return jax.nn.silu(x)

def _sigmoid(x):
    return jax.nn.sigmoid(x)

def _layernorm(x, axis=-1, eps=1e-05):
    m = jnp.mean(x, axis=axis, keepdims=True)
    v = jnp.var(x, axis=axis, keepdims=True)
    return (x - m) / jnp.sqrt(v + eps)

def _scatter_add(tgt, idx, src, axis=0):
    return tgt.at[idx].add(src)

def _segment_sum(src, seg, n):
    return jax.ops.segment_sum(src, seg, n)
kernel_name = 'mk_flamingo_gated_d2_seqx_r8_64de3c'

def setup_inputs(seed: int=0):
    np.random.seed(seed)
    _w = jnp.asarray

    def _rec_inputs():
        import jax
        import jax.numpy as jnp
        _rk = jax.random.key(seed)
        x = -0.0005207 + 1.001 * jax.random.normal(jax.random.fold_in(_rk, 1), (2, 256, 128), jnp.float32)
        _lenS = 256 - jax.random.randint(jax.random.fold_in(_rk, 7), (2,), 0, max(1, 256 // 4) + 1, jnp.int32)
        _lenS2 = 512 - jax.random.randint(jax.random.fold_in(_rk, 8), (2,), 0, max(1, 512 // 4) + 1, jnp.int32)
        _ctx_1024P = jax.random.normal(jax.random.fold_in(_rk, 11), (2, 16, 128), jnp.float32)
        _ctx_1024c = jax.random.dirichlet(jax.random.fold_in(_rk, 511), 0.3 * jnp.ones((16,), jnp.float32), (2, 512))
        _ctx_1024t = jnp.einsum('bsk,bkd->bsd', _ctx_1024c, _ctx_1024P)
        _ctx_1024t = _ctx_1024t * jax.lax.rsqrt(jnp.mean(jnp.square(_ctx_1024t)) + 1e-12) * 0.953939
        ctx_1024 = 2.81802e-05 + 1.00001 * (_ctx_1024t + 0.3 * jax.random.normal(jax.random.fold_in(_rk, 611), (2, 512, 128), jnp.float32))
        _g = jax.random.normal(jax.random.fold_in(_rk, 9001), (2, 2), jnp.float32)
        _g = jnp.sign(_g) * jnp.maximum(jnp.abs(_g), 1.0) + (_g == 0) * 1.0
        g_xattn = _g[0]
        g_ffn = _g[1]
        return (x, ctx_1024, g_xattn, g_ffn)
    x, ctx_1024, g_xattn, g_ffn = _rec_inputs()

    def _L0_xattn_setup():
        import jax, jax.numpy as jnp
        import numpy as np
        E = 128
        H = 16
        D = E // H
        key = jax.random.key(seed)
        ks = jax.random.split(key, 12)
        B, Tq, Tk = (2, 128, 1024)
        s = 0.02
        return {'hidden_states': jax.random.normal(ks[0], (B, Tq, E), jnp.float32), 'key_value_states': jax.random.normal(ks[1], (B, Tk, E), jnp.float32), 'Wq': jax.random.normal(ks[2], (E, E), jnp.float32) * s, 'bq': jnp.zeros((E,), jnp.float32), 'Wk': jax.random.normal(ks[3], (E, E), jnp.float32) * s, 'bk': jnp.zeros((E,), jnp.float32), 'Wv': jax.random.normal(ks[4], (E, E), jnp.float32) * s, 'bv': jnp.zeros((E,), jnp.float32), 'Wo': jax.random.normal(ks[5], (E, E), jnp.float32) * s, 'bo': jnp.zeros((E,), jnp.float32), 'stride': 16}
    _L0_xattn_all = _L0_xattn_setup()
    _L0_xattn_in = {k: v for k, v in _L0_xattn_all.items() if k in ('Wq', 'bq', 'Wk', 'bk', 'Wv', 'bv', 'Wo', 'bo')}
    del _L0_xattn_all

    def _L0_ffn_setup():
        import jax, jax.numpy as jnp
        import numpy as np
        B, S, D = (4, 512, 128)
        DD = 4 * D
        N_EXPERTS = 8
        CAPACITY = 1.0
        LN_EPS = 1e-05
        key = jax.random.key(seed)
        ks = jax.random.split(key, 8)
        s1 = 1.0 / np.sqrt(D)
        s2 = 1.0 / np.sqrt(DD)
        return {'x': jax.random.normal(ks[0], (B, S, D), jnp.float32), 'gate_w': jax.random.normal(ks[1], (N_EXPERTS, D), jnp.float32) * 0.02, 'ln_w': jnp.ones((D,), jnp.float32), 'ln_b': jnp.zeros((D,), jnp.float32), 'fc1s': jax.random.normal(ks[2], (N_EXPERTS, DD, D), jnp.float32) * s1, 'b1s': jax.random.normal(ks[3], (N_EXPERTS, DD), jnp.float32) * s1, 'fc2s': jax.random.normal(ks[4], (N_EXPERTS, D, DD), jnp.float32) * s2, 'b2s': jax.random.normal(ks[5], (N_EXPERTS, D), jnp.float32) * s2}
    _L0_ffn_all = _L0_ffn_setup()
    _L0_ffn_in = {k: v for k, v in _L0_ffn_all.items() if k in ('gate_w', 'ln_w', 'ln_b', 'fc1s', 'b1s', 'fc2s', 'b2s')}
    del _L0_ffn_all

    def _L1_xattn_setup():
        import jax, jax.numpy as jnp
        import numpy as np
        NUM_HEADS = 16
        D_MODEL = 128
        D_K = D_MODEL // NUM_HEADS

        def _split_heads(x):
            B, S, _ = x.shape
            return x.reshape(B, S, NUM_HEADS, D_K).transpose(0, 2, 1, 3)
        key = jax.random.key(seed)
        ks = jax.random.split(key, 11)
        B, S, D = (1, 512, D_MODEL)
        scale = 1.0 / np.sqrt(D)
        return {'Q': jax.random.normal(ks[0], (B, S, D), jnp.float32), 'K': jax.random.normal(ks[1], (B, S, D), jnp.float32), 'V': jax.random.normal(ks[2], (B, S, D), jnp.float32), 'W_Q': jax.random.normal(ks[3], (D, D), jnp.float32) * scale, 'b_Q': jax.random.normal(ks[4], (D,), jnp.float32) * 0.02, 'W_K': jax.random.normal(ks[5], (D, D), jnp.float32) * scale, 'b_K': jax.random.normal(ks[6], (D,), jnp.float32) * 0.02, 'W_V': jax.random.normal(ks[7], (D, D), jnp.float32) * scale, 'b_V': jax.random.normal(ks[8], (D,), jnp.float32) * 0.02, 'W_O': jax.random.normal(ks[9], (D, D), jnp.float32) * scale, 'b_O': jax.random.normal(ks[10], (D,), jnp.float32) * 0.02}
    _L1_xattn_all = _L1_xattn_setup()
    _L1_xattn_in = {k: v for k, v in _L1_xattn_all.items() if k in ('W_Q', 'b_Q', 'W_K', 'b_K', 'W_V', 'b_V', 'W_O', 'b_O')}
    del _L1_xattn_all

    def _L1_ffn_setup():
        import jax, jax.numpy as jnp
        import numpy as np
        B, S, H = (2, 256, 128)
        N, F, SF, K = (16, 128, 512, 1)
        key = jax.random.key(seed)
        ks = jax.random.split(key, 7)
        std = 0.02
        return {'hidden_states': jax.random.normal(ks[0], (B, S, H), dtype=jnp.float32), 'router_w': jax.random.normal(ks[1], (N, H), dtype=jnp.float32) * std, 'gate_up_proj': jax.random.normal(ks[2], (N, H, 2 * F), dtype=jnp.float32) * std, 'down_proj': jax.random.normal(ks[3], (N, F, H), dtype=jnp.float32) * std, 'shared_gate_w': jax.random.normal(ks[4], (SF, H), dtype=jnp.float32) * std, 'shared_up_w': jax.random.normal(ks[5], (SF, H), dtype=jnp.float32) * std, 'shared_down_w': jax.random.normal(ks[6], (H, SF), dtype=jnp.float32) * std}
    _L1_ffn_all = _L1_ffn_setup()
    _L1_ffn_in = {k: v for k, v in _L1_ffn_all.items() if k in ('router_w', 'gate_up_proj', 'down_proj', 'shared_gate_w', 'shared_up_w', 'shared_down_w')}
    del _L1_ffn_all
    return {'x': x, 'ctx_1024': ctx_1024, 'g_xattn': g_xattn, 'g_ffn': g_ffn, 'L0_xattn_Wq': _L0_xattn_in['Wq'], 'L0_xattn_bq': _L0_xattn_in['bq'], 'L0_xattn_Wk': _L0_xattn_in['Wk'], 'L0_xattn_bk': _L0_xattn_in['bk'], 'L0_xattn_Wv': _L0_xattn_in['Wv'], 'L0_xattn_bv': _L0_xattn_in['bv'], 'L0_xattn_Wo': _L0_xattn_in['Wo'], 'L0_xattn_bo': _L0_xattn_in['bo'], 'L0_ffn_gate_w': _L0_ffn_in['gate_w'], 'L0_ffn_ln_w': _L0_ffn_in['ln_w'], 'L0_ffn_ln_b': _L0_ffn_in['ln_b'], 'L0_ffn_fc1s': _L0_ffn_in['fc1s'], 'L0_ffn_b1s': _L0_ffn_in['b1s'], 'L0_ffn_fc2s': _L0_ffn_in['fc2s'], 'L0_ffn_b2s': _L0_ffn_in['b2s'], 'L1_xattn_W_Q': _L1_xattn_in['W_Q'], 'L1_xattn_b_Q': _L1_xattn_in['b_Q'], 'L1_xattn_W_K': _L1_xattn_in['W_K'], 'L1_xattn_b_K': _L1_xattn_in['b_K'], 'L1_xattn_W_V': _L1_xattn_in['W_V'], 'L1_xattn_b_V': _L1_xattn_in['b_V'], 'L1_xattn_W_O': _L1_xattn_in['W_O'], 'L1_xattn_b_O': _L1_xattn_in['b_O'], 'L1_ffn_router_w': _L1_ffn_in['router_w'], 'L1_ffn_gate_up_proj': _L1_ffn_in['gate_up_proj'], 'L1_ffn_down_proj': _L1_ffn_in['down_proj'], 'L1_ffn_shared_gate_w': _L1_ffn_in['shared_gate_w'], 'L1_ffn_shared_up_w': _L1_ffn_in['shared_up_w'], 'L1_ffn_shared_down_w': _L1_ffn_in['shared_down_w']}

def reference(x, ctx_1024, g_xattn, g_ffn, L0_xattn_Wq, L0_xattn_bq, L0_xattn_Wk, L0_xattn_bk, L0_xattn_Wv, L0_xattn_bv, L0_xattn_Wo, L0_xattn_bo, L0_ffn_gate_w, L0_ffn_ln_w, L0_ffn_ln_b, L0_ffn_fc1s, L0_ffn_b1s, L0_ffn_fc2s, L0_ffn_b2s, L1_xattn_W_Q, L1_xattn_b_Q, L1_xattn_W_K, L1_xattn_b_K, L1_xattn_W_V, L1_xattn_b_V, L1_xattn_W_O, L1_xattn_b_O, L1_ffn_router_w, L1_ffn_gate_up_proj, L1_ffn_down_proj, L1_ffn_shared_gate_w, L1_ffn_shared_up_w, L1_ffn_shared_down_w):
    import jax
    import jax.numpy as jnp

    def _L0_xattn_ref(hidden_states, key_value_states, Wq, bq, Wk, bk, Wv, bv, Wo, bo, stride):
        import jax, jax.numpy as jnp
        import numpy as np
        E = 128
        H = 16
        D = E // H
        B, Tq, _ = hidden_states.shape
        Tk = key_value_states.shape[1]
        scaling = D ** (-0.5)
        Q = (hidden_states @ Wq.T + bq).reshape(B, Tq, H, D).transpose(0, 2, 1, 3)
        K = (key_value_states @ Wk.T + bk).reshape(B, Tk, H, D).transpose(0, 2, 1, 3)
        V = (key_value_states @ Wv.T + bv).reshape(B, Tk, H, D).transpose(0, 2, 1, 3)
        m = Tk // stride
        idx = jnp.arange(H)[:, None] + stride * jnp.arange(m)[None, :]
        gather = idx[None, :, :, None]
        Kg = jnp.take_along_axis(K, gather, axis=2)
        Vg = jnp.take_along_axis(V, gather, axis=2)
        scores = jnp.einsum('bhqd,bhkd->bhqk', Q, Kg) * scaling
        attn = jax.nn.softmax(scores, axis=-1)
        out = jnp.einsum('bhqk,bhkd->bhqd', attn, Vg)
        out = out.transpose(0, 2, 1, 3).reshape(B, Tq, E)
        return out @ Wo.T + bo

    def _L0_ffn_ref(x, gate_w, ln_w, ln_b, fc1s, b1s, fc2s, b2s):
        import jax, jax.numpy as jnp
        import numpy as np
        B, S, D = (4, 512, 128)
        DD = 4 * D
        N_EXPERTS = 8
        CAPACITY = 1.0
        LN_EPS = 1e-05
        og_shape = x.shape
        d = og_shape[-1]
        xf = x.reshape(-1, d)
        bs = xf.shape[0]
        n = gate_w.shape[0]
        k = int(bs * CAPACITY) // n
        scores = jax.nn.softmax(xf @ gate_w.T, axis=-1)
        vals, idx = jax.lax.top_k(scores.T, k)
        kept_w = vals.T
        kept_idx = idx.T
        flat_idx = kept_idx.reshape(-1)
        y = xf[flat_idx].reshape(k, n, d)
        mu = y.mean(-1, keepdims=True)
        var = ((y - mu) ** 2).mean(-1, keepdims=True)
        y = (y - mu) * jax.lax.rsqrt(var + LN_EPS) * ln_w + ln_b
        h = jnp.einsum('knd,nfd->knf', y, fc1s) + b1s
        h = jax.nn.gelu(h, approximate=True)
        out = jnp.einsum('knf,ndf->knd', h, fc2s) + b2s
        out = out * kept_w[..., None]
        xf = xf.at[flat_idx].add(out.reshape(k * n, d))
        return xf.reshape(og_shape)

    def _L1_xattn_ref(Q, K, V, W_Q, b_Q, W_K, b_K, W_V, b_V, W_O, b_O):
        import jax, jax.numpy as jnp
        import numpy as np
        NUM_HEADS = 16
        D_MODEL = 128
        D_K = D_MODEL // NUM_HEADS

        def _split_heads(x):
            B, S, _ = x.shape
            return x.reshape(B, S, NUM_HEADS, D_K).transpose(0, 2, 1, 3)
        q = _split_heads(Q @ W_Q + b_Q)
        k = _split_heads(K @ W_K + b_K)
        v = _split_heads(V @ W_V + b_V)
        inv_sqrt_dk = jnp.asarray(1.0 / np.sqrt(D_K), q.dtype)
        scores = jnp.einsum('bhqd,bhkd->bhqk', q, k) * inv_sqrt_dk
        weights = jax.nn.softmax(scores, axis=-1)
        out = jnp.einsum('bhqk,bhkd->bhqd', weights, v)
        B, _, S, _ = out.shape
        combined = out.transpose(0, 2, 1, 3).reshape(B, S, D_MODEL)
        return combined @ W_O + b_O

    def _L1_ffn_ref(hidden_states, router_w, gate_up_proj, down_proj, shared_gate_w, shared_up_w, shared_down_w):
        import jax, jax.numpy as jnp
        import numpy as np
        B, S, H = (2, 256, 128)
        N, F, SF, K = (16, 128, 512, 1)
        b, s, h = hidden_states.shape
        hidden = hidden_states.reshape(-1, h)
        t = hidden.shape[0]
        logits = hidden @ router_w.T
        top_vals, top_idx = jax.lax.top_k(logits, K)
        scores = jnp.full_like(logits, -jnp.inf)
        scores = scores.at[jnp.arange(t)[:, None], top_idx].set(top_vals)
        scores = jax.nn.sigmoid(scores.astype(jnp.float32)).astype(hidden.dtype)
        routed_in = hidden[None, :, :] * scores.T[:, :, None]
        gate_up = jnp.einsum('nth,nhf->ntf', routed_in, gate_up_proj)
        gate, up = jnp.split(gate_up, 2, axis=-1)
        routed_out = jnp.einsum('ntf,nfh->nth', up * jax.nn.silu(gate), down_proj)
        expert_sum = routed_out.sum(axis=0)
        shared = jax.nn.silu(hidden @ shared_gate_w.T) * (hidden @ shared_up_w.T) @ shared_down_w.T
        return (shared + expert_sum).reshape(b, s, h)
    x = x + jnp.tanh(g_xattn[0]) * _L0_xattn_ref(_layernorm(x, axis=-1), ctx_1024, L0_xattn_Wq, L0_xattn_bq, L0_xattn_Wk, L0_xattn_bk, L0_xattn_Wv, L0_xattn_bv, L0_xattn_Wo, L0_xattn_bo, 16)
    x = x + jnp.tanh(g_ffn[0]) * _L0_ffn_ref(_layernorm(x, axis=-1), L0_ffn_gate_w, L0_ffn_ln_w, L0_ffn_ln_b, L0_ffn_fc1s, L0_ffn_b1s, L0_ffn_fc2s, L0_ffn_b2s)
    x = x + jnp.tanh(g_xattn[1]) * _L1_xattn_ref(_layernorm(x, axis=-1), ctx_1024, ctx_1024, L1_xattn_W_Q, L1_xattn_b_Q, L1_xattn_W_K, L1_xattn_b_K, L1_xattn_W_V, L1_xattn_b_V, L1_xattn_W_O, L1_xattn_b_O)
    x = x + jnp.tanh(g_ffn[1]) * _L1_ffn_ref(_layernorm(x, axis=-1), L1_ffn_router_w, L1_ffn_gate_up_proj, L1_ffn_down_proj, L1_ffn_shared_gate_w, L1_ffn_shared_up_w, L1_ffn_shared_down_w)
    return x

_drawn_inputs = setup_inputs


def setup_inputs(seed=0):
    import zlib

    import numpy as np

    out = dict(_drawn_inputs(seed))
    spreads = {'g_ffn': (-1.0, 0.6),
     'L0_xattn_bq': (0.0, 0.8),
     'L0_xattn_bk': (0.0, 0.8),
     'L0_xattn_bv': (0.0, 0.325),
     'L0_xattn_bo': (0.0, 0.1),
     'L0_ffn_ln_w': (1.0, 0.2),
     'L0_ffn_ln_b': (0.0, 0.368)}
    factors = {'L0_xattn_Wq': 8.0,
     'L0_xattn_Wk': 7.183,
     'L0_ffn_b1s': 2.738,
     'L0_ffn_b2s': 3.642,
     'L1_xattn_b_Q': 7.489,
     'L1_xattn_b_K': 8.0,
     'L1_ffn_router_w': 8.0,
     'L1_ffn_gate_up_proj': 8.0,
     'L1_ffn_down_proj': 8.0,
     'L1_ffn_shared_gate_w': 3.152,
     'L1_ffn_shared_up_w': 3.308,
     'L1_ffn_shared_down_w': 3.287}
    for name, (base, spread) in spreads.items():
        noise = np.random.default_rng([zlib.crc32(name.encode()), seed]).standard_normal(out[name].shape)
        drawn = base * np.exp(spread * noise) if base else spread * noise
        out[name] = jnp.asarray(drawn.astype(out[name].dtype))
    for name, factor in factors.items():
        out[name] = (out[name] * factor).astype(out[name].dtype)
    return out
```

```python
from contextlib import ExitStack

import concourse.bass as bass
from concourse import mybir

P = 128
D = 128
NB = 2
SQ = 256
SK = 512
T = NB * SQ
NT = T // P
KC = SK // P
H = 16
DH = D // H
EPS = 1e-5
SCALE = DH ** -0.5

E0 = 8
CAP0 = T // E0
FF0 = 512
FC0 = FF0 // P
PR0 = E0 * CAP0 // P

E1 = 16
F1 = 128
WIN = 128
LAST = T - WIN
PLACES = T + WIN
WIDE = PLACES + WIN
PC1 = PLACES // P
MORE = T // WIN
SF = 512
SFC = SF // P

TERMS = [(i, j) for i in range(3) for j in range(3)]
NROW = len(TERMS) * DH
MROW = NROW
PK = MROW + 2
GH = 4
NG = H // GH
UNITS = NB * NG

C_VEC = 0
V_BQ, V_BK, V_BV, V_LNW, V_LNB, V_BQ1, V_BK1, V_BV1 = range(8)
C_B1 = 8
C_GATE = C_B1 + E0 * FC0
C_ROUT = C_GATE + E0
C_END = C_ROUT + E1

K_ID = 0
K_HE = K_ID + P
K_HS = K_HE + H
K_RANK = K_HS + H
K_WSEL = K_RANK + E1
K_TRI = K_WSEL + PR0 * 3 * E0
K_IOTA = K_TRI + P
K_ONE = K_IOTA + CAP0
K_END = K_ONE + P

ALU = mybir.AluOpType
ACT = mybir.ActivationFunctionType
AX_X = mybir.AxisListType.X
F32 = mybir.dt.float32
BF16 = mybir.dt.bfloat16
I32 = mybir.dt.int32


def build(nc, x, small, consts, selq, onerows, gates, rows, ctxT, w0, w1, fc1T, fc2, b2, shGU, shD, gateup, down, kscr, out):
    with ExitStack() as ctx:
        def sb(name, shape, dt=F32):
            return ctx.enter_context(nc.sbuf_tensor(name, shape, dt))

        def sem(name):
            return ctx.enter_context(nc.semaphore(name))

        bank = ctx.enter_context(nc.psum_tensor("bank", [P, 8, 512], F32))

        x_sb = sb("x_sb", [P, NT, D])
        small_sb = sb("small_sb", [P, C_END])
        const_sb = sb("const_sb", [P, K_END])
        gates_sb = sb("gates_sb", [P, 4])
        rows_sb = sb("rows_sb", [1, 2, D])
        ctxT_sb = sb("ctxT_sb", [D, NB * SK])
        w0_sb = sb("w0_sb", [P, 4, D])
        w1_sb = sb("w1_sb", [P, 4, D])
        fc1T_sb = sb("fc1T_sb", [P, E0, FF0])
        fc2_sb = sb("fc2_sb", [P, E0, FC0, D])
        b2_sb = sb("b2_sb", [P, PR0, D])
        shGU_sb = sb("shGU_sb", [P, 2, SF])
        shD_sb = sb("shD_sb", [P, SFC, D])
        gateup_sb = fc2_sb[:].rearrange("p e f d -> p (e f d)").rearrange("p (e k) -> p e k", e=E1)

        ident = const_sb[:, K_ID:K_ID + P]

        def vec(n):
            return small_sb[:, C_VEC + n:C_VEC + n + 1]

        arena = sb("arena", [P, 6 * NT * SK])

        def at(pos, n, pattern, dt=F32, **k):
            v = arena[:, pos:pos + n]
            return (v.bitcast(dt) if dt is not F32 else v).rearrange(pattern, **k)

        def view(n, pattern, **k):
            return at(n * NT * SK, NT * SK, pattern, **k)

        down_sb = view(0, "p (e d) -> p e d", e=E1)

        res_b = sb("res_b", [P, NT, D])
        res = [res_b, x_sb, res_b, x_sb]
        ln_in = [x_sb, res[0], res[1], res[2]]
        normed = [sb(f"normed{k}", [P, NT, D]) for k in range(2)] * 2
        normedT = [sb(f"normedT{k}", [P, NT, P]) for k in range(2)] * 2
        stats = sb("stats", [P, 5, NT, 6])
        meanvar = sb("meanvar", [P, 5, NT, 2])
        rstd = sb("rstd", [P, 5, NT])
        minus_half = sb("minus_half", [P, NT])
        tanhg = sb("tanhg", [P, 4])
        tri_bf = sb("tri_bf", [P, P], BF16)
        ones_bf = sb("ones_bf", [P, P], BF16)
        ident_bf = sb("ident_bf", [P, P], BF16)
        selq_bf = sb("selq_bf", [P, 3, H, NROW], BF16)
        iota_bf = sb("iota_bf", [P, CAP0], BF16)
        zeros_bf = sb("zeros_bf", [P, P], BF16)
        bvcol = sb("bvcol", [P, 2, P])
        bias = sb("bias", [P, 2, D])
        gbias = sb("gbias", [P, 2, D])
        xb_sb = sb("xb", [P, NT, D])

        qpack = fc1T_sb[:].rearrange("p e f -> p (e f)").bitcast(BF16).rearrange("p (h t) -> p h t", h=H)
        kpack = sb("kpack", [P, H, NB * SK], BF16)
        late = kpack[:].rearrange("p h s -> p (h s)").bitcast(F32)

        def late_view(at, n, pattern, dt=F32, **k):
            v = late[:, at:at + n]
            return (v.bitcast(dt) if dt is not F32 else v).rearrange(pattern, **k)

        k0 = sb("k0", [P, NB, SK])
        va0 = sb("va0", [P, NB * KC, H, DH + 1])
        q0T = sb("q0T", [P, NT, P])
        mx0 = sb("mx0", [P, NT, H])
        shifted = view(0, "p (i s) -> p i s", i=NT)
        probs0 = view(1, "p (i s) -> p i s", i=NT)
        probs0T = view(2, "p (i s) -> p i s", i=NT)
        rden0 = sb("rden0", [P, NT, H])
        att = [sb("att", [P, NT, H, DH])] * 2
        attT = [sb("attT", [P, NT, P])] * 2

        ex = sb("ex", [P, NT, E0])
        mxe = sb("mxe", [P, NT])
        sme = sb("sme", [P, NT])
        score = sb("score", [P, NT, E0])
        score_hi = sb("score_hi", [P, NT, E0])
        score3 = sb("score3", [P, NT, 3, E0], BF16)
        scoreT = q0T[0:E0, :, :].rearrange("p i t -> p (i t)")
        work = k0[0:E0, :, :]
        top8 = sb("top8", [E0, 8, 8])
        chosenT = sb("chosenT", [E0, T])
        chosen = sb("chosen", [P, NT, E0], BF16)
        slot0 = sb("slot0", [P, NT, E0], BF16)
        sel0 = at(5 * 2048, 1024, "p (i e s) -> p i e s", BF16, i=NT, e=E0)
        sel0T = view(3, "p (c t) -> p c t", c=PR0)
        yn = at(2 * 2048, 512, "p (i d) -> p i d", i=NT)
        ynr = at(2 * 2048 + 512, 512, "p (i d) -> p i d", i=NT)
        yn3 = at(2 * 2048 + 1024, 768, "p (k i d) -> p k i d", BF16, k=3, i=NT)
        yT = arena[:, 5 * 2048 + 1024:5 * 2048 + 1536]
        keptp = sb("keptp", [P, PR0, 3 * E0])
        kept = sb("kept", [P, PR0])
        b2w = b2_sb
        hid = view(4, "p (c u f s) -> p c u f s", c=PR0, u=2, f=FC0)
        hidg = hid
        moe0 = at(5 * 2048 + 1536, 512, "p (c d) -> p c d", c=PR0)
        xg = sb("xg", [P, NT, D])

        k1 = arena[:, 0:1024]
        k1r = arena[:, 1024:2048]
        k3 = at(2048, 1536, "p (k s) -> p k s", BF16, k=3)
        va1 = sb("va1", [P, NB * KC, H, 32])
        q1 = ctxT_sb[:, 0:T]
        q1r = ctxT_sb[:, T:2 * T]
        q3 = va0[:].rearrange("p c h d -> p (c h d)")[:, 0:768].bitcast(BF16).rearrange("p (k t) -> p k t", k=3)
        mx1 = sb("mx1", [P, NT, H])
        mrow = sb("mrow", [GH, 2, 2, SQ], BF16)
        probs1 = arena[:, 0:2 * GH * KC * SQ].rearrange("p (n c q) -> p n c q", n=2 * GH, c=KC)
        outT1 = sb("outT1", [P, 2, SQ])
        rden1 = sb("rden1", [P, NT, H])

        va1_flat = va1[:].rearrange("p c h w -> p (c h w)")

        mx16 = sb("mx16", [P, NT])
        eq16 = sb("eq16", [P, NT, E1])
        kmax = sb("kmax", [P, NT])
        sig = sb("sig", [P, 3, NT])
        oh = sb("oh", [P, NT, E1], BF16)
        count = sb("count", [P, E1])
        upto = sb("upto", [P, E1])
        start = sb("start", [P, E1])
        start_moved = sb("start_moved", [P, E1])
        last_start = sb("last_start", [P, E1])
        clipped = sb("clipped", [1, E1])
        placed = sb("placed", [P, NT, E1])
        place = sb("place", [P, NT])
        starts_int = sb("starts_int", [1, E1], I32)
        general_int = sb("general_int", [1, E1 * MORE], I32)
        most = sb("most", [1, 1])
        most_int = sb("most_int", [1, 1], I32)
        zn = va1_flat[:, 0:512].rearrange("p (i d) -> p i d", i=NT)
        znr = va1_flat[:, 512:1024].rearrange("p (i d) -> p i d", i=NT)
        zn3 = va1_flat[:, 1024:1792].bitcast(BF16).rearrange("p (k i d) -> p k i d", k=3, i=NT)
        sel1 = late_view(0, 1280, "p (i s) -> p i s", BF16, i=NT)
        sel1T = at(2 * GH * KC * SQ, PC1 * T, "p (c t) -> p c t", c=PC1)
        zT = late_view(1280, WIDE, "p s -> p s")
        sgate = va1_flat[:, 1792:2816].rearrange("p (k s) -> p k s", k=2)
        shh = late_view(2048, 2048, "p (f t) -> p f t", f=SFC)
        xs = va1_flat[:, 2816:3328].rearrange("p (i d) -> p i d", i=NT)
        gate1 = late_view(4096, WIDE, "p s -> p s")
        hid1 = late_view(4864, WIDE, "p s -> p s")
        moe1T = late_view(5632, PLACES, "p s -> p s")
        moe1 = late_view(6272, PLACES, "p (c d) -> p c d", c=PC1)
        iota_places = late_view(6912, PLACES, "p s -> p s")

        L = {n: sem("load_" + n) for n in ("x", "small", "const", "gates", "rows", "ctx", "selq", "one", "w0", "w1", "fc1", "fc2",
                                           "b2", "sh", "shd", "gu", "down")}
        S = {n: sem(n) for n in (
            "half_set", "vchain", "gchain", "tanh_done", "consts_bf", "bvcol_set", "k0_ps", "v0_ps", "k0_sb", "va0_sb",
            "bias0_ps", "bias0_sb", "xb0", "xb1", "nT0_ps", "nT0_sb", "q0_ps", "q0_sb", "sc0_ps", "shift0", "probs0_sb",
            "p0T_ps", "p0T_sb", "pv0_ps", "att0", "attT0_ps", "attT0_sb", "o0_ps", "nT1_ps", "nT1_sb", "lg0_ps",
            "sh0", "ex0", "score_sb", "scT_ps", "chosenT_sb", "chosen_ps", "chosen_sb", "cum0_ps", "sel0_sb",
            "sel0T_ps", "sel0T_sb", "yn_sb", "yn_p1", "yn_r1", "yn_p2", "yn_p3", "score3_sb", "yT_ps", "yT_sb",
            "kept_ps", "kept_sb", "b2w_sb", "fc1_ps", "hid_sb", "hidg_sb", "fc2_ps", "moe0_sb", "sc_ps", "xg_sb",
            "k1_ps", "v1_ps", "bias1_ps", "k1_sb", "va1_zero", "va1_sb", "bias1_sb", "k3_sb", "kpack_in", "nT2_ps",
            "nT2_sb", "q1_ps", "q1_sb", "q3_sb", "ring_full", "ring_free", "mrow_in", "qp_ps", "qpack_sb", "kscr_out", "s1_ps",
            "probs1_sb", "pv1_ps", "outT1_sb", "attT1_ps", "attT1_sb", "o1_ps", "nT3_ps", "nT3_sb", "lg1_ps",
            "mx16_sb", "sig_e", "oh_sb", "cum1_ps", "sel1_sb", "zn_sb", "zn_p1", "zn_r1", "zn_p2", "zn_p3",
            "shg_ps", "shg_sb", "shh_sb", "shd_ps", "xs_sb", "sel1T_ps", "sel1T_sb", "zT_ps", "zT_sb", "gu_ps", "gate1_sb", "hid1_sb",
            "down_ps", "moe1T_sb", "moe1_ps", "moe1_sb", "iota_places_set", "count_ps", "starts_set", "general_set", "final_ps", "res3", "sigma_sb", "stored")}
        LN_MV = [sem(f"ln_meanvar{k}") for k in range(5)]
        LN_RS = [sem(f"ln_rstd{k}") for k in range(5)]
        RES = sem("residual")
        LN_N = sem("ln_normed")

        SCB = [6, 7, 0, 1]

        block = ctx.enter_context(nc.Block())

        @block.sync
        def _(sp):
            sp.dma_start(x_sb[:], x).then_inc(L["x"], 16)
            sp.dma_start(const_sb[:], consts).then_inc(L["const"], 16)
            sp.dma_start(ctxT_sb[:], ctxT).then_inc(L["ctx"], 16)
            sp.dma_start(w0_sb[:], w0).then_inc(L["w0"], 16)
            sp.dma_start(w1_sb[:], w1).then_inc(L["w1"], 16)
            sp.dma_start(selq_bf[:], selq).then_inc(L["selq"], 16)
            sp.dma_start(kpack[MROW:PK, :, :], onerows).then_inc(L["one"], 16)
            sp.dma_start(fc1T_sb[:], fc1T).then_inc(L["fc1"], 16)
            sp.dma_start(fc2_sb[:], fc2).then_inc(L["fc2"], 16)
            sp.dma_start(shGU_sb[:], shGU).then_inc(L["sh"], 16)
            sp.dma_start(shD_sb[:], shD).then_inc(L["shd"], 16)


            sp.wait_ge(S["k3_sb"], 1)
            sp.dma_start(kscr, k3[:]).then_inc(S["kscr_out"], 16)
            sp.wait_ge(S["kscr_out"], 16)
            for n, (i, j) in enumerate(TERMS):
                sp.dma_start(kpack[n * DH:(n + 1) * DH, :, :],
                             kscr[:, j, :].rearrange("(h d) s -> d h s", d=DH)).then_inc(S["kpack_in"], 16)
            sp.wait_ge(S["fc2_ps"], PR0)
            sp.dma_start(gateup_sb, gateup).then_inc(L["gu"], 16)
            for u in range(UNITS):
                g, b = divmod(u, NB)
                sp.wait_ge(S["ring_free"], MAX_ITEM[u])
                for part in range(2):
                    sp.dma_start(qpack[MROW + part:MROW + part + 1, g * GH:(g + 1) * GH, b * SQ:(b + 1) * SQ],
                                 mrow[:, u % 2, part, :]).then_inc(S["mrow_in"], 16)
            sp.wait_ge(S["pv1_ps"], UNITS)
            sp.dma_start(down_sb, down).then_inc(L["down"], 16)
            for i in range(NT):
                sp.wait_ge(S["res3"], i + 1)
                sp.dma_start(out[:, i, :], res[3][:, i, :]).then_inc(S["stored"], 16)
            sp.wait_ge(S["stored"], 16 * NT)

        @block.gpsimd
        def _(pool):
            pool.dma_start(small_sb[:], small).then_inc(L["small"], 16)
            pool.dma_start(gates_sb[:], gates).then_inc(L["gates"], 16)
            pool.dma_start(rows_sb[:], rows).then_inc(L["rows"], 16)
            pool.dma_start(b2_sb[:], b2).then_inc(L["b2"], 16)
            pool.memset(minus_half[:], -0.5).then_inc(S["half_set"], 1)
            pool.memset(zeros_bf[:], 0.0).then_inc(S["half_set"], 1)
            pool.wait_ge(S["half_set"], 1)

            def ln_rstd(k, i):
                pool.wait_ge(LN_MV[k], i + 1)
                pool.tensor_scalar(rstd[:, k, i:i + 1], meanvar[:, k, i, 1:2], EPS, None, ALU.add)\
                    .then_inc(S["gchain"], 1)
                gc[0] += 1
                pool.wait_ge(S["gchain"], gc[0])
                pool.tensor_tensor(rstd[:, k, i:i + 1], rstd[:, k, i:i + 1], minus_half[:, i:i + 1], ALU.pow)\
                    .then_inc(LN_RS[k], 1)

            gc = [0]

            def link(ins):
                gc[0] += 1
                ins.then_inc(S["gchain"], 1)
                pool.wait_ge(S["gchain"], gc[0])

            def residual_bias(l, src):
                pool.wait_ge(S["tanh_done"], 1)
                pool.wait_ge(S[f"bias{l}_sb"], 1)
                link(pool.tensor_scalar(gbias[:, l, :], bias[:, l, :], tanhg[:, l:l + 1], None, ALU.mult))
                if l:
                    pool.wait_ge(RES, (1 + 1) * NT)
                for i in range(NT):
                    pool.tensor_tensor(xb_sb[:, i, :], src[:, i, :], gbias[:, l, :], ALU.add).then_inc(S[f"xb{l}"], 1)

            for i in range(NT):
                ln_rstd(0, i)
            pool.memset(va1[:], 0.0).then_inc(S["va1_zero"], 1)
            pool.wait_ge(S["va1_zero"], 1)
            pool.memset(va1[:, :, :, DH:DH + 1], 1.0).then_inc(S["va1_zero"], 1)
            residual_bias(0, x_sb)
            for i in range(NT):
                ln_rstd(1, i)
            for i in range(NT):
                ln_rstd(4, i)
            for i in range(NT):
                pool.wait_ge(LN_RS[4], i + 1)
                pool.tensor_scalar(yn[:, i, :], normed[1][:, i, :], meanvar[:, 4, i, 0:1], rstd[:, 4, i:i + 1],
                                   ALU.subtract, ALU.mult).then_inc(S["yn_sb"], 1)
            pool.wait_ge(S["yn_p1"], 1)
            pool.tensor_tensor(ynr[:], yn[:], yn3[:, 0, :, :], ALU.subtract).then_inc(S["yn_r1"], 1)
            pool.wait_ge(S["yn_p2"], 1)
            pool.wait_ge(S["yn_r1"], 1)
            pool.tensor_tensor(yn3[:, 2, :, :], ynr[:], yn3[:, 1, :, :], ALU.subtract).then_inc(S["yn_p3"], 1)
            pool.wait_ge(S["score_sb"], 1)
            link(pool.tensor_copy(score3[:, :, 0, :], score[:]))
            link(pool.tensor_tensor(score_hi[:], score[:], score3[:, :, 0, :], ALU.subtract))
            link(pool.tensor_copy(score3[:, :, 1, :], score_hi[:]))
            pool.tensor_tensor(score3[:, :, 2, :], score_hi[:], score3[:, :, 1, :], ALU.subtract)\
                .then_inc(S["score3_sb"], 1)
            pool.wait_ge(S["k1_sb"], NB)
            link(pool.tensor_copy(k3[:, 0, :], k1[:]))
            link(pool.tensor_tensor(k1r[:], k1[:], k3[:, 0, :], ALU.subtract))
            link(pool.tensor_copy(k3[:, 1, :], k1r[:]))
            pool.tensor_tensor(k3[:, 2, :], k1r[:], k3[:, 1, :], ALU.subtract).then_inc(S["k3_sb"], 1)
            for i in range(NT):
                if i == 0:
                    link(pool.tensor_scalar(xg[:], normed[1][:], tanhg[:, 2:3], None, ALU.mult))
                pool.tensor_tensor(xg[:, i, :], xg[:, i, :], res[0][:, i, :], ALU.add).then_inc(S["xg_sb"], 1)
            pool.wait_ge(S["kept_sb"], 1)
            pool.wait_ge(L["b2"], 16)
            for c in range(PR0):
                pool.tensor_scalar(b2w[:, c, :], b2_sb[:, c, :], kept[:, c:c + 1], None, ALU.mult)\
                    .then_inc(S["b2w_sb"], 1)
            for i in range(NT):
                ln_rstd(2, i)
            residual_bias(1, res[1])
            for i in range(NT):
                ln_rstd(3, i)
            pool.wait_ge(S["s1_ps"], UNITS * GH)
            pool.iota(iota_places, [[1, PLACES]], base=0, channel_multiplier=0,
                      allow_small_or_imprecise_dtypes=True).then_inc(S["iota_places_set"], 1)
            pool.memset(zT[:, PLACES:WIDE], 0.0).then_inc(S["iota_places_set"], 1)
            pool.wait_ge(S["sigma_sb"], 1)
            for i in range(NT):
                pool.tensor_scalar(zn[:, i, :], normed[3][:, i, :], sig[:, 2, i:i + 1], None, ALU.mult)\
                    .then_inc(S["zn_sb"], 1)
            pool.wait_ge(S["zn_p1"], 1)
            pool.tensor_tensor(znr[:], zn[:], zn3[:, 0, :, :], ALU.subtract).then_inc(S["zn_r1"], 1)
            pool.wait_ge(S["zn_p2"], 1)
            pool.tensor_tensor(zn3[:, 2, :, :], znr[:], zn3[:, 1, :, :], ALU.subtract).then_inc(S["zn_p3"], 1)

        @block.tensor
        def _(pe):
            def mm(o, lhsT, rhs, start=True, stop=True, **k):
                return pe.matmul(o, lhsT, rhs, start=start, stop=stop, **k)

            pe.wait_ge(L["ctx"], 16)
            pe.wait_ge(L["w0"], 16)
            for b in range(NB):
                mm(bank[:, b, :], w0_sb[:, 1, :], ctxT_sb[:, b * SK:(b + 1) * SK]).then_inc(S["k0_ps"], 1)
            for c in range(NB * KC):
                mm(bank[:, 2 + c // KC, (c % KC) * P:(c % KC + 1) * P], ctxT_sb[:, c * P:(c + 1) * P],
                   w0_sb[:, 2, :]).then_inc(S["v0_ps"], 1)

            def transpose(o, src, n=P):
                return pe.transpose(o, src, ident[0:n, 0:n])

            pe.wait_ge(L["const"], 16)
            for i in range(NT):
                pe.wait_ge(LN_N, 0 * NT + i + 1)
                transpose(bank[:, 4 + i, 0:P], normed[0][:, i, :]).then_inc(S["nT0_ps"], 1)
            pe.wait_ge(S["k0_sb"], 1)
            pe.wait_ge(S["bvcol_set"], 2)
            pe.wait_ge(L["rows"], 16)
            mm(bank[:, 0, 0:D], bvcol[:, 0, :], w0_sb[:, 3, :], stop=False)
            mm(bank[:, 0, 0:D], const_sb[0:1, K_ONE:K_ONE + P], rows_sb[0:1, 0, :], start=False).then_inc(S["bias0_ps"], 1)
            for i in range(NT):
                pe.wait_ge(S["nT0_sb"], i + 1)
                if i == 0:
                    pe.wait_ge(S["bias0_sb"], 1)
                if i == 1:
                    pe.wait_ge(S["k0_sb"], NB)
                if i == 2:
                    pe.wait_ge(S["va0_sb"], KC)
                if i == 3:
                    pe.wait_ge(S["va0_sb"], NB * KC)
                mm(bank[:, i, 0:P], w0_sb[:, 0, :], normedT[0][:, i, :]).then_inc(S["q0_ps"], 1)
            for i in range(NT):
                pe.wait_ge(S["q0_sb"], i + 1)
                mm(bank[:, 4 + i, :], q0T[:, i, :], k0[:, i // 2, :]).then_inc(S["sc0_ps"], 1)
            for i in range(NT):
                pe.wait_ge(S["probs0_sb"], i + 1)
                for c in range(KC):
                    ins = transpose(bank[:, i, c * P:(c + 1) * P], probs0[:, i, c * P:(c + 1) * P])
                ins.then_inc(S["p0T_ps"], 1)
            for i in range(NT):
                pe.wait_ge(S["p0T_sb"], i + 1)
                for c in range(KC):
                    ins = mm(bank[:, 4 + i, 0:H * (DH + 1)], probs0T[:, i, c * P:(c + 1) * P],
                             va0[:, (i // 2) * KC + c, :, :], start=c == 0, stop=c == KC - 1)
                ins.then_inc(S["pv0_ps"], 1)
            for i in range(NT):
                pe.wait_ge(S["att0"], i + 1)
                transpose(bank[:, i, 0:P], att[0][:, i, :, :]).then_inc(S["attT0_ps"], 1)
            for i in range(NT):
                pe.wait_ge(S["attT0_sb"], i + 1)
                mm(bank[:, 4 + i, 0:D], attT[0][:, i, :], w0_sb[:, 3, :]).then_inc(S["o0_ps"], 1)
            for i in range(NT):
                pe.wait_ge(LN_N, 1 * NT + i + 1)
                transpose(bank[:, i, 0:P], normed[1][:, i, :]).then_inc(S["nT1_ps"], 1)
            pe.wait_ge(L["small"], 16)
            for i in range(NT):
                pe.wait_ge(S["nT1_sb"], i + 1)
                mm(bank[:, 4, i * E0:(i + 1) * E0], normedT[1][:, i, :], small_sb[:, C_GATE:C_GATE + E0])\
                    .then_inc(S["lg0_ps"], 1)
            pe.wait_ge(S["nT1_sb"], NT)
            pe.wait_ge(L["w1"], 16)
            for b in range(NB):
                mm(bank[:, b, :], w1_sb[:, 1, :], ctxT_sb[:, b * SK:(b + 1) * SK]).then_inc(S["k1_ps"], 1)
            for c in range(NB * KC):
                mm(bank[:, 2 + c // KC, (c % KC) * P:(c % KC + 1) * P], ctxT_sb[:, c * P:(c + 1) * P],
                   w1_sb[:, 2, :]).then_inc(S["v1_ps"], 1)
            mm(bank[:, 6, 0:D], bvcol[:, 1, :], w1_sb[:, 3, :], stop=False)
            mm(bank[:, 6, 0:D], const_sb[0:1, K_ONE:K_ONE + P], rows_sb[0:1, 1, :], start=False).then_inc(S["bias1_ps"], 1)
            pe.wait_ge(S["score_sb"], 1)
            for i in range(NT):
                ins = transpose(bank[0:E0, 5, i * P:(i + 1) * P], score[:, i, :])
            ins.then_inc(S["scT_ps"], 1)
            pe.wait_ge(S["chosenT_sb"], 1)
            pe.wait_ge(S["bias1_sb"], 1)
            for i in range(NT):
                ins = transpose(bank[:, 6, i * E0:(i + 1) * E0], chosenT[:, i * P:(i + 1) * P], E0)
            ins.then_inc(S["chosen_ps"], 1)

            def count_before(pb, mask, n):
                for i in range(NT):
                    for k in range(i):
                        mm(bank[:, pb, i * n:(i + 1) * n], ones_bf[:], mask[:, k, :], start=k == 0, stop=False)
                    ins = mm(bank[:, pb, i * n:(i + 1) * n], tri_bf[:], mask[:, i, :], start=i == 0)
                return ins

            pe.wait_ge(S["consts_bf"], 4)
            pe.wait_ge(S["chosen_sb"], 1)
            count_before(7, chosen, E0).then_inc(S["cum0_ps"], 1)
            pe.wait_ge(S["k1_sb"], NB)
            pe.wait_ge(S["va1_sb"], NB * KC)
            for i in range(NT):
                pe.wait_ge(S["sel0_sb"], i + 1)
                for c in range(PR0):
                    ins = pe.transpose(bank[:, c, 0:T // 2].bitcast(BF16)[:, i * P:(i + 1) * P],
                                       sel0[:, i, 2 * c:2 * c + 2, :], ident_bf[:])
                ins.then_inc(S["sel0T_ps"], 1)
            pe.wait_ge(S["yn_p1"], 1)
            pe.wait_ge(S["yn_p2"], 1)
            pe.wait_ge(S["yn_p3"], 1)
            for i in range(NT):
                for part in range(3):
                    ins = mm(bank[:, 4, :], yn3[:, part, i, :], sel0[:, i, :, :],
                             start=i == 0 and part == 0, stop=i == NT - 1 and part == 2)
            ins.then_inc(S["yT_ps"], 1)
            pe.wait_ge(S["score3_sb"], 1)
            for c in range(PR0):
                for i in range(NT):
                    ins = mm(bank[:, 5, c * 3 * E0:(c + 1) * 3 * E0], sel0[:, i, 2 * c:2 * c + 2, :],
                             score3[:, i, :, :], start=i == 0, stop=i == NT - 1)
            ins.then_inc(S["kept_ps"], 1)
            pe.wait_ge(S["yT_sb"], 1)
            pe.wait_ge(L["fc1"], 16)
            for c in range(PR0):
                if c == 2:
                    pe.wait_ge(S["sel0T_sb"], PR0)
                for e in (2 * c, 2 * c + 1):
                    for f in range(FC0):
                        o = (e % 2 * FC0 + f) * CAP0
                        ins = mm(bank[:, SCB[c], o:o + CAP0], fc1T_sb[:, e, f * P:(f + 1) * P],
                                 yT[:, e * CAP0:(e + 1) * CAP0])
                ins.then_inc(S["fc1_ps"], 1)
            pe.wait_ge(L["fc2"], 16)
            for c in range(PR0):
                pe.wait_ge(S["hidg_sb"], c + 1)
                if c == 3:
                    pe.wait_ge(S["kept_sb"], 1)
                for f in range(FC0):
                    for u in range(2):
                        ins = mm(bank[u * CAP0:(u + 1) * CAP0, 2 + c, 0:D], hidg[:, c, u, f, :],
                                 fc2_sb[:, 2 * c + u, f, :], start=f == 0, stop=f == FC0 - 1)
                ins.then_inc(S["fc2_ps"], 1)
            pe.wait_ge(S["moe0_sb"], PR0)
            for i in range(NT):
                for c in range(PR0):
                    ins = mm(bank[:, SCB[i], 0:D], sel0T[:, c, i * P:(i + 1) * P], moe0[:, c, :],
                             start=c == 0, stop=c == PR0 - 1)
                ins.then_inc(S["sc_ps"], 1)
            for i in range(NT):
                pe.wait_ge(LN_N, 2 * NT + i + 1)
                transpose(bank[:, 2 + i, 0:P], normed[2][:, i, :]).then_inc(S["nT2_ps"], 1)
            for i in range(NT):
                pe.wait_ge(S["nT2_sb"], i + 1)
                mm(bank[:, SCB[i], 0:P], w1_sb[:, 0, :], normedT[2][:, i, :]).then_inc(S["q1_ps"], 1)

            pe.wait_ge(S["q1_sb"], NT)
            pe.wait_ge(S["q3_sb"], 1)
            pe.wait_ge(L["selq"], 16)
            ring = [0]

            def next_ring():
                n = ring[0]
                ring[0] += 1
                if n >= 2:
                    pe.wait_ge(S["ring_free"], n - 1)
                return n % 2

            def pack_q(h):
                if h >= 2:
                    pe.wait_ge(S["qpack_sb"], h - 1)
                for part in range(3):
                    ins = mm(bank[0:NROW, 6 + h % 2, :], selq_bf[:, part, h, :], q3[:, part, :],
                             start=part == 0, stop=part == 2)
                ins.then_inc(S["qp_ps"], 1)

            def raw_scores(u, j, qt):
                g, b = divmod(u, NB)
                h = g * GH + j
                t0 = b * SQ + qt * P
                r = next_ring()
                mm(bank[:, r, :], qpack[0:NROW, h, t0:t0 + P], kpack[0:NROW, h, b * SK:(b + 1) * SK])\
                    .then_inc(S["ring_full"], 1)

            def max_rows(u):
                g, b = divmod(u, NB)
                r = next_ring()
                for qt in range(2):
                    ins = transpose(bank[0:GH, r, qt * P:(qt + 1) * P], mx1[:, b * 2 + qt, g * GH:(g + 1) * GH])
                ins.then_inc(S["ring_full"], 1)

            def scores(u, j):
                g, b = divmod(u, NB)
                h = g * GH + j
                n = u * GH + j
                if n >= 2:
                    pe.wait_ge(S["probs1_sb"], n - 1)
                if j == 0:
                    pe.wait_ge(S["mrow_in"], 32 * (u + 1))
                for kc in range(KC):
                    s0 = b * SK + kc * P
                    ins = mm(bank[:, 2 + 2 * (n % 2) + kc // 2, (kc % 2) * SQ:(kc % 2 + 1) * SQ],
                             kpack[0:PK, h, s0:s0 + P], qpack[0:PK, h, b * SQ:(b + 1) * SQ])
                ins.then_inc(S["s1_ps"], 1)

            def weighted(u, kc):
                g, b = divmod(u, NB)
                if kc == 0:
                    pe.wait_ge(S["probs1_sb"], (u + 1) * GH)
                    if u >= 2:
                        pe.wait_ge(S["outT1_sb"], u - 1)
                for j in range(GH):
                    ins = mm(bank[32 * j:32 * j + 32, 6 + u % 2, 0:SQ], va1[:, b * KC + kc, g * GH + j, :],
                             probs1[:, (u % 2) * GH + j, kc, :], start=kc == 0, stop=kc == KC - 1)
                if kc == KC - 1:
                    ins.then_inc(S["pv1_ps"], 1)

            def out_rows(u):
                pe.wait_ge(S["outT1_sb"], u + 1)
                r = next_ring()
                for qt in range(2):
                    ins = transpose(bank[:, r, qt * P:(qt + 1) * P], outT1[:, u % 2, qt * P:(qt + 1) * P])
                ins.then_inc(S["ring_full"], 1)

            for h in range(H):
                pack_q(h)
            pe.wait_ge(S["qpack_sb"], H)
            pe.wait_ge(L["one"], 16)
            pe.wait_ge(S["kpack_in"], 16 * len(TERMS))
            for s in range(UNITS + 5):
                for j in range(GH):
                    if s < UNITS:
                        raw_scores(s, j, 0)
                        raw_scores(s, j, 1)
                    if j == 1 and 0 <= s - 1 < UNITS:
                        pe.wait_ge(S["ring_free"], MAXED[s - 1])
                        max_rows(s - 1)
                    if 0 <= s - 2 < UNITS:
                        scores(s - 2, j)
                    if 0 <= s - 3 < UNITS:
                        weighted(s - 3, j)
                    if j == 2 and 0 <= s - 4 < UNITS:
                        out_rows(s - 4)
            pe.wait_ge(S["ring_free"], len(RING))
            for i in range(NT):
                transpose(bank[:, 2 + i, 0:P], att[1][:, i, :, :]).then_inc(S["attT1_ps"], 1)
            for i in range(NT):
                pe.wait_ge(S["attT1_sb"], i + 1)
                mm(bank[:, SCB[i], 0:D], attT[1][:, i, :], w1_sb[:, 3, :]).then_inc(S["o1_ps"], 1)
            for i in range(NT):
                pe.wait_ge(LN_N, 3 * NT + i + 1)
                transpose(bank[:, 2 + i, 0:P], normed[3][:, i, :]).then_inc(S["nT3_ps"], 1)
            for i in range(NT):
                pe.wait_ge(S["nT3_sb"], i + 1)
                mm(bank[:, 6, i * E1:(i + 1) * E1], normedT[3][:, i, :], small_sb[:, C_ROUT:C_ROUT + E1])\
                    .then_inc(S["lg1_ps"], 1)
            pe.wait_ge(L["sh"], 16)
            for f in range(SFC):
                if f >= 2:
                    pe.wait_ge(S["shh_sb"], f - 1)
                for k in range(2):
                    ins = mm(bank[:, 2 + 2 * (f % 2) + k, :], shGU_sb[:, k, f * P:(f + 1) * P], normedT[3][:])
                ins.then_inc(S["shg_ps"], 1)
                if f == 1:
                    pe.wait_ge(S["oh_sb"], 1)
                    for i in range(NT):
                        ins = mm(bank[:, 6, NT * E1:(NT + 1) * E1], ones_bf[:], oh[:, i, :], start=i == 0, stop=i == NT - 1)
                    ins.then_inc(S["count_ps"], 1)
                    count_before(7, oh, E1).then_inc(S["cum1_ps"], 1)
            pe.wait_ge(L["shd"], 16)
            pe.wait_ge(S["shh_sb"], SFC)
            for i in range(NT):
                for f in range(SFC):
                    ins = mm(bank[:, 0, i * P:(i + 1) * P], shh[:, f, i * P:(i + 1) * P], shD_sb[:, f, :],
                             start=f == 0, stop=f == SFC - 1)
            ins.then_inc(S["shd_ps"], 1)
            for i in range(NT):
                pe.wait_ge(S["sel1_sb"], i + 1)
                for c in range(PC1):
                    ins = pe.transpose(bank[:, 2 + c // 2, :].bitcast(BF16)[:, (c % 2) * T + i * P:(c % 2) * T + (i + 1) * P],
                                       sel1[:, i, c * P:(c + 1) * P], ident_bf[:])
                ins.then_inc(S["sel1T_ps"], 1)
            pe.wait_ge(S["zn_p1"], 1)
            pe.wait_ge(S["zn_p2"], 1)
            pe.wait_ge(S["zn_p3"], 1)
            for w, n in ((0, T), (1, PLACES - T)):
                for i in range(NT):
                    for part in range(3):
                        ins = mm(bank[:, 6 + w, 0:n], zn3[:, part, i, :], sel1[:, i, w * T:w * T + n],
                                 start=i == 0 and part == 0, stop=i == NT - 1 and part == 2)
                ins.then_inc(S["zT_ps"], 1)
            pe.wait_ge(S["xs_sb"], NT)
            pe.wait_ge(S["sel1T_sb"], PC1)
            for w, n in ((0, T), (1, WIDE - T)):
                for at_bank in (0, 2, 4):
                    mm(bank[:, at_bank + w, 0:n], zeros_bf[:], sel1[:, 0, 0:n])
            pe.wait_ge(L["gu"], 16)
            pe.wait_ge(S["zT_sb"], 2)
            pe.wait_ge(S["iota_places_set"], 2)
            pe.wait_ge(S["starts_set"], 1)
            gate_ps, up_ps, down_ps = (bank[:, b:b + 2, :].rearrange("p b n -> p (b n)") for b in (0, 2, 4))
            with ExitStack() as regs:
                first = [pe.value_load(starts_int[0:1, e:e + 1], min_val=0, max_val=PLACES) for e in range(E1)]

                def gate_up(e, at):
                    for k, o in ((0, gate_ps), (1, up_ps)):
                        ins = mm(o[:, bass.ds(at, WIN)], gateup_sb[:, e, k * F1:(k + 1) * F1], zT[:, bass.ds(at, WIN)])
                    return ins

                def project(e, at):
                    return mm(down_ps[:, bass.ds(at, WIN)], down_sb[:, e, :], hid1[:, bass.ds(at, WIN)])

                def general(one):
                    for e in range(E1):
                        for k in range(MORE):
                            n = e * MORE + k
                            one(e, pe.value_load(general_int[0:1, n:n + 1], min_val=0, max_val=PLACES))

                for e in range(E1 - 1):
                    gate_up(e, first[e])
                pe.wait_ge(S["general_set"], 1)
                large = pe.value_load(most_int[0:1, 0:1], min_val=0, max_val=T)
                with pe.If(large > WIN):
                    general(gate_up)
                gate_up(E1 - 1, first[E1 - 1]).then_inc(S["gu_ps"], 1)
                pe.wait_ge(L["down"], 16)
                pe.wait_ge(S["hid1_sb"], 1)
                for e in range(E1 - 1):
                    project(e, first[e])
                with pe.If(large > WIN):
                    general(project)
                project(E1 - 1, first[E1 - 1]).then_inc(S["down_ps"], 1)
            for c in range(PC1):
                if c == 0:
                    pe.wait_ge(S["moe1T_sb"], 1)
                ins = transpose(bank[:, 6 + c // KC, (c % KC) * P:(c % KC + 1) * P], moe1T[:, c * P:(c + 1) * P])
            ins.then_inc(S["moe1_ps"], 1)
            pe.wait_ge(S["moe1_sb"], 1)
            for i in range(NT):
                for c in range(PC1):
                    ins = mm(bank[:, i, 0:D], sel1T[:, c, i * P:(i + 1) * P], moe1[:, c, :],
                             start=c == 0, stop=c == PC1 - 1)
                ins.then_inc(S["final_ps"], 1)

        @block.scalar
        def _(act):
            act.wait_ge(L["gates"], 16)
            act.activation(tanhg[:], gates_sb[:], ACT.Tanh).then_inc(S["tanh_done"], 1)

            def copies(ps, sbs, dst, src):
                for i in range(NT):
                    act.wait_ge(S[ps], i + 1)
                    act.copy(dst(i), src(i)).then_inc(S[sbs], 1)

            act.wait_ge(L["small"], 16)
            copies("nT0_ps", "nT0_sb", lambda i: normedT[0][:, i, :], lambda i: bank[:, 4 + i, 0:P])
            act.wait_ge(S["bias0_ps"], 1)
            act.copy(bias[:, 0, :], bank[:, 0, 0:D]).then_inc(S["bias0_sb"], 1)
            for i in range(NT):
                act.wait_ge(S["q0_ps"], i + 1)
                act.activation(q0T[:, i, :], bank[:, i, 0:P], ACT.Identity, bias=vec(V_BQ)).then_inc(S["q0_sb"], 1)
            for i in range(NT):
                act.wait_ge(S["shift0"], i + 1)
                act.activation(probs0[:, i, :], shifted[:, i, :], ACT.Exp, scale=SCALE).then_inc(S["probs0_sb"], 1)
            copies("p0T_ps", "p0T_sb", lambda i: probs0T[:, i, :], lambda i: bank[:, i, :])
            copies("attT0_ps", "attT0_sb", lambda i: attT[0][:, i, :], lambda i: bank[:, i, 0:P])
            copies("nT1_ps", "nT1_sb", lambda i: normedT[1][:, i, :], lambda i: bank[:, i, 0:P])
            act.wait_ge(S["sh0"], 1)
            act.activation(ex[:], ex[:], ACT.Exp).then_inc(S["ex0"], 1)
            for b in range(NB):
                act.wait_ge(S["k1_ps"], b + 1)
                act.activation(k1[:, b * SK:(b + 1) * SK], bank[:, b, :], ACT.Identity, bias=vec(V_BK1))\
                    .then_inc(S["k1_sb"], 1)
            act.wait_ge(S["va1_zero"], 2)
            for c in range(NB * KC):
                act.wait_ge(S["v1_ps"], KC * (c // KC + 1))
                act.copy(va1[:, c, :, 0:DH], bank[:, 2 + c // KC, (c % KC) * P:(c % KC + 1) * P]
                         .rearrange("p (h d) -> p h d", d=DH)).then_inc(S["va1_sb"], 1)
            act.wait_ge(S["bias1_ps"], 1)
            act.copy(bias[:, 1, :], bank[:, 6, 0:D]).then_inc(S["bias1_sb"], 1)
            act.wait_ge(S["yn_sb"], NT)
            act.copy(yn3[:, 0, :, :], yn[:]).then_inc(S["yn_p1"], 1)
            act.wait_ge(S["yn_r1"], 1)
            act.copy(yn3[:, 1, :, :], ynr[:]).then_inc(S["yn_p2"], 1)
            act.wait_ge(S["sel0T_ps"], NT)
            for c in range(PR0):
                act.copy(sel0T[:, c, :], bank[:, c, 0:T // 2].bitcast(BF16)).then_inc(S["sel0T_sb"], 1)
            for c in range(PR0):
                act.wait_ge(S["hid_sb"], c + 1)
                act.activation(hidg[:, c, :, :, :], hid[:, c, :, :, :], ACT.Gelu_apprx_tanh).then_inc(S["hidg_sb"], 1)
            copies("nT2_ps", "nT2_sb", lambda i: normedT[2][:, i, :], lambda i: bank[:, 2 + i, 0:P])
            for i in range(NT):
                act.wait_ge(S["q1_ps"], i + 1)
                act.activation(q1[:, i * P:(i + 1) * P], bank[:, SCB[i], 0:P], ACT.Identity, bias=vec(V_BQ1))\
                    .then_inc(S["q1_sb"], 1)
            for h in range(H):
                act.wait_ge(S["qp_ps"], h + 1)
                act.copy(qpack[0:NROW, h, :], bank[0:NROW, 6 + h % 2, :]).then_inc(S["qpack_sb"], 1)
            for s in range(UNITS + 5):
                for j in range(GH):
                    if 0 <= s - 2 < UNITS:
                        n = (s - 2) * GH + j
                        act.wait_ge(S["s1_ps"], n + 1)
                        if s - 2 >= 2:
                            act.wait_ge(S["pv1_ps"], s - 3)
                        act.activation(probs1[:, n % (2 * GH), :, :],
                                       bank[:, 2 + 2 * (n % 2):4 + 2 * (n % 2), :], ACT.Exp, scale=SCALE)\
                            .then_inc(S["probs1_sb"], 1)
                    if j == 0 and 0 <= s - 4 < UNITS:
                        u = s - 4
                        act.wait_ge(S["pv1_ps"], u + 1)
                        if u >= 2:
                            act.wait_ge(S["ring_full"], OUT_ITEM[u - 2])
                        act.copy(outT1[:, u % 2, :], bank[:, 6 + u % 2, 0:SQ]).then_inc(S["outT1_sb"], 1)
            copies("attT1_ps", "attT1_sb", lambda i: attT[1][:, i, :], lambda i: bank[:, 2 + i, 0:P])
            copies("nT3_ps", "nT3_sb", lambda i: normedT[3][:, i, :], lambda i: bank[:, 2 + i, 0:P])
            act.wait_ge(S["mx16_sb"], 1)
            act.activation(sig[:, 0, :], mx16[:], ACT.Exp, scale=-1.0).then_inc(S["sig_e"], 1)
            for f in range(SFC):
                act.wait_ge(S["shg_ps"], f + 1)
                if f >= 2:
                    act.wait_ge(S["shh_sb"], f - 1)
                act.activation(sgate[:, f % 2, :], bank[:, 2 + 2 * (f % 2), :], ACT.Silu).then_inc(S["shg_sb"], 1)
            act.wait_ge(S["zn_sb"], NT)
            act.copy(zn3[:, 0, :, :], zn[:]).then_inc(S["zn_p1"], 1)
            act.wait_ge(S["zn_r1"], 1)
            act.copy(zn3[:, 1, :, :], znr[:]).then_inc(S["zn_p2"], 1)
            act.wait_ge(S["sel1T_ps"], NT)
            for c in range(PC1):
                act.copy(sel1T[:, c, :], bank[:, 2 + c // 2, :].bitcast(BF16)[:, (c % 2) * T:(c % 2 + 1) * T])\
                    .then_inc(S["sel1T_sb"], 1)
            for w, n in ((0, T), (1, PLACES - T)):
                act.wait_ge(S["zT_ps"], w + 1)
                act.copy(zT[:, w * T:w * T + n], bank[:, 6 + w, 0:n]).then_inc(S["zT_sb"], 1)
            act.wait_ge(S["gu_ps"], 1)
            act.activation(gate1, bank[:, 0:2, :].rearrange("p b n -> p (b n)")[:, 0:WIDE], ACT.Silu)\
                .then_inc(S["gate1_sb"], 1)
            act.wait_ge(S["down_ps"], 1)
            act.copy(moe1T, bank[:, 4:6, :].rearrange("p b n -> p (b n)")[:, 0:PLACES]).then_inc(S["moe1T_sb"], 1)
            act.wait_ge(S["moe1_ps"], 1)
            act.copy(moe1, bank[:, 6:8, :].rearrange("p b n -> p (b n)")[:, 0:PLACES]).then_inc(S["moe1_sb"], 1)

        @block.vector
        def _(dve):
            chain = [0]

            def link(ins):
                chain[0] += 1
                ins.then_inc(S["vchain"], 1)
                dve.wait_ge(S["vchain"], chain[0])

            def ln_stats(k, i, src):
                link(dve.bn_stats(stats[:, k, i, :], src))
                dve.bn_aggr(meanvar[:, k, i, :], stats[:, k, i, :]).then_inc(LN_MV[k], 1)

            def ln_apply(k, i):
                dve.wait_ge(LN_RS[k], i + 1)
                dve.tensor_scalar(normed[k][:, i, :], ln_in[k][:, i, :], meanvar[:, k, i, 0:1], rstd[:, k, i:i + 1],
                                  ALU.subtract, ALU.mult).then_inc(LN_N, 1)

            dve.wait_ge(L["x"], 16)
            for i in range(NT):
                ln_stats(0, i, x_sb[:, i, :])
            dve.wait_ge(L["small"], 16)
            for l, v in ((0, V_BV), (1, V_BV1)):
                dve.tensor_copy(bvcol[:, l, :], vec(v).to_broadcast([P, P])).then_inc(S["bvcol_set"], 1)
            for i in range(NT):
                ln_apply(0, i)
            dve.wait_ge(L["const"], 16)
            he = const_sb[:, K_HE:K_HE + H]
            hs = const_sb[:, K_HS:K_HS + H]
            for b in range(NB):
                dve.wait_ge(S["k0_ps"], b + 1)
                dve.scalar_tensor_tensor(
                    out=k0[:, b, :].rearrange("p (j h) -> p j h", h=H),
                    in0=bank[:, b, :].rearrange("p (j h) -> p j h", h=H), scalar=vec(V_BK),
                    in1=he.unsqueeze(1).to_broadcast([P, SK // H, H]), op0=ALU.add, op1=ALU.mult)\
                    .then_inc(S["k0_sb"], 1)
            for c in range(NB * KC):
                if c % KC == 0:
                    dve.wait_ge(S["v0_ps"], c + KC)
                dve.tensor_copy(va0[:, c, :, DH:DH + 1], hs.unsqueeze(2))
                dve.tensor_tensor(va0[:, c, :, 0:DH],
                                  bank[:, 2 + c // KC, (c % KC) * P:(c % KC + 1) * P].rearrange("p (h d) -> p h d", d=DH),
                                  hs.unsqueeze(2).to_broadcast([P, H, DH]), ALU.mult).then_inc(S["va0_sb"], 1)
            dve.tensor_copy(tri_bf[:], const_sb[:, K_TRI:K_TRI + P]).then_inc(S["consts_bf"], 1)
            dve.tensor_copy(ones_bf[:], const_sb[:, K_ONE:K_ONE + P]).then_inc(S["consts_bf"], 1)
            dve.tensor_copy(ident_bf[:], ident).then_inc(S["consts_bf"], 1)
            dve.tensor_copy(iota_bf[:], const_sb[:, K_IOTA:K_IOTA + CAP0]).then_inc(S["consts_bf"], 1)
            for i in range(NT):
                dve.wait_ge(S["sc0_ps"], i + 1)
                s_v = bank[:, 4 + i, :].rearrange("p (j h) -> p j h", h=H)
                link(dve.tensor_reduce(mx0[:, i, :], bank[:, 4 + i, :].rearrange("p (j h) -> p h j", h=H), AX_X, ALU.max))
                dve.tensor_tensor(shifted[:, i, :].rearrange("p (j h) -> p j h", h=H), s_v,
                                  mx0[:, i, :].unsqueeze(1).to_broadcast([P, SK // H, H]), ALU.subtract)\
                    .then_inc(S["shift0"], 1)
            for i in range(NT):
                dve.wait_ge(S["pv0_ps"], i + 1)
                pv = bank[:, 4 + i, 0:H * (DH + 1)].rearrange("p (h d) -> p h d", d=DH + 1)
                link(dve.reciprocal(rden0[:, i, :].unsqueeze(2), pv[:, :, DH:DH + 1]))
                dve.tensor_tensor(att[0][:, i, :, :], pv[:, :, 0:DH],
                                  rden0[:, i, :].unsqueeze(2).to_broadcast([P, H, DH]), ALU.mult).then_inc(S["att0"], 1)
            for i in range(NT):
                dve.wait_ge(S["o0_ps"], i + 1)
                dve.wait_ge(S["xb0"], i + 1)
                dve.scalar_tensor_tensor(out=res[0][:, i, :], in0=bank[:, 4 + i, 0:D], scalar=tanhg[:, 0:1],
                                         in1=xb_sb[:, i, :], op0=ALU.mult, op1=ALU.add).then_inc(RES, 1)
                dve.wait_ge(RES, 0 * NT + i + 1)
                ln_stats(1, i, res[0][:, i, :])
            for i in range(NT):
                ln_apply(1, i)
            for i in range(NT):
                dve.wait_ge(LN_N, 1 * NT + i + 1)
                ln_stats(4, i, normed[1][:, i, :])
            dve.wait_ge(S["lg0_ps"], NT)
            lg = bank[:, 4, 0:NT * E0].rearrange("p (i e) -> p i e", e=E0)
            link(dve.tensor_reduce(mxe[:], lg, AX_X, ALU.max))
            dve.tensor_tensor(ex[:], lg, mxe[:].unsqueeze(2).to_broadcast([P, NT, E0]), ALU.subtract).then_inc(S["sh0"], 1)
            dve.wait_ge(S["ex0"], 1)
            link(dve.tensor_reduce(sme[:], ex[:], AX_X, ALU.add))
            link(dve.reciprocal(sme[:], sme[:]))
            dve.tensor_tensor(score[:], ex[:], sme[:].unsqueeze(2).to_broadcast([P, NT, E0]), ALU.mult)\
                .then_inc(S["score_sb"], 1)
            dve.wait_ge(S["scT_ps"], 1)
            link(dve.tensor_copy(scoreT, bank[0:E0, 5, :]))
            src = scoreT
            for r in range(CAP0 // 8):
                link(dve.max(top8[:, r, :], src))
                link(dve.match_replace(work[:, r % 2, :], top8[:, r, :], src, -1.0))
                src = work[:, r % 2, :]
            dve.tensor_scalar(chosenT[:], src, 0.0, None, ALU.is_lt).then_inc(S["chosenT_sb"], 1)
            dve.wait_ge(S["chosen_ps"], 1)
            dve.tensor_copy(chosen[:], bank[:, 6, 0:NT * E0].rearrange("p (i e) -> p i e", e=E0))\
                .then_inc(S["chosen_sb"], 1)
            dve.wait_ge(S["chosen_sb"], 1)
            dve.wait_ge(S["cum0_ps"], 1)
            link(dve.scalar_tensor_tensor(out=slot0[:], in0=bank[:, 7, 0:NT * E0].rearrange("p (i e) -> p i e", e=E0),
                                          scalar=1.0, in1=chosen[:], op0=ALU.add, op1=ALU.mult))
            for i in range(NT):
                dve.tensor_tensor(sel0[:, i, :, :], iota_bf[:].unsqueeze(1).to_broadcast([P, E0, CAP0]),
                                  slot0[:, i, :].unsqueeze(2).to_broadcast([P, E0, CAP0]), ALU.is_equal)\
                    .then_inc(S["sel0_sb"], 1)
            dve.wait_ge(S["yT_ps"], 1)
            dve.tensor_scalar(yT[:], bank[:, 4, :], vec(V_LNW), vec(V_LNB), ALU.mult, ALU.add).then_inc(S["yT_sb"], 1)
            dve.wait_ge(S["kept_ps"], 1)
            link(dve.tensor_tensor(keptp[:], bank[:, 5, 0:PR0 * 3 * E0].rearrange("p (c k) -> p c k", k=3 * E0),
                                   const_sb[:, K_WSEL:K_WSEL + PR0 * 3 * E0].rearrange("p (c k) -> p c k", k=3 * E0),
                                   ALU.mult))
            dve.tensor_reduce(kept[:], keptp[:], AX_X, ALU.add).then_inc(S["kept_sb"], 1)
            for c in range(PR0):
                dve.wait_ge(S["fc1_ps"], c + 1)
                dve.tensor_tensor(
                    hid[:, c, :, :, :].rearrange("p u f s -> p (u f) s"),
                    bank[:, SCB[c], :].rearrange("p (k s) -> p k s", s=CAP0),
                    small_sb[:, C_B1 + 2 * FC0 * c:C_B1 + 2 * FC0 * (c + 1)].unsqueeze(2)
                    .to_broadcast([P, 2 * FC0, CAP0]), ALU.add).then_inc(S["hid_sb"], 1)
            for c in range(PR0):
                dve.wait_ge(S["fc2_ps"], c + 1)
                dve.wait_ge(S["b2w_sb"], c + 1)
                dve.scalar_tensor_tensor(out=moe0[:, c, :], in0=bank[:, 2 + c, 0:D], scalar=kept[:, c:c + 1],
                                         in1=b2w[:, c, :], op0=ALU.mult, op1=ALU.add).then_inc(S["moe0_sb"], 1)
            for i in range(NT):
                dve.wait_ge(S["sc_ps"], i + 1)
                dve.wait_ge(S["xg_sb"], i + 1)
                dve.scalar_tensor_tensor(out=res[1][:, i, :], in0=bank[:, SCB[i], 0:D], scalar=tanhg[:, 2:3],
                                         in1=xg[:, i, :], op0=ALU.mult, op1=ALU.add).then_inc(RES, 1)
                dve.wait_ge(RES, 1 * NT + i + 1)
                ln_stats(2, i, res[1][:, i, :])
            for i in range(NT):
                ln_apply(2, i)
            dve.wait_ge(S["q1_sb"], NT)
            link(dve.tensor_copy(q3[:, 0, :], q1[:]))
            link(dve.tensor_tensor(q1r[:], q1[:], q3[:, 0, :], ALU.subtract))
            link(dve.tensor_copy(q3[:, 1, :], q1r[:]))
            dve.tensor_tensor(q3[:, 2, :], q1r[:], q3[:, 1, :], ALU.subtract).then_inc(S["q3_sb"], 1)

            for n, item in enumerate(RING):
                dve.wait_ge(S["ring_full"], n + 1)
                r = n % 2
                if item[0] == "score":
                    _, u, j, qt = item
                    g, b = divmod(u, NB)
                    dve.tensor_reduce(mx1[:, b * 2 + qt, g * GH + j:g * GH + j + 1], bank[:, r, :], AX_X, ALU.max)\
                        .then_inc(S["ring_free"], 1)
                elif item[0] == "max":
                    u = item[1]
                    if u >= 2:
                        dve.wait_ge(S["mrow_in"], 32 * (u - 1))
                    link(dve.tensor_scalar(mrow[:, u % 2, 0, :], bank[0:GH, r, 0:SQ], -1.0, None, ALU.mult))
                    dve.scalar_tensor_tensor(out=mrow[:, u % 2, 1, :], in0=bank[0:GH, r, 0:SQ], scalar=-1.0,
                                             in1=mrow[:, u % 2, 0, :], op0=ALU.mult, op1=ALU.subtract)\
                        .then_inc(S["ring_free"], 1)
                else:
                    u = item[1]
                    g, b = divmod(u, NB)
                    o = bank[:, r, 0:2 * P].rearrange("p (t h d) -> p t h d", t=2, d=32)
                    rd = rden1[:, b * 2:b * 2 + 2, g * GH:(g + 1) * GH]
                    link(dve.reciprocal(rd.unsqueeze(3), o[:, :, :, DH:DH + 1]))
                    dve.tensor_tensor(att[1][:, b * 2:b * 2 + 2, g * GH:(g + 1) * GH, :], o[:, :, :, 0:DH],
                                      rd.unsqueeze(3).to_broadcast([P, 2, GH, DH]), ALU.mult)\
                        .then_inc(S["ring_free"], 1)
            for i in range(NT):
                dve.wait_ge(S["o1_ps"], i + 1)
                dve.wait_ge(S["xb1"], i + 1)
                dve.scalar_tensor_tensor(out=res[2][:, i, :], in0=bank[:, SCB[i], 0:D], scalar=tanhg[:, 1:2],
                                         in1=xb_sb[:, i, :], op0=ALU.mult, op1=ALU.add).then_inc(RES, 1)
                dve.wait_ge(RES, 2 * NT + i + 1)
                ln_stats(3, i, res[2][:, i, :])
            for i in range(NT):
                ln_apply(3, i)
            dve.wait_ge(S["lg1_ps"], NT)
            lg1 = bank[:, 6, 0:NT * E1].rearrange("p (i e) -> p i e", e=E1)
            rank = const_sb[:, K_RANK:K_RANK + E1].unsqueeze(1).to_broadcast([P, NT, E1])
            dve.tensor_reduce(mx16[:], lg1, AX_X, ALU.max).then_inc(S["mx16_sb"], 1)
            dve.wait_ge(S["mx16_sb"], 1)
            link(dve.tensor_tensor(eq16[:], lg1, mx16[:].unsqueeze(2).to_broadcast([P, NT, E1]), ALU.is_equal))
            link(dve.tensor_tensor(eq16[:], eq16[:], rank, ALU.mult))
            link(dve.tensor_reduce(kmax[:], eq16[:], AX_X, ALU.max))
            dve.tensor_tensor(oh[:], eq16[:], kmax[:].unsqueeze(2).to_broadcast([P, NT, E1]), ALU.is_equal)\
                .then_inc(S["oh_sb"], 1)
            dve.wait_ge(S["sig_e"], 1)
            link(dve.tensor_scalar(sig[:, 1, :], sig[:, 0, :], 1.0, None, ALU.add))
            dve.reciprocal(sig[:, 2, :], sig[:, 1, :]).then_inc(S["sigma_sb"], 1)

            def shared_hidden(f):
                dve.wait_ge(S["shg_sb"], f + 1)
                dve.tensor_tensor(shh[:, f, :], bank[:, 3 + 2 * (f % 2), :], sgate[:, f % 2, :], ALU.mult)\
                    .then_inc(S["shh_sb"], 1)

            shared_hidden(0)
            shared_hidden(1)
            dve.wait_ge(S["count_ps"], 1)
            link(dve.tensor_copy(count[:], bank[:, 6, NT * E1:(NT + 1) * E1]))
            link(dve.tensor_tensor_scan(upto[:], const_sb[:, K_ONE:K_ONE + E1], count[:], 0.0, ALU.mult, ALU.add))
            link(dve.tensor_tensor(start[:], upto[:], count[:], ALU.subtract))
            link(dve.tensor_scalar(start_moved[:], start[:], float(LAST), float(WIN), ALU.is_gt, ALU.mult))
            link(dve.tensor_tensor(start[:], start[:], start_moved[:], ALU.add))
            dve.tensor_copy(starts_int[:], start[0:1, :]).then_inc(S["starts_set"], 1)
            dve.wait_ge(S["cum1_ps"], 1)
            link(dve.tensor_tensor(placed[:], bank[:, 7, 0:NT * E1].rearrange("p (i e) -> p i e", e=E1),
                                   start[:].unsqueeze(1).to_broadcast([P, NT, E1]), ALU.add))
            link(dve.tensor_tensor(placed[:], placed[:], oh[:], ALU.mult))
            link(dve.tensor_reduce(place[:], placed[:], AX_X, ALU.add))
            dve.wait_ge(S["iota_places_set"], 1)
            for i in range(NT):
                dve.tensor_scalar(sel1[:, i, :], iota_places, place[:, i:i + 1], None, ALU.is_equal)\
                    .then_inc(S["sel1_sb"], 1)
                if i < 2:
                    shared_hidden(2 + i)
            link(dve.tensor_tensor(last_start[:], start[:], count[:], ALU.add))
            link(dve.tensor_scalar(last_start[:], last_start[:], float(-WIN), None, ALU.add))
            for k in range(MORE):
                link(dve.scalar_tensor_tensor(out=clipped[:], in0=start[0:1, :], scalar=float(k * WIN),
                                              in1=last_start[0:1, :], op0=ALU.add, op1=ALU.min))
                link(dve.tensor_tensor(general_int[0:1, k:E1 * MORE:MORE], clipped[:], start[0:1, :], ALU.max))
            link(dve.tensor_reduce(most[:], count[0:1, :], AX_X, ALU.max))
            dve.tensor_copy(most_int[:], most[:]).then_inc(S["general_set"], 1)
            dve.wait_ge(S["shd_ps"], 1)
            for i in range(NT):
                dve.scalar_tensor_tensor(out=xs[:, i, :], in0=bank[:, 0, i * P:(i + 1) * P], scalar=tanhg[:, 3:4],
                                         in1=res[2][:, i, :], op0=ALU.mult, op1=ALU.add).then_inc(S["xs_sb"], 1)
            dve.wait_ge(S["gate1_sb"], 1)
            dve.tensor_tensor(hid1, bank[:, 2:4, :].rearrange("p b n -> p (b n)")[:, 0:WIDE], gate1, ALU.mult)\
                .then_inc(S["hid1_sb"], 1)
            for i in range(NT):
                dve.wait_ge(S["final_ps"], i + 1)
                dve.wait_ge(S["xs_sb"], i + 1)
                dve.scalar_tensor_tensor(out=res[3][:, i, :], in0=bank[:, i, 0:D], scalar=tanhg[:, 3:4],
                                         in1=xs[:, i, :], op0=ALU.mult, op1=ALU.add).then_inc(S["res3"], 1)


def ring_items():
    items = []
    for s in range(UNITS + 5):
        for j in range(GH):
            if s < UNITS:
                items += [("score", s, j, 0), ("score", s, j, 1)]
            if j == 1 and 0 <= s - 1 < UNITS:
                items.append(("max", s - 1))
            if j == 2 and 0 <= s - 4 < UNITS:
                items.append(("out", s - 4))
    return items


RING = ring_items()
MAXED = [1 + max(n for n, it in enumerate(RING) if it[0] == "score" and it[1] == u) for u in range(UNITS)]
MAX_ITEM = [1 + RING.index(("max", u)) for u in range(UNITS)]
OUT_ITEM = [1 + RING.index(("out", u)) for u in range(UNITS)]



def kernel(**a):
    import numpy as np
    import concourse.bacc as bacc
    from concourse.bass_utils import run_bass_kernel_spmd as run

    a = {k: np.asarray(v) for k, v in a.items()}
    f32 = np.float32
    tiles = a["x"].reshape(NT, P, D).transpose(1, 0, 2)
    col = lambda n: a[n].reshape(D, 1)
    small = np.concatenate(
        [col("L0_xattn_bq"), col("L0_xattn_bk"), col("L0_xattn_bv"), col("L0_ffn_ln_w"), col("L0_ffn_ln_b"),
         col("L1_xattn_b_Q"), col("L1_xattn_b_K"), col("L1_xattn_b_V"),
         a["L0_ffn_b1s"].reshape(E0 * FC0, P).T, a["L0_ffn_gate_w"].T, a["L1_ffn_router_w"].T], axis=1)
    p = np.arange(P)
    heads = np.arange(H)
    wsel = np.zeros((P, PR0, 3, E0), f32)
    for c in range(PR0):
        for u in range(2):
            wsel[u * CAP0:(u + 1) * CAP0, c, :, 2 * c + u] = 1
    consts = np.concatenate(
        [np.eye(P, dtype=f32), (p[:, None] // DH == heads).astype(f32), (p[:, None] % H == heads).astype(f32),
         np.tile(np.arange(E1, 0, -1, dtype=f32), (P, 1)), wsel.reshape(P, -1),
         (p[:, None] < p[None, :]).astype(f32), np.tile(np.arange(1, CAP0 + 1, dtype=f32), (P, 1)),
         np.ones((P, P), f32)], axis=1)
    selq = np.zeros((P, 3, H, NROW), mybir.dt.np(BF16))
    for n, (i, j) in enumerate(TERMS):
        for h in range(H):
            for d in range(DH):
                selq[h * DH + d, i, h, n * DH + d] = 1
    b2 = np.repeat(a["L0_ffn_b2s"].reshape(PR0, 2, D).transpose(1, 0, 2), CAP0, axis=0)
    arrays = {
        "x": tiles, "small": small, "consts": consts, "selq": selq, "onerows": np.ones((2, H, NB * SK), mybir.dt.np(BF16)),
        "gates": np.tile(np.concatenate([a["g_xattn"], a["g_ffn"]]), (P, 1)),
        "rows": np.stack([a["L0_xattn_bo"], a["L1_xattn_b_O"]])[None],
        "ctxT": a["ctx_1024"].reshape(NB * SK, D).T,
        "w0": np.stack([a[f"L0_xattn_W{n}"].T for n in "qkvo"], axis=1),
        "w1": np.stack([a[f"L1_xattn_W_{n}"] for n in "QKVO"], axis=1),
        "fc1T": a["L0_ffn_fc1s"].transpose(2, 0, 1),
        "fc2": a["L0_ffn_fc2s"].transpose(2, 0, 1).reshape(FC0, P, E0, D).transpose(1, 2, 0, 3),
        "b2": b2,
        "shGU": np.stack([a["L1_ffn_shared_gate_w"].T, a["L1_ffn_shared_up_w"].T], axis=1),
        "shD": a["L1_ffn_shared_down_w"].T.reshape(SFC, P, D).transpose(1, 0, 2),
        "gateup": a["L1_ffn_gate_up_proj"].transpose(1, 0, 2),
        "down": a["L1_ffn_down_proj"].transpose(1, 0, 2),
    }
    nc = bacc.Bacc("TRN2", target_bir_lowering=False, num_devices=1)
    feed, aps = {}, {}
    for name, v in arrays.items():
        feed[f"in_{name}"] = np.ascontiguousarray(v)
        aps[name] = nc.dram_tensor(f"in_{name}", v.shape, mybir.dt.from_np(v.dtype), kind="ExternalInput").ap()
    kscr = nc.dram_tensor("k_parts", (P, 3, NB * SK), BF16).ap()
    out = nc.dram_tensor("out", (P, NT, D), F32, kind="ExternalOutput").ap()
    build(nc, **aps, kscr=kscr, out=out)
    r = run(nc, [feed], core_ids=[0])
    got = r.results[0]["out"]
    return np.ascontiguousarray(np.asarray(got).transpose(1, 0, 2)).reshape(NB, SQ, D)
```

```python
from contextlib import ExitStack

import concourse.bass as bass
from concourse import mybir

P = 128
D = 128
NB = 2
SQ = 256
SK = 512
T = NB * SQ
NT = T // P
KC = SK // P
H = 16
DH = D // H
EPS = 1e-5
SCALE = DH ** -0.5

E0 = 8
CAP0 = T // E0
FF0 = 512
FC0 = FF0 // P
PR0 = E0 * CAP0 // P

E1 = 16
F1 = 128
WIN = 128
LAST = T - WIN
PLACES = T + WIN
WIDE = PLACES + WIN
PC1 = PLACES // P
MORE = T // WIN
SF = 512
SFC = SF // P

TERMS = [(i, j) for i in range(3) for j in range(3)]
NROW = len(TERMS) * DH
MROW = NROW
TERM_END = 64
GH = 4
NG = H // GH
UNITS = NB * NG

C_VEC = 0
V_BQ, V_BK, V_BV, V_LNW, V_LNB, V_BQ1, V_BK1, V_BV1 = range(8)
C_B1 = 8
C_GATE = C_B1 + E0 * FC0
C_ROUT = C_GATE + E0
C_END = C_ROUT + E1

K_ID = 0
K_HE = K_ID + P
K_HS = K_HE + H
K_RANK = K_HS + H
K_WSEL = K_RANK + E1
K_TRI = K_WSEL + PR0 * 3 * E0
K_IOTA = K_TRI + P
K_ONE = K_IOTA + CAP0
K_END = K_ONE + P

ALU = mybir.AluOpType
ACT = mybir.ActivationFunctionType
AX_X = mybir.AxisListType.X
F32 = mybir.dt.float32
BF16 = mybir.dt.bfloat16
I32 = mybir.dt.int32


def build(nc, x, small, consts, selq, onerows, gates, rows, ctxT, w0, w1, fc1T, fc2, b2, shGU, shD, gateup, down, kscr, out):
    with ExitStack() as ctx:
        def sb(name, shape, dt=F32):
            return ctx.enter_context(nc.sbuf_tensor(name, shape, dt))

        def sem(name):
            return ctx.enter_context(nc.semaphore(name))

        bank = ctx.enter_context(nc.psum_tensor("bank", [P, 8, 512], F32))

        x_sb = sb("x_sb", [P, NT, D])
        small_sb = sb("small_sb", [P, C_END])
        const_sb = sb("const_sb", [P, K_END])
        gates_sb = sb("gates_sb", [P, 4])
        rows_sb = sb("rows_sb", [1, 2, D])
        ctxT_sb = sb("ctxT_sb", [D, NB * SK])
        w0_sb = sb("w0_sb", [P, 4, D])
        w1_sb = sb("w1_sb", [P, 4, D])
        fc1T_sb = sb("fc1T_sb", [P, E0, FF0])
        fc2_sb = sb("fc2_sb", [P, E0, FC0, D])
        b2_sb = sb("b2_sb", [P, PR0, D])
        shGU_sb = sb("shGU_sb", [P, 2, SF])
        shD_sb = sb("shD_sb", [P, SFC, D])
        gateup_sb = fc2_sb[:].rearrange("p e f d -> p (e f d)").rearrange("p (e k) -> p e k", e=E1)

        ident = const_sb[:, K_ID:K_ID + P]

        def vec(n):
            return small_sb[:, C_VEC + n:C_VEC + n + 1]

        arena = sb("arena", [P, 6 * NT * SK])

        def at(pos, n, pattern, dt=F32, **k):
            v = arena[:, pos:pos + n]
            return (v.bitcast(dt) if dt is not F32 else v).rearrange(pattern, **k)

        def view(n, pattern, **k):
            return at(n * NT * SK, NT * SK, pattern, **k)

        down_sb = view(0, "p (e d) -> p e d", e=E1)

        res_b = sb("res_b", [P, NT, D])
        res = [res_b, x_sb, res_b, x_sb]
        ln_in = [x_sb, res[0], res[1], res[2]]
        normed = [sb(f"normed{k}", [P, NT, D]) for k in range(2)] * 2
        normedT = [sb(f"normedT{k}", [P, NT, P]) for k in range(2)] * 2
        stats = sb("stats", [P, 5, NT, 6])
        meanvar = sb("meanvar", [P, 5, NT, 2])
        rstd = sb("rstd", [P, 5, NT])
        minus_half = sb("minus_half", [P, NT])
        tanhg = sb("tanhg", [P, 4])
        tri_bf = sb("tri_bf", [P, P], BF16)
        ones_bf = sb("ones_bf", [P, P], BF16)
        ident_bf = sb("ident_bf", [P, P], BF16)
        selq_bf = sb("selq_bf", [P, 3, H, NROW], BF16)
        iota_bf = sb("iota_bf", [P, CAP0], BF16)
        zeros_bf = sb("zeros_bf", [P, P], BF16)
        bvcol = sb("bvcol", [P, 2, P])
        bias = sb("bias", [P, 2, D])
        gbias = sb("gbias", [P, 2, D])
        xb_sb = sb("xb", [P, NT, D])

        qpack = fc1T_sb[:].rearrange("p e f -> p (e f)").bitcast(BF16).rearrange("p (h t) -> p h t", h=H)
        kpack = sb("kpack", [P, H, NB * SK], BF16)
        late = kpack[:].rearrange("p h s -> p (h s)").bitcast(F32)

        def late_view(at, n, pattern, dt=F32, **k):
            v = late[:, at:at + n]
            return (v.bitcast(dt) if dt is not F32 else v).rearrange(pattern, **k)

        k0 = sb("k0", [P, NB, SK])
        va0 = sb("va0", [P, NB * KC, H, DH + 1])
        q0T = sb("q0T", [P, NT, P])
        mx0 = sb("mx0", [P, NT, H])
        shifted = view(0, "p (i s) -> p i s", i=NT)
        probs0 = view(1, "p (i s) -> p i s", i=NT)
        probs0T = view(2, "p (i s) -> p i s", i=NT)
        rden0 = sb("rden0", [P, NT, H])
        att = [sb("att", [P, NT, H, DH])] * 2
        attT = [sb("attT", [P, NT, P])] * 2

        ex = sb("ex", [P, NT, E0])
        mxe = sb("mxe", [P, NT])
        sme = sb("sme", [P, NT])
        score = sb("score", [P, NT, E0])
        score_hi = sb("score_hi", [P, NT, E0])
        score3 = sb("score3", [P, NT, 3, E0], BF16)
        scoreT = q0T[0:E0, :, :].rearrange("p i t -> p (i t)")
        work = k0[0:E0, :, :]
        top8 = sb("top8", [E0, 8, 8])
        chosenT = sb("chosenT", [E0, T])
        chosen = sb("chosen", [P, NT, E0], BF16)
        slot0 = sb("slot0", [P, NT, E0], BF16)
        sel0 = at(5 * 2048, 1024, "p (i e s) -> p i e s", BF16, i=NT, e=E0)
        sel0T = view(3, "p (c t) -> p c t", c=PR0)
        yn = at(2 * 2048, 512, "p (i d) -> p i d", i=NT)
        ynr = at(2 * 2048 + 512, 512, "p (i d) -> p i d", i=NT)
        yn3 = at(2 * 2048 + 1024, 768, "p (k i d) -> p k i d", BF16, k=3, i=NT)
        yT = arena[:, 5 * 2048 + 1024:5 * 2048 + 1536]
        keptp = sb("keptp", [P, PR0, 3 * E0])
        kept = sb("kept", [P, PR0])
        b2w = b2_sb
        hid = view(4, "p (c u f s) -> p c u f s", c=PR0, u=2, f=FC0)
        hidg = hid
        moe0 = at(5 * 2048 + 1536, 512, "p (c d) -> p c d", c=PR0)
        xg = sb("xg", [P, NT, D])

        k1 = arena[:, 0:1024]
        k1r = arena[:, 1024:2048]
        k3 = at(2048, 1536, "p (k s) -> p k s", BF16, k=3)
        va1 = sb("va1", [P, NB * KC, H, 32])
        q1 = ctxT_sb[:, 0:T]
        q1r = ctxT_sb[:, T:2 * T]
        q3 = va0[:].rearrange("p c h d -> p (c h d)")[:, 0:768].bitcast(BF16).rearrange("p (k t) -> p k t", k=3)
        mx1 = sb("mx1", [P, NT, H])
        minus_max = sb("minus_max", [P, 2, 2, 2, GH], BF16)
        mrow = sb("mrow", [2 * GH, 2, SQ], BF16)
        probs1 = arena[:, 0:2 * GH * KC * SQ].rearrange("p (n c q) -> p n c q", n=2 * GH, c=KC)
        outT1 = sb("outT1", [P, 2, SQ])
        rden1 = sb("rden1", [P, NT, H])

        va1_flat = va1[:].rearrange("p c h w -> p (c h w)")

        mx16 = sb("mx16", [P, NT])
        eq16 = sb("eq16", [P, NT, E1])
        kmax = sb("kmax", [P, NT])
        sig = sb("sig", [P, 3, NT])
        oh = sb("oh", [P, NT, E1], BF16)
        count = sb("count", [P, E1])
        upto = sb("upto", [P, E1])
        start = sb("start", [P, E1])
        start_moved = sb("start_moved", [P, E1])
        last_start = sb("last_start", [P, E1])
        clipped = sb("clipped", [1, E1])
        placed = sb("placed", [P, NT, E1])
        place = sb("place", [P, NT])
        starts_int = sb("starts_int", [1, E1], I32)
        general_int = sb("general_int", [1, E1 * MORE], I32)
        most = sb("most", [1, 1])
        most_int = sb("most_int", [1, 1], I32)
        zn = va1_flat[:, 0:512].rearrange("p (i d) -> p i d", i=NT)
        znr = va1_flat[:, 512:1024].rearrange("p (i d) -> p i d", i=NT)
        zn3 = va1_flat[:, 1024:1792].bitcast(BF16).rearrange("p (k i d) -> p k i d", k=3, i=NT)
        sel1 = late_view(0, 1280, "p (i s) -> p i s", BF16, i=NT)
        sel1T = at(2 * GH * KC * SQ, PC1 * T, "p (c t) -> p c t", c=PC1)
        zT = late_view(1280, WIDE, "p s -> p s")
        sgate = va1_flat[:, 1792:2816].rearrange("p (k s) -> p k s", k=2)
        shh = late_view(2048, 2048, "p (f t) -> p f t", f=SFC)
        xs = va1_flat[:, 2816:3328].rearrange("p (i d) -> p i d", i=NT)
        gate1 = late_view(4096, WIDE, "p s -> p s")
        hid1 = late_view(4864, WIDE, "p s -> p s")
        moe1T = late_view(5632, PLACES, "p s -> p s")
        moe1 = late_view(6272, PLACES, "p (c d) -> p c d", c=PC1)
        iota_places = late_view(6912, PLACES, "p s -> p s")

        L = {n: sem("load_" + n) for n in ("x", "small", "const", "gates", "rows", "ctx", "selq", "w0", "w1", "fc1", "fc2",
                                           "b2", "sh", "gu", "down")}
        S = {n: sem(n) for n in (
            "half_set", "vchain", "gchain", "tanh_done", "consts_bf", "bvcol_set", "k0_ps", "v0_ps", "k0_sb", "va0_sb",
            "bias0_ps", "bias0_sb", "xb0", "xb1", "nT0_ps", "nT0_sb", "q0_ps", "q0_sb", "sc0_ps", "shift0", "probs0_sb",
            "p0T_ps", "p0T_sb", "pv0_ps", "att0", "attT0_ps", "attT0_sb", "o0_ps", "nT1_ps", "nT1_sb", "lg0_ps",
            "sh0", "ex0", "score_sb", "scT_ps", "chosenT_sb", "chosen_ps", "chosen_sb", "cum0_ps", "sel0_sb",
            "sel0T_ps", "sel0T_sb", "yn_sb", "yn_p1", "yn_r1", "yn_p2", "yn_p3", "score3_sb", "yT_ps", "yT_sb",
            "kept_ps", "kept_sb", "b2w_sb", "fc1_ps", "hid_sb", "hidg_sb", "fc2_ps", "moe0_sb", "sc_ps", "xg_sb",
            "k1_ps", "v1_ps", "bias1_ps", "k1_sb", "va1_zero", "va1_sb", "bias1_sb", "k3_sb", "kpack_zero", "qpack_zero", "kpack_in", "nT2_ps",
            "nT2_sb", "q1_ps", "q1_sb", "q3_sb", "ring_full", "ring_free", "minus_max_set", "mrow_ps", "mrow_sb", "mrow_in", "qp_ps", "qpack_sb", "kscr_out", "s1_ps",
            "probs1_sb", "pv1_ps", "outT1_sb", "attT1_ps", "attT1_sb", "o1_ps", "nT3_ps", "nT3_sb", "lg1_ps",
            "mx16_sb", "sig_e", "oh_sb", "cum1_ps", "sel1_sb", "zn_sb", "zn_p1", "zn_r1", "zn_p2", "zn_p3",
            "shg_ps", "shg_sb", "shh_sb", "shd_ps", "xs_sb", "sel1T_ps", "sel1T_sb", "zT_ps", "zT_sb", "gu_ps", "gate1_sb", "hid1_sb",
            "down_ps", "moe1T_sb", "moe1_ps", "moe1_sb", "iota_places_set", "count_ps", "starts_set", "general_set", "final_ps", "res3", "sigma_sb", "stored")}
        LN_MV = [sem(f"ln_meanvar{k}") for k in range(5)]
        LN_RS = [sem(f"ln_rstd{k}") for k in range(5)]
        RES = sem("residual")
        LN_N = sem("ln_normed")

        PACKB = [6, 2, 3, 4, 7]
        SELB = [2, 2, 3, 3, 7]
        FINB = [0, 1, 2, 3]
        SCB = [6, 7, 0, 1]

        block = ctx.enter_context(nc.Block())

        @block.sync
        def _(sp):
            sp.dma_start(x_sb[:], x).then_inc(L["x"], 16)
            sp.dma_start(const_sb[:], consts).then_inc(L["const"], 16)
            sp.dma_start(ctxT_sb[:], ctxT).then_inc(L["ctx"], 16)
            sp.dma_start(w0_sb[:], w0).then_inc(L["w0"], 16)
            sp.dma_start(w1_sb[:], w1).then_inc(L["w1"], 16)
            sp.dma_start(selq_bf[:], selq).then_inc(L["selq"], 16)
            sp.dma_start(fc1T_sb[:], fc1T).then_inc(L["fc1"], 16)
            sp.dma_start(fc2_sb[:], fc2).then_inc(L["fc2"], 16)
            sp.dma_start(shGU_sb[:], shGU).then_inc(L["sh"], 16)
            sp.dma_start(shD_sb[:], shD).then_inc(L["sh"], 16)
            sp.wait_ge(S["kpack_zero"], 1)
            sp.dma_start(kpack[MROW:MROW + 2, :, :], onerows).then_inc(S["kpack_in"], 16)

            sp.wait_ge(S["k3_sb"], 1)
            sp.dma_start(kscr, k3[:]).then_inc(S["kscr_out"], 16)
            sp.wait_ge(S["kscr_out"], 16)
            for n, (i, j) in enumerate(TERMS):
                sp.dma_start(kpack[n * DH:(n + 1) * DH, :, :],
                             kscr[:, j, :].rearrange("(h d) s -> d h s", d=DH)).then_inc(S["kpack_in"], 16)
            sp.wait_ge(S["fc2_ps"], PR0)
            sp.dma_start(gateup_sb, gateup).then_inc(L["gu"], 16)
            for u in range(UNITS):
                b, g = divmod(u, NG)
                sp.wait_ge(S["mrow_sb"], u + 1)
                for part in range(2):
                    sp.dma_start(qpack[MROW + part:MROW + part + 1, g * GH:(g + 1) * GH, b * SQ:(b + 1) * SQ],
                                 mrow[part * GH:(part + 1) * GH, u % 2, :]).then_inc(S["mrow_in"], 16)
            sp.wait_ge(S["pv1_ps"], UNITS)
            sp.dma_start(down_sb, down).then_inc(L["down"], 16)
            for i in range(NT):
                sp.wait_ge(S["res3"], i + 1)
                sp.dma_start(out[:, i, :], res[3][:, i, :]).then_inc(S["stored"], 16)
            sp.wait_ge(S["stored"], 16 * NT)

        @block.gpsimd
        def _(pool):
            pool.dma_start(small_sb[:], small).then_inc(L["small"], 16)
            pool.dma_start(gates_sb[:], gates).then_inc(L["gates"], 16)
            pool.dma_start(rows_sb[:], rows).then_inc(L["rows"], 16)
            pool.dma_start(b2_sb[:], b2).then_inc(L["b2"], 16)
            pool.memset(minus_half[:], -0.5).then_inc(S["half_set"], 1)
            pool.memset(zeros_bf[:], 0.0).then_inc(S["half_set"], 1)
            pool.wait_ge(S["half_set"], 1)

            def ln_rstd(k, i):
                pool.wait_ge(LN_MV[k], i + 1)
                pool.tensor_scalar(rstd[:, k, i:i + 1], meanvar[:, k, i, 1:2], EPS, None, ALU.add)\
                    .then_inc(S["gchain"], 1)
                gc[0] += 1
                pool.wait_ge(S["gchain"], gc[0])
                pool.tensor_tensor(rstd[:, k, i:i + 1], rstd[:, k, i:i + 1], minus_half[:, i:i + 1], ALU.pow)\
                    .then_inc(LN_RS[k], 1)

            gc = [0]

            def link(ins):
                gc[0] += 1
                ins.then_inc(S["gchain"], 1)
                pool.wait_ge(S["gchain"], gc[0])

            def residual_bias(l, src):
                pool.wait_ge(S["tanh_done"], 1)
                pool.wait_ge(S[f"bias{l}_sb"], 1)
                link(pool.tensor_scalar(gbias[:, l, :], bias[:, l, :], tanhg[:, l:l + 1], None, ALU.mult))
                if l:
                    pool.wait_ge(RES, (1 + 1) * NT)
                for i in range(NT):
                    pool.tensor_tensor(xb_sb[:, i, :], src[:, i, :], gbias[:, l, :], ALU.add).then_inc(S[f"xb{l}"], 1)

            for i in range(NT):
                ln_rstd(0, i)
            pool.memset(va1[:], 0.0).then_inc(S["va1_zero"], 1)
            pool.wait_ge(S["va1_zero"], 1)
            pool.memset(va1[:, :, :, DH:DH + 1], 1.0).then_inc(S["va1_zero"], 1)
            residual_bias(0, x_sb)
            pool.wait_ge(S["xb0"], NT)
            pool.memset(late[TERM_END:P, :], 0.0).then_inc(S["kpack_zero"], 1)
            pool.wait_ge(S["kpack_zero"], 1)
            for i in range(NT):
                ln_rstd(1, i)
            for i in range(NT):
                ln_rstd(4, i)
            for i in range(NT):
                pool.wait_ge(LN_RS[4], i + 1)
                pool.tensor_scalar(yn[:, i, :], normed[1][:, i, :], meanvar[:, 4, i, 0:1], rstd[:, 4, i:i + 1],
                                   ALU.subtract, ALU.mult).then_inc(S["yn_sb"], 1)
            pool.wait_ge(S["yn_p1"], 1)
            pool.tensor_tensor(ynr[:], yn[:], yn3[:, 0, :, :], ALU.subtract).then_inc(S["yn_r1"], 1)
            pool.wait_ge(S["yn_p2"], 1)
            pool.wait_ge(S["yn_r1"], 1)
            pool.tensor_tensor(yn3[:, 2, :, :], ynr[:], yn3[:, 1, :, :], ALU.subtract).then_inc(S["yn_p3"], 1)
            pool.wait_ge(S["score_sb"], 1)
            link(pool.tensor_copy(score3[:, :, 0, :], score[:]))
            link(pool.tensor_tensor(score_hi[:], score[:], score3[:, :, 0, :], ALU.subtract))
            link(pool.tensor_copy(score3[:, :, 1, :], score_hi[:]))
            pool.tensor_tensor(score3[:, :, 2, :], score_hi[:], score3[:, :, 1, :], ALU.subtract)\
                .then_inc(S["score3_sb"], 1)
            pool.wait_ge(S["k1_sb"], NB)
            link(pool.tensor_copy(k3[:, 0, :], k1[:]))
            link(pool.tensor_tensor(k1r[:], k1[:], k3[:, 0, :], ALU.subtract))
            link(pool.tensor_copy(k3[:, 1, :], k1r[:]))
            pool.tensor_tensor(k3[:, 2, :], k1r[:], k3[:, 1, :], ALU.subtract).then_inc(S["k3_sb"], 1)
            for i in range(NT):
                if i == 0:
                    link(pool.tensor_scalar(xg[:], normed[1][:], tanhg[:, 2:3], None, ALU.mult))
                pool.tensor_tensor(xg[:, i, :], xg[:, i, :], res[0][:, i, :], ALU.add).then_inc(S["xg_sb"], 1)
            pool.wait_ge(S["kept_sb"], 1)
            pool.wait_ge(L["b2"], 16)
            for c in range(PR0):
                pool.tensor_scalar(b2w[:, c, :], b2_sb[:, c, :], kept[:, c:c + 1], None, ALU.mult)\
                    .then_inc(S["b2w_sb"], 1)
            pool.wait_ge(S["fc1_ps"], PR0)
            pool.wait_ge(S["b2w_sb"], PR0)
            pool.memset(fc1T_sb[TERM_END:P, :, :], 0.0).then_inc(S["qpack_zero"], 1)
            pool.wait_ge(S["qpack_zero"], 1)
            for i in range(NT):
                ln_rstd(2, i)
            residual_bias(1, res[1])
            for i in range(NT):
                ln_rstd(3, i)
            pool.wait_ge(S["s1_ps"], UNITS * GH)
            pool.iota(iota_places, [[1, PLACES]], base=0, channel_multiplier=0,
                      allow_small_or_imprecise_dtypes=True).then_inc(S["iota_places_set"], 1)
            pool.memset(zT[:, PLACES:WIDE], 0.0).then_inc(S["iota_places_set"], 1)
            pool.wait_ge(S["sigma_sb"], 1)
            for i in range(NT):
                pool.tensor_scalar(zn[:, i, :], normed[3][:, i, :], sig[:, 2, i:i + 1], None, ALU.mult)\
                    .then_inc(S["zn_sb"], 1)
            pool.wait_ge(S["zn_p1"], 1)
            pool.tensor_tensor(znr[:], zn[:], zn3[:, 0, :, :], ALU.subtract).then_inc(S["zn_r1"], 1)
            pool.wait_ge(S["zn_p2"], 1)
            pool.tensor_tensor(zn3[:, 2, :, :], znr[:], zn3[:, 1, :, :], ALU.subtract).then_inc(S["zn_p3"], 1)

        @block.tensor
        def _(pe):
            def mm(o, lhsT, rhs, start=True, stop=True, **k):
                return pe.matmul(o, lhsT, rhs, start=start, stop=stop, **k)

            pe.wait_ge(L["ctx"], 16)
            pe.wait_ge(L["w0"], 16)
            for b in range(NB):
                mm(bank[:, b, :], w0_sb[:, 1, :], ctxT_sb[:, b * SK:(b + 1) * SK]).then_inc(S["k0_ps"], 1)

            def transpose(o, src, n=P):
                return pe.transpose(o, src, ident[0:n, 0:n])

            pe.wait_ge(L["const"], 16)
            for i in range(NT):
                pe.wait_ge(LN_N, 0 * NT + i + 1)
                transpose(bank[:, 4 + i, 0:P], normed[0][:, i, :]).then_inc(S["nT0_ps"], 1)
            for i in range(NT):
                pe.wait_ge(S["nT0_sb"], i + 1)
                if i >= 2:
                    pe.wait_ge(S["q0_sb"], i - 1)
                mm(bank[:, 2 + i % 2, 0:P], w0_sb[:, 0, :], normedT[0][:, i, :]).then_inc(S["q0_ps"], 1)
            pe.wait_ge(S["k0_sb"], NB)
            for i in range(NT):
                pe.wait_ge(S["q0_sb"], i + 1)
                mm(bank[:, 4 + i, :], q0T[:, i, :], k0[:, i // 2, :]).then_inc(S["sc0_ps"], 1)
            for c in range(NB * KC):
                mm(bank[:, 2 + c // KC, (c % KC) * P:(c % KC + 1) * P], ctxT_sb[:, c * P:(c + 1) * P],
                   w0_sb[:, 2, :]).then_inc(S["v0_ps"], 1)
            pe.wait_ge(S["bvcol_set"], 2)
            pe.wait_ge(L["rows"], 16)
            mm(bank[:, 0, 0:D], bvcol[:, 0, :], w0_sb[:, 3, :], stop=False)
            mm(bank[:, 0, 0:D], const_sb[0:1, K_ONE:K_ONE + P], rows_sb[0:1, 0, :], start=False).then_inc(S["bias0_ps"], 1)
            for i in range(NT):
                pe.wait_ge(S["probs0_sb"], i + 1)
                if i == 0:
                    pe.wait_ge(S["bias0_sb"], 1)
                if i >= 2:
                    pe.wait_ge(S["va0_sb"], KC * (i - 1))
                for c in range(KC):
                    ins = transpose(bank[:, i, c * P:(c + 1) * P], probs0[:, i, c * P:(c + 1) * P])
                ins.then_inc(S["p0T_ps"], 1)
            for i in range(NT):
                pe.wait_ge(S["p0T_sb"], i + 1)
                pe.wait_ge(S["va0_sb"], KC * (i // 2 + 1))
                for c in range(KC):
                    ins = mm(bank[:, 4 + i, 0:H * (DH + 1)], probs0T[:, i, c * P:(c + 1) * P],
                             va0[:, (i // 2) * KC + c, :, :], start=c == 0, stop=c == KC - 1)
                ins.then_inc(S["pv0_ps"], 1)
            for i in range(NT):
                pe.wait_ge(S["att0"], i + 1)
                transpose(bank[:, i, 0:P], att[0][:, i, :, :]).then_inc(S["attT0_ps"], 1)
            for i in range(NT):
                pe.wait_ge(S["attT0_sb"], i + 1)
                mm(bank[:, 4 + i, 0:D], attT[0][:, i, :], w0_sb[:, 3, :]).then_inc(S["o0_ps"], 1)
            for i in range(NT):
                pe.wait_ge(LN_N, 1 * NT + i + 1)
                transpose(bank[:, i, 0:P], normed[1][:, i, :]).then_inc(S["nT1_ps"], 1)
            pe.wait_ge(L["small"], 16)
            for i in range(NT):
                pe.wait_ge(S["nT1_sb"], i + 1)
                mm(bank[:, 4, i * E0:(i + 1) * E0], normedT[1][:, i, :], small_sb[:, C_GATE:C_GATE + E0])\
                    .then_inc(S["lg0_ps"], 1)
            pe.wait_ge(S["score_sb"], 1)
            for i in range(NT):
                ins = transpose(bank[0:E0, 5, i * P:(i + 1) * P], score[:, i, :])
            ins.then_inc(S["scT_ps"], 1)
            pe.wait_ge(S["nT1_sb"], NT)
            pe.wait_ge(L["w1"], 16)
            for b in range(NB):
                mm(bank[:, b, :], w1_sb[:, 1, :], ctxT_sb[:, b * SK:(b + 1) * SK]).then_inc(S["k1_ps"], 1)
            for c in range(NB * KC):
                mm(bank[:, 2 + c // KC, (c % KC) * P:(c % KC + 1) * P], ctxT_sb[:, c * P:(c + 1) * P],
                   w1_sb[:, 2, :]).then_inc(S["v1_ps"], 1)
            mm(bank[:, 6, 0:D], bvcol[:, 1, :], w1_sb[:, 3, :], stop=False)
            mm(bank[:, 6, 0:D], const_sb[0:1, K_ONE:K_ONE + P], rows_sb[0:1, 1, :], start=False).then_inc(S["bias1_ps"], 1)
            pe.wait_ge(S["chosenT_sb"], 1)
            pe.wait_ge(S["bias1_sb"], 1)
            for i in range(NT):
                ins = transpose(bank[:, 6, i * E0:(i + 1) * E0], chosenT[:, i * P:(i + 1) * P], E0)
            ins.then_inc(S["chosen_ps"], 1)

            def count_before(pb, mask, n):
                for i in range(NT):
                    for k in range(i):
                        mm(bank[:, pb, i * n:(i + 1) * n], ones_bf[:], mask[:, k, :], start=k == 0, stop=False)
                    ins = mm(bank[:, pb, i * n:(i + 1) * n], tri_bf[:], mask[:, i, :], start=i == 0)
                return ins

            pe.wait_ge(S["consts_bf"], 4)
            pe.wait_ge(S["chosen_sb"], 1)
            count_before(7, chosen, E0).then_inc(S["cum0_ps"], 1)
            pe.wait_ge(S["yn_p1"], 1)
            pe.wait_ge(S["yn_p2"], 1)
            pe.wait_ge(S["yn_p3"], 1)
            for i in range(NT):
                pe.wait_ge(S["sel0_sb"], i + 1)
                for part in range(3):
                    ins = mm(bank[:, 4, :], yn3[:, part, i, :], sel0[:, i, :, :],
                             start=i == 0 and part == 0, stop=i == NT - 1 and part == 2)
            ins.then_inc(S["yT_ps"], 1)
            pe.wait_ge(S["score3_sb"], 1)
            for c in range(PR0):
                for i in range(NT):
                    ins = mm(bank[:, 5, c * 3 * E0:(c + 1) * 3 * E0], sel0[:, i, 2 * c:2 * c + 2, :],
                             score3[:, i, :, :], start=i == 0, stop=i == NT - 1)
            ins.then_inc(S["kept_ps"], 1)
            pe.wait_ge(S["k1_sb"], NB)
            pe.wait_ge(S["va1_sb"], NB * KC)
            for i in range(NT):
                for c in range(PR0):
                    ins = pe.transpose(bank[:, c, 0:T // 2].bitcast(BF16)[:, i * P:(i + 1) * P],
                                       sel0[:, i, 2 * c:2 * c + 2, :], ident_bf[:])
                ins.then_inc(S["sel0T_ps"], 1)
            pe.wait_ge(S["yT_sb"], 1)
            pe.wait_ge(L["fc1"], 16)
            for c in range(PR0):
                if c == 2:
                    pe.wait_ge(S["sel0T_sb"], PR0)
                for e in (2 * c, 2 * c + 1):
                    for f in range(FC0):
                        o = (e % 2 * FC0 + f) * CAP0
                        ins = mm(bank[:, SCB[c], o:o + CAP0], fc1T_sb[:, e, f * P:(f + 1) * P],
                                 yT[:, e * CAP0:(e + 1) * CAP0])
                ins.then_inc(S["fc1_ps"], 1)
            pe.wait_ge(L["fc2"], 16)
            for c in range(PR0):
                pe.wait_ge(S["hidg_sb"], c + 1)
                if c == 3:
                    pe.wait_ge(S["kept_sb"], 1)
                for f in range(FC0):
                    for u in range(2):
                        ins = mm(bank[u * CAP0:(u + 1) * CAP0, 2 + c, 0:D], hidg[:, c, u, f, :],
                                 fc2_sb[:, 2 * c + u, f, :], start=f == 0, stop=f == FC0 - 1)
                ins.then_inc(S["fc2_ps"], 1)
            pe.wait_ge(S["moe0_sb"], PR0)
            for i in range(NT):
                for c in range(PR0):
                    ins = mm(bank[:, SCB[i], 0:D], sel0T[:, c, i * P:(i + 1) * P], moe0[:, c, :],
                             start=c == 0, stop=c == PR0 - 1)
                ins.then_inc(S["sc_ps"], 1)
            for i in range(NT):
                pe.wait_ge(LN_N, 2 * NT + i + 1)
                transpose(bank[:, 2 + i, 0:P], normed[2][:, i, :]).then_inc(S["nT2_ps"], 1)
            for i in range(NT):
                pe.wait_ge(S["nT2_sb"], i + 1)
                mm(bank[:, SCB[i], 0:P], w1_sb[:, 0, :], normedT[2][:, i, :]).then_inc(S["q1_ps"], 1)

            pe.wait_ge(S["q1_sb"], NT)
            pe.wait_ge(S["q3_sb"], 1)
            pe.wait_ge(L["selq"], 16)
            ring = [0]

            def next_ring():
                n = ring[0]
                ring[0] += 1
                before = [k for k in range(n) if RING_BANK[k] == RING_BANK[n]]
                if not before:
                    if RING_BANK[n] == PACKB[GH]:
                        pe.wait_ge(S["qpack_sb"], H)
                elif RING[before[-1]][0] == "max":
                    pe.wait_ge(S["mrow_sb"], RING[before[-1]][1] + 1)
                else:
                    pe.wait_ge(S["ring_free"], READ[before[-1]])
                return RING_BANK[n]

            def pack_q(h):
                if h >= GH:
                    pe.wait_ge(S["qpack_sb"], h)
                for part in range(3):
                    ins = mm(bank[0:NROW, PACKB[min(h, GH)], :], selq_bf[:, part, h, :], q3[:, part, :],
                             start=part == 0, stop=part == 2)
                ins.then_inc(S["qp_ps"], 1)

            def raw_scores(u, j, qt):
                b, g = divmod(u, NG)
                h = g * GH + j
                t0 = b * SQ + qt * P
                r = next_ring()
                mm(bank[:, r, :], qpack[:, h, t0:t0 + P], kpack[:, h, b * SK:(b + 1) * SK])\
                    .then_inc(S["ring_full"], 1)

            def max_rows(u):
                r = next_ring()
                pe.wait_ge(S["minus_max_set"], u + 1)
                for qt in range(2):
                    ins = pe.transpose(bank[0:2 * GH, r, :].bitcast(BF16)[:, qt * P:(qt + 1) * P],
                                       minus_max[:, u % 2, qt, :, :], ident_bf[:])
                ins.then_inc(S["mrow_ps"], 1)

            def scores(u, j):
                b, g = divmod(u, NG)
                h = g * GH + j
                n = u * GH + j
                if n >= 2:
                    pe.wait_ge(S["probs1_sb"], n - 1)
                if j == 0:
                    pe.wait_ge(S["mrow_in"], 32 * (u + 1))
                for kc in range(KC):
                    s0 = b * SK + kc * P
                    ins = mm(bank[:, 2 + 2 * (n % 2) + kc // 2, (kc % 2) * SQ:(kc % 2 + 1) * SQ],
                             kpack[:, h, s0:s0 + P], qpack[:, h, b * SQ:(b + 1) * SQ])
                ins.then_inc(S["s1_ps"], 1)

            def weighted(u, kc):
                b, g = divmod(u, NG)
                if kc == 0:
                    pe.wait_ge(S["probs1_sb"], (u + 1) * GH)
                    if u >= 1:
                        pe.wait_ge(S["outT1_sb"], u)
                for j in range(GH):
                    ins = mm(bank[32 * j:32 * j + 32, 6, 0:SQ], va1[:, b * KC + kc, g * GH + j, :],
                             probs1[:, (u % 2) * GH + j, kc, :], start=kc == 0, stop=kc == KC - 1)
                if kc == KC - 1:
                    ins.then_inc(S["pv1_ps"], 1)

            def out_rows(u):
                pe.wait_ge(S["outT1_sb"], u + 1)
                r = next_ring()
                for qt in range(2):
                    ins = transpose(bank[:, r, qt * P:(qt + 1) * P], outT1[:, u % 2, qt * P:(qt + 1) * P])
                ins.then_inc(S["ring_full"], 1)

            pack_q(0)
            pack_q(1)
            pe.wait_ge(S["kpack_in"], 16 * (len(TERMS) + 1))
            for s in range(UNITS + 5):
                for j in range(GH):
                    if s < min(UNITS, NG):
                        pe.wait_ge(S["qpack_sb"], s * GH + j + 1)
                    if s < UNITS:
                        raw_scores(s, j, 0)
                    if 0 <= s - 2 < UNITS:
                        scores(s - 2, j)
                    if s < UNITS:
                        raw_scores(s, j, 1)
                    if j == max_slot(s) and 0 <= s - 1 < UNITS:
                        max_rows(s - 1)
                    if j == 2 and 0 <= s - 4 < UNITS:
                        out_rows(s - 4)
                    if s * GH + j + 2 < H:
                        pack_q(s * GH + j + 2)
                    if 0 <= s - 3 < UNITS:
                        for kc in ((), (0,), (1, 2), (3,))[j]:
                            weighted(s - 3, kc)
            pe.wait_ge(S["ring_free"], READ[-1])
            for i in range(NT):
                transpose(bank[:, 2 + i, 0:P], att[1][:, i, :, :]).then_inc(S["attT1_ps"], 1)
            for i in range(NT):
                pe.wait_ge(S["attT1_sb"], i + 1)
                mm(bank[:, SCB[i], 0:D], attT[1][:, i, :], w1_sb[:, 3, :]).then_inc(S["o1_ps"], 1)
            for i in range(NT):
                pe.wait_ge(LN_N, 3 * NT + i + 1)
                transpose(bank[:, 2 + i, 0:P], normed[3][:, i, :]).then_inc(S["nT3_ps"], 1)
            for i in range(NT):
                pe.wait_ge(S["nT3_sb"], i + 1)
                mm(bank[:, 6, i * E1:(i + 1) * E1], normedT[3][:, i, :], small_sb[:, C_ROUT:C_ROUT + E1])\
                    .then_inc(S["lg1_ps"], 1)
            pe.wait_ge(L["sh"], 32)
            first = []

            def load_starts(n):
                pe.wait_ge(S["starts_set"], 1)
                for e in range(len(first), min(len(first) + n, E1)):
                    first.append(pe.value_load(starts_int[0:1, e:e + 1], min_val=0, max_val=PLACES))

            for f in range(SFC):
                if f >= 2:
                    pe.wait_ge(S["shh_sb"], f - 1)
                for k in range(2):
                    ins = mm(bank[:, 2 + 2 * (f % 2) + k, :], shGU_sb[:, k, f * P:(f + 1) * P], normedT[3][:])
                    if (f, k) == (0, 0):
                        pe.wait_ge(S["oh_sb"], 1)
                        for i in range(NT):
                            cnt = mm(bank[:, 6, NT * E1:(NT + 1) * E1], ones_bf[:], oh[:, i, :],
                                     start=i == 0, stop=i == NT - 1)
                        cnt.then_inc(S["count_ps"], 1)
                        count_before(7, oh, E1).then_inc(S["cum1_ps"], 1)
                ins.then_inc(S["shg_ps"], 1)
                if f:
                    load_starts((4, 3, 2)[f - 1])

            def no_window(at_bank):
                for w, n in ((0, T), (1, WIDE - T)):
                    mm(bank[:, at_bank + w, 0:n], zeros_bf[:], selq_bf[:].rearrange("p k h r -> p (k h r)")[:, 0:n])

            pe.wait_ge(S["shh_sb"], SFC - 1)
            for i in range(NT):
                pe.wait_ge(S["sel1_sb"], i + 1)
                for c in range(PC1):
                    ins = pe.transpose(bank[:, SELB[c], :].bitcast(BF16)[:, (c % 2) * T + i * P:(c % 2) * T + (i + 1) * P],
                                       sel1[:, i, c * P:(c + 1) * P], ident_bf[:])
                ins.then_inc(S["sel1T_ps"], 1)
            no_window(0)
            pe.wait_ge(S["shh_sb"], SFC)
            no_window(4)
            pe.wait_ge(S["zn_p1"], 1)
            pe.wait_ge(S["zn_p2"], 1)
            pe.wait_ge(S["zn_p3"], 1)
            for w, n in ((0, T), (1, PLACES - T)):
                if w:
                    load_starts(5)
                    pe.wait_ge(S["sel1T_sb"], 1)
                for i in range(NT):
                    for part in range(3):
                        ins = mm(bank[:, 6 + w, 0:n], zn3[:, part, i, :], sel1[:, i, w * T:w * T + n],
                                 start=i == 0 and part == 0, stop=i == NT - 1 and part == 2)
                ins.then_inc(S["zT_ps"], 1)

            def shared_down(i):
                for f in range(SFC):
                    ins = mm(bank[:, 6, i * P:(i + 1) * P], shh[:, f, i * P:(i + 1) * P], shD_sb[:, f, :],
                             start=f == 0, stop=f == SFC - 1)
                return ins

            load_starts(1)
            pe.wait_ge(L["gu"], 16)
            pe.wait_ge(S["zT_sb"], 2)
            pe.wait_ge(S["iota_places_set"], 2)
            gate_ps, up_ps, down_ps = (bank[:, b:b + 2, :].rearrange("p b n -> p (b n)") for b in (0, 4, 2))

            def gate_up(e, at):
                for k, o in ((0, gate_ps), (1, up_ps)):
                    ins = mm(o[:, bass.ds(at, WIN)], gateup_sb[:, e, k * F1:(k + 1) * F1], zT[:, bass.ds(at, WIN)])
                return ins

            def project(e, at):
                return mm(down_ps[:, bass.ds(at, WIN)], down_sb[:, e, :], hid1[:, bass.ds(at, WIN)])

            def general(one):
                for e in range(E1):
                    for k in range(MORE):
                        n = e * MORE + k
                        one(e, pe.value_load(general_int[0:1, n:n + 1], min_val=0, max_val=PLACES))

            for e in range(E1 - 1):
                gate_up(e, first[e])
                if e % 4 == 3:
                    load_starts(1)
            pe.wait_ge(S["general_set"], 1)
            large = pe.value_load(most_int[0:1, 0:1], min_val=0, max_val=T)
            with pe.If(large > WIN):
                general(gate_up)
            gate_up(E1 - 1, first[E1 - 1]).then_inc(S["gu_ps"], 1)
            pe.wait_ge(L["sh"], 32)
            pe.wait_ge(S["sel1T_sb"], PC1)
            no_window(2)
            shared_down(0)
            shared_down(1)
            pe.wait_ge(L["down"], 16)
            pe.wait_ge(S["hid1_sb"], 1)
            for e in range(E1 - 1):
                project(e, first[e])
            with pe.If(large > WIN):
                general(project)
            project(E1 - 1, first[E1 - 1]).then_inc(S["down_ps"], 1)
            shared_down(2)
            pe.wait_ge(S["moe1T_sb"], 1)
            for c in range(PC1):
                ins = transpose(bank[:, 4 + c // KC, (c % KC) * P:(c % KC + 1) * P], moe1T[:, c * P:(c + 1) * P])
            ins.then_inc(S["moe1_ps"], 1)
            shared_down(3).then_inc(S["shd_ps"], 1)
            pe.wait_ge(S["moe1_sb"], 1)
            for i in range(NT):
                for c in range(PC1):
                    ins = mm(bank[:, FINB[i], 0:D], sel1T[:, c, i * P:(i + 1) * P], moe1[:, c, :],
                             start=c == 0, stop=c == PC1 - 1)
                ins.then_inc(S["final_ps"], 1)

        @block.scalar
        def _(act):
            act.wait_ge(L["gates"], 16)
            act.activation(tanhg[:], gates_sb[:], ACT.Tanh).then_inc(S["tanh_done"], 1)

            def copies(ps, sbs, dst, src):
                for i in range(NT):
                    act.wait_ge(S[ps], i + 1)
                    act.copy(dst(i), src(i)).then_inc(S[sbs], 1)

            act.wait_ge(L["small"], 16)
            copies("nT0_ps", "nT0_sb", lambda i: normedT[0][:, i, :], lambda i: bank[:, 4 + i, 0:P])
            for i in range(NT):
                act.wait_ge(S["q0_ps"], i + 1)
                act.activation(q0T[:, i, :], bank[:, 2 + i % 2, 0:P], ACT.Identity, bias=vec(V_BQ)).then_inc(S["q0_sb"], 1)
            for i in range(NT):
                act.wait_ge(S["shift0"], i + 1)
                act.activation(probs0[:, i, :], shifted[:, i, :], ACT.Exp, scale=SCALE).then_inc(S["probs0_sb"], 1)
                if i == 0:
                    act.wait_ge(S["bias0_ps"], 1)
                    act.copy(bias[:, 0, :], bank[:, 0, 0:D]).then_inc(S["bias0_sb"], 1)
            copies("p0T_ps", "p0T_sb", lambda i: probs0T[:, i, :], lambda i: bank[:, i, :])
            copies("attT0_ps", "attT0_sb", lambda i: attT[0][:, i, :], lambda i: bank[:, i, 0:P])
            copies("nT1_ps", "nT1_sb", lambda i: normedT[1][:, i, :], lambda i: bank[:, i, 0:P])
            act.wait_ge(S["sh0"], 1)
            act.activation(ex[:], ex[:], ACT.Exp).then_inc(S["ex0"], 1)
            for b in range(NB):
                act.wait_ge(S["k1_ps"], b + 1)
                act.activation(k1[:, b * SK:(b + 1) * SK], bank[:, b, :], ACT.Identity, bias=vec(V_BK1))\
                    .then_inc(S["k1_sb"], 1)
            act.wait_ge(S["va1_zero"], 2)
            for c in range(NB * KC):
                act.wait_ge(S["v1_ps"], KC * (c // KC + 1))
                act.copy(va1[:, c, :, 0:DH], bank[:, 2 + c // KC, (c % KC) * P:(c % KC + 1) * P]
                         .rearrange("p (h d) -> p h d", d=DH)).then_inc(S["va1_sb"], 1)
            act.wait_ge(S["bias1_ps"], 1)
            act.copy(bias[:, 1, :], bank[:, 6, 0:D]).then_inc(S["bias1_sb"], 1)
            act.wait_ge(S["yn_sb"], NT)
            act.copy(yn3[:, 0, :, :], yn[:]).then_inc(S["yn_p1"], 1)
            act.wait_ge(S["yn_r1"], 1)
            act.copy(yn3[:, 1, :, :], ynr[:]).then_inc(S["yn_p2"], 1)
            act.wait_ge(S["sel0T_ps"], NT)
            for c in range(PR0):
                act.copy(sel0T[:, c, :], bank[:, c, 0:T // 2].bitcast(BF16)).then_inc(S["sel0T_sb"], 1)
            for c in range(PR0):
                act.wait_ge(S["hid_sb"], c + 1)
                act.activation(hidg[:, c, :, :, :], hid[:, c, :, :, :], ACT.Gelu_apprx_tanh).then_inc(S["hidg_sb"], 1)
            copies("nT2_ps", "nT2_sb", lambda i: normedT[2][:, i, :], lambda i: bank[:, 2 + i, 0:P])
            for i in range(NT):
                act.wait_ge(S["q1_ps"], i + 1)
                act.activation(q1[:, i * P:(i + 1) * P], bank[:, SCB[i], 0:P], ACT.Identity, bias=vec(V_BQ1))\
                    .then_inc(S["q1_sb"], 1)
            act.wait_ge(S["qpack_zero"], 1)

            def pack(h):
                act.wait_ge(S["qp_ps"], h + 1)
                act.copy(qpack[0:NROW, h, :], bank[0:NROW, PACKB[min(h, GH)], :]).then_inc(S["qpack_sb"], 1)

            act.activation(sig[:, 0, :], gates_sb[:], ACT.Exp)
            pack(0)
            pack(1)
            for s in range(UNITS + 5):
                for j in range(GH):
                    if j == 0 and 0 <= s - 4 < UNITS:
                        u = s - 4
                        act.wait_ge(S["pv1_ps"], u + 1)
                        if u >= 2:
                            act.wait_ge(S["ring_full"], OUT_ITEM[u - 2])
                        act.copy(outT1[:, u % 2, :], bank[:, 6, 0:SQ]).then_inc(S["outT1_sb"], 1)
                    if 0 <= s - 2 < UNITS:
                        n = (s - 2) * GH + j
                        act.wait_ge(S["s1_ps"], n + 1)
                        if s - 2 >= 2:
                            act.wait_ge(S["pv1_ps"], s - 3)
                        act.activation(probs1[:, n % (2 * GH), :, :],
                                       bank[:, 2 + 2 * (n % 2):4 + 2 * (n % 2), :], ACT.Exp, scale=SCALE)\
                            .then_inc(S["probs1_sb"], 1)
                    if j == max_slot(s) and 0 <= s - 1 < UNITS:
                        u = s - 1
                        act.wait_ge(S["mrow_ps"], u + 1)
                        if u >= 2:
                            act.wait_ge(S["mrow_in"], 32 * (u - 1))
                        act.copy(mrow[:, u % 2, :], bank[0:2 * GH, RING_BANK[RING.index(("max", u))], :].bitcast(BF16)[:, 0:SQ]).then_inc(S["mrow_sb"], 1)
                    if s * GH + j + 2 < H:
                        pack(s * GH + j + 2)
            copies("attT1_ps", "attT1_sb", lambda i: attT[1][:, i, :], lambda i: bank[:, 2 + i, 0:P])
            copies("nT3_ps", "nT3_sb", lambda i: normedT[3][:, i, :], lambda i: bank[:, 2 + i, 0:P])
            act.wait_ge(S["mx16_sb"], 1)
            act.activation(sig[:, 0, :], mx16[:], ACT.Exp, scale=-1.0).then_inc(S["sig_e"], 1)
            for f in range(SFC):
                act.wait_ge(S["shg_ps"], f + 1)
                if f >= 2:
                    act.wait_ge(S["shh_sb"], f - 1)
                act.activation(sgate[:, f % 2, :], bank[:, 2 + 2 * (f % 2), :], ACT.Silu).then_inc(S["shg_sb"], 1)
                if f == 0:
                    act.wait_ge(S["zn_sb"], NT)
                    act.copy(zn3[:, 0, :, :], zn[:]).then_inc(S["zn_p1"], 1)
                if f == 1:
                    act.wait_ge(S["zn_r1"], 1)
                    act.copy(zn3[:, 1, :, :], znr[:]).then_inc(S["zn_p2"], 1)
            act.wait_ge(S["sel1T_ps"], NT)
            for c in reversed(range(PC1)):
                act.copy(sel1T[:, c, :], bank[:, SELB[c], :].bitcast(BF16)[:, (c % 2) * T:(c % 2 + 1) * T])\
                    .then_inc(S["sel1T_sb"], 1)
            for w, n in ((0, T), (1, PLACES - T)):
                act.wait_ge(S["zT_ps"], w + 1)
                act.copy(zT[:, w * T:w * T + n], bank[:, 6 + w, 0:n]).then_inc(S["zT_sb"], 1)
            act.wait_ge(S["gu_ps"], 1)
            act.activation(gate1, bank[:, 0:2, :].rearrange("p b n -> p (b n)")[:, 0:WIDE], ACT.Silu)\
                .then_inc(S["gate1_sb"], 1)
            act.wait_ge(S["down_ps"], 1)
            act.copy(moe1T, bank[:, 2:4, :].rearrange("p b n -> p (b n)")[:, 0:PLACES]).then_inc(S["moe1T_sb"], 1)
            act.wait_ge(S["moe1_ps"], 1)
            act.copy(moe1, bank[:, 4:6, :].rearrange("p b n -> p (b n)")[:, 0:PLACES]).then_inc(S["moe1_sb"], 1)

        @block.vector
        def _(dve):
            chain = [0]

            def link(ins):
                chain[0] += 1
                ins.then_inc(S["vchain"], 1)
                dve.wait_ge(S["vchain"], chain[0])

            def ln_stats(k, i, src):
                link(dve.bn_stats(stats[:, k, i, :], src))
                dve.bn_aggr(meanvar[:, k, i, :], stats[:, k, i, :]).then_inc(LN_MV[k], 1)

            def ln_apply(k, i):
                dve.wait_ge(LN_RS[k], i + 1)
                dve.tensor_scalar(normed[k][:, i, :], ln_in[k][:, i, :], meanvar[:, k, i, 0:1], rstd[:, k, i:i + 1],
                                  ALU.subtract, ALU.mult).then_inc(LN_N, 1)

            dve.wait_ge(L["x"], 16)
            for i in range(NT):
                ln_stats(0, i, x_sb[:, i, :])
            dve.wait_ge(L["small"], 16)
            for l, v in ((0, V_BV), (1, V_BV1)):
                dve.tensor_copy(bvcol[:, l, :], vec(v).to_broadcast([P, P])).then_inc(S["bvcol_set"], 1)
            for i in range(NT):
                ln_apply(0, i)
            dve.wait_ge(L["const"], 16)
            he = const_sb[:, K_HE:K_HE + H]
            hs = const_sb[:, K_HS:K_HS + H]
            for c in range(NB * KC):
                dve.tensor_copy(va0[:, c, :, DH:DH + 1], hs.unsqueeze(2))
            for b in range(NB):
                dve.wait_ge(S["k0_ps"], b + 1)
                dve.scalar_tensor_tensor(
                    out=k0[:, b, :].rearrange("p (j h) -> p j h", h=H),
                    in0=bank[:, b, :].rearrange("p (j h) -> p j h", h=H), scalar=vec(V_BK),
                    in1=he.unsqueeze(1).to_broadcast([P, SK // H, H]), op0=ALU.add, op1=ALU.mult)\
                    .then_inc(S["k0_sb"], 1)

            def masked_v(b):
                dve.wait_ge(S["v0_ps"], (b + 1) * KC)
                for c in range(b * KC, (b + 1) * KC):
                    dve.tensor_tensor(va0[:, c, :, 0:DH],
                                      bank[:, 2 + b, (c % KC) * P:(c % KC + 1) * P].rearrange("p (h d) -> p h d", d=DH),
                                      hs.unsqueeze(2).to_broadcast([P, H, DH]), ALU.mult).then_inc(S["va0_sb"], 1)

            for i in range(NT):
                dve.wait_ge(S["sc0_ps"], i + 1)
                s_v = bank[:, 4 + i, :].rearrange("p (j h) -> p j h", h=H)
                link(dve.tensor_reduce(mx0[:, i, :], bank[:, 4 + i, :].rearrange("p (j h) -> p h j", h=H), AX_X, ALU.max))
                dve.tensor_tensor(shifted[:, i, :].rearrange("p (j h) -> p j h", h=H), s_v,
                                  mx0[:, i, :].unsqueeze(1).to_broadcast([P, SK // H, H]), ALU.subtract)\
                    .then_inc(S["shift0"], 1)
                if i in (1, 2):
                    masked_v(i - 1)
            dve.tensor_copy(tri_bf[:], const_sb[:, K_TRI:K_TRI + P]).then_inc(S["consts_bf"], 1)
            dve.tensor_copy(ones_bf[:], const_sb[:, K_ONE:K_ONE + P]).then_inc(S["consts_bf"], 1)
            dve.tensor_copy(ident_bf[:], ident).then_inc(S["consts_bf"], 1)
            dve.tensor_copy(iota_bf[:], const_sb[:, K_IOTA:K_IOTA + CAP0]).then_inc(S["consts_bf"], 1)
            for i in range(NT):
                dve.wait_ge(S["pv0_ps"], i + 1)
                pv = bank[:, 4 + i, 0:H * (DH + 1)].rearrange("p (h d) -> p h d", d=DH + 1)
                link(dve.reciprocal(rden0[:, i, :].unsqueeze(2), pv[:, :, DH:DH + 1]))
                dve.tensor_tensor(att[0][:, i, :, :], pv[:, :, 0:DH],
                                  rden0[:, i, :].unsqueeze(2).to_broadcast([P, H, DH]), ALU.mult).then_inc(S["att0"], 1)
            for i in range(NT):
                dve.wait_ge(S["o0_ps"], i + 1)
                dve.wait_ge(S["xb0"], i + 1)
                dve.scalar_tensor_tensor(out=res[0][:, i, :], in0=bank[:, 4 + i, 0:D], scalar=tanhg[:, 0:1],
                                         in1=xb_sb[:, i, :], op0=ALU.mult, op1=ALU.add).then_inc(RES, 1)
                dve.wait_ge(RES, 0 * NT + i + 1)
                ln_stats(1, i, res[0][:, i, :])
            for i in range(NT):
                ln_apply(1, i)
            for i in range(NT):
                dve.wait_ge(LN_N, 1 * NT + i + 1)
                ln_stats(4, i, normed[1][:, i, :])
            dve.wait_ge(S["lg0_ps"], NT)
            lg = bank[:, 4, 0:NT * E0].rearrange("p (i e) -> p i e", e=E0)
            link(dve.tensor_reduce(mxe[:], lg, AX_X, ALU.max))
            dve.tensor_tensor(ex[:], lg, mxe[:].unsqueeze(2).to_broadcast([P, NT, E0]), ALU.subtract).then_inc(S["sh0"], 1)
            dve.wait_ge(S["ex0"], 1)
            link(dve.tensor_reduce(sme[:], ex[:], AX_X, ALU.add))
            link(dve.reciprocal(sme[:], sme[:]))
            dve.tensor_tensor(score[:], ex[:], sme[:].unsqueeze(2).to_broadcast([P, NT, E0]), ALU.mult)\
                .then_inc(S["score_sb"], 1)
            dve.wait_ge(S["scT_ps"], 1)
            link(dve.tensor_copy(scoreT, bank[0:E0, 5, :]))
            src = scoreT
            for r in range(CAP0 // 8):
                link(dve.max(top8[:, r, :], src))
                link(dve.match_replace(work[:, r % 2, :], top8[:, r, :], src, -1.0))
                src = work[:, r % 2, :]
            dve.tensor_scalar(chosenT[:], src, 0.0, None, ALU.is_lt).then_inc(S["chosenT_sb"], 1)
            dve.wait_ge(S["chosen_ps"], 1)
            dve.tensor_copy(chosen[:], bank[:, 6, 0:NT * E0].rearrange("p (i e) -> p i e", e=E0))\
                .then_inc(S["chosen_sb"], 1)
            dve.wait_ge(S["chosen_sb"], 1)
            dve.wait_ge(S["cum0_ps"], 1)
            link(dve.scalar_tensor_tensor(out=slot0[:], in0=bank[:, 7, 0:NT * E0].rearrange("p (i e) -> p i e", e=E0),
                                          scalar=1.0, in1=chosen[:], op0=ALU.add, op1=ALU.mult))
            for i in range(NT):
                dve.tensor_tensor(sel0[:, i, :, :], iota_bf[:].unsqueeze(1).to_broadcast([P, E0, CAP0]),
                                  slot0[:, i, :].unsqueeze(2).to_broadcast([P, E0, CAP0]), ALU.is_equal)\
                    .then_inc(S["sel0_sb"], 1)
            dve.wait_ge(S["yT_ps"], 1)
            dve.tensor_scalar(yT[:], bank[:, 4, :], vec(V_LNW), vec(V_LNB), ALU.mult, ALU.add).then_inc(S["yT_sb"], 1)
            dve.wait_ge(S["kept_ps"], 1)
            link(dve.tensor_tensor(keptp[:], bank[:, 5, 0:PR0 * 3 * E0].rearrange("p (c k) -> p c k", k=3 * E0),
                                   const_sb[:, K_WSEL:K_WSEL + PR0 * 3 * E0].rearrange("p (c k) -> p c k", k=3 * E0),
                                   ALU.mult))
            dve.tensor_reduce(kept[:], keptp[:], AX_X, ALU.add).then_inc(S["kept_sb"], 1)
            for c in range(PR0):
                dve.wait_ge(S["fc1_ps"], c + 1)
                dve.tensor_tensor(
                    hid[:, c, :, :, :].rearrange("p u f s -> p (u f) s"),
                    bank[:, SCB[c], :].rearrange("p (k s) -> p k s", s=CAP0),
                    small_sb[:, C_B1 + 2 * FC0 * c:C_B1 + 2 * FC0 * (c + 1)].unsqueeze(2)
                    .to_broadcast([P, 2 * FC0, CAP0]), ALU.add).then_inc(S["hid_sb"], 1)
            for c in range(PR0):
                dve.wait_ge(S["fc2_ps"], c + 1)
                dve.wait_ge(S["b2w_sb"], c + 1)
                dve.scalar_tensor_tensor(out=moe0[:, c, :], in0=bank[:, 2 + c, 0:D], scalar=kept[:, c:c + 1],
                                         in1=b2w[:, c, :], op0=ALU.mult, op1=ALU.add).then_inc(S["moe0_sb"], 1)
            for i in range(NT):
                dve.wait_ge(S["sc_ps"], i + 1)
                dve.wait_ge(S["xg_sb"], i + 1)
                dve.scalar_tensor_tensor(out=res[1][:, i, :], in0=bank[:, SCB[i], 0:D], scalar=tanhg[:, 2:3],
                                         in1=xg[:, i, :], op0=ALU.mult, op1=ALU.add).then_inc(RES, 1)
                dve.wait_ge(RES, 1 * NT + i + 1)
                ln_stats(2, i, res[1][:, i, :])
            for i in range(NT):
                ln_apply(2, i)
            dve.wait_ge(S["q1_sb"], NT)
            link(dve.tensor_copy(q3[:, 0, :], q1[:]))
            link(dve.tensor_tensor(q1r[:], q1[:], q3[:, 0, :], ALU.subtract))
            link(dve.tensor_copy(q3[:, 1, :], q1r[:]))
            dve.tensor_tensor(q3[:, 2, :], q1r[:], q3[:, 1, :], ALU.subtract).then_inc(S["q3_sb"], 1)

            high_at = {}

            def unit_max(u):
                b, g = divmod(u, NG)
                return mx1[:, b * 2:b * 2 + 2, g * GH:(g + 1) * GH]

            def max_high(u):
                dve.wait_ge(S["ring_free"], MAXED[u])
                if u >= 2:
                    dve.wait_ge(S["mrow_ps"], u - 1)
                dve.tensor_scalar(minus_max[:, u % 2, :, 0, :], unit_max(u), -1.0, None, ALU.mult).then_inc(S["vchain"], 1)
                chain[0] += 1
                high_at[u] = chain[0]

            def max_low(u):
                dve.wait_ge(S["vchain"], high_at[u])
                dve.scalar_tensor_tensor(out=minus_max[:, u % 2, :, 1, :], in0=unit_max(u), scalar=-1.0,
                                         in1=minus_max[:, u % 2, :, 0, :], op0=ALU.mult, op1=ALU.subtract)\
                    .then_inc(S["minus_max_set"], 1)

            for n, item in enumerate(RING):
                if item[0] == "max":
                    continue
                dve.wait_ge(S["ring_full"], READ[n])
                r = RING_BANK[n]
                if item[0] == "score":
                    _, u, j, qt = item
                    b, g = divmod(u, NG)
                    dve.tensor_reduce(mx1[:, b * 2 + qt, g * GH + j:g * GH + j + 1], bank[:, r, :], AX_X, ALU.max)\
                        .then_inc(S["ring_free"], 1)
                    if j == 0 and u >= 1:
                        (max_low if qt else max_high)(u - 1)
                    if (u, j, qt) == (UNITS - 1, GH - 1, 1):
                        max_high(u)
                        max_low(u)
                else:
                    u = item[1]
                    b, g = divmod(u, NG)
                    o = bank[:, r, 0:2 * P].rearrange("p (t h d) -> p t h d", t=2, d=32)
                    rd = rden1[:, b * 2:b * 2 + 2, g * GH:(g + 1) * GH]
                    link(dve.reciprocal(rd.unsqueeze(3), o[:, :, :, DH:DH + 1]))
                    dve.tensor_tensor(att[1][:, b * 2:b * 2 + 2, g * GH:(g + 1) * GH, :], o[:, :, :, 0:DH],
                                      rd.unsqueeze(3).to_broadcast([P, 2, GH, DH]), ALU.mult)\
                        .then_inc(S["ring_free"], 1)
            for i in range(NT):
                dve.wait_ge(S["o1_ps"], i + 1)
                dve.wait_ge(S["xb1"], i + 1)
                dve.scalar_tensor_tensor(out=res[2][:, i, :], in0=bank[:, SCB[i], 0:D], scalar=tanhg[:, 1:2],
                                         in1=xb_sb[:, i, :], op0=ALU.mult, op1=ALU.add).then_inc(RES, 1)
                dve.wait_ge(RES, 2 * NT + i + 1)
                ln_stats(3, i, res[2][:, i, :])
            for i in range(NT):
                ln_apply(3, i)
            dve.wait_ge(S["lg1_ps"], NT)
            lg1 = bank[:, 6, 0:NT * E1].rearrange("p (i e) -> p i e", e=E1)
            rank = const_sb[:, K_RANK:K_RANK + E1].unsqueeze(1).to_broadcast([P, NT, E1])
            dve.tensor_reduce(mx16[:], lg1, AX_X, ALU.max).then_inc(S["mx16_sb"], 1)
            dve.wait_ge(S["mx16_sb"], 1)
            link(dve.tensor_tensor(eq16[:], lg1, mx16[:].unsqueeze(2).to_broadcast([P, NT, E1]), ALU.is_equal))
            link(dve.tensor_tensor(eq16[:], eq16[:], rank, ALU.mult))
            link(dve.tensor_reduce(kmax[:], eq16[:], AX_X, ALU.max))
            dve.tensor_tensor(oh[:], eq16[:], kmax[:].unsqueeze(2).to_broadcast([P, NT, E1]), ALU.is_equal)\
                .then_inc(S["oh_sb"], 1)
            dve.wait_ge(S["sig_e"], 1)
            link(dve.tensor_scalar(sig[:, 1, :], sig[:, 0, :], 1.0, None, ALU.add))
            dve.reciprocal(sig[:, 2, :], sig[:, 1, :]).then_inc(S["sigma_sb"], 1)

            def shared_hidden(f):
                dve.wait_ge(S["shg_sb"], f + 1)
                dve.tensor_tensor(shh[:, f, :], bank[:, 3 + 2 * (f % 2), :], sgate[:, f % 2, :], ALU.mult)\
                    .then_inc(S["shh_sb"], 1)

            dve.wait_ge(S["count_ps"], 1)
            link(dve.tensor_copy(count[:], bank[:, 6, NT * E1:(NT + 1) * E1]))
            link(dve.tensor_tensor_scan(upto[:], const_sb[:, K_ONE:K_ONE + E1], count[:], 0.0, ALU.mult, ALU.add))
            link(dve.tensor_tensor(start[:], upto[:], count[:], ALU.subtract))
            link(dve.tensor_scalar(start_moved[:], start[:], float(LAST), float(WIN), ALU.is_gt, ALU.mult))
            link(dve.tensor_tensor(start[:], start[:], start_moved[:], ALU.add))
            dve.tensor_copy(starts_int[:], start[0:1, :]).then_inc(S["starts_set"], 1)
            dve.wait_ge(S["cum1_ps"], 1)
            link(dve.tensor_tensor(placed[:], bank[:, 7, 0:NT * E1].rearrange("p (i e) -> p i e", e=E1),
                                   start[:].unsqueeze(1).to_broadcast([P, NT, E1]), ALU.add))
            link(dve.tensor_tensor(placed[:], placed[:], oh[:], ALU.mult))
            link(dve.tensor_reduce(place[:], placed[:], AX_X, ALU.add))
            shared_hidden(0)
            shared_hidden(1)
            dve.wait_ge(S["iota_places_set"], 1)
            for i in range(NT):
                dve.tensor_scalar(sel1[:, i, :], iota_places, place[:, i:i + 1], None, ALU.is_equal)\
                    .then_inc(S["sel1_sb"], 1)
            shared_hidden(2)
            shared_hidden(3)
            link(dve.tensor_tensor(last_start[:], start[:], count[:], ALU.add))
            link(dve.tensor_scalar(last_start[:], last_start[:], float(-WIN), None, ALU.add))
            for k in range(MORE):
                link(dve.scalar_tensor_tensor(out=clipped[:], in0=start[0:1, :], scalar=float(k * WIN),
                                              in1=last_start[0:1, :], op0=ALU.add, op1=ALU.min))
                link(dve.tensor_tensor(general_int[0:1, k:E1 * MORE:MORE], clipped[:], start[0:1, :], ALU.max))
            link(dve.tensor_reduce(most[:], count[0:1, :], AX_X, ALU.max))
            dve.tensor_copy(most_int[:], most[:]).then_inc(S["general_set"], 1)
            dve.wait_ge(S["gate1_sb"], 1)
            dve.tensor_tensor(hid1, bank[:, 4:6, :].rearrange("p b n -> p (b n)")[:, 0:WIDE], gate1, ALU.mult)\
                .then_inc(S["hid1_sb"], 1)
            dve.wait_ge(S["shd_ps"], 1)
            for i in range(NT):
                dve.scalar_tensor_tensor(out=xs[:, i, :], in0=bank[:, 6, i * P:(i + 1) * P], scalar=tanhg[:, 3:4],
                                         in1=res[2][:, i, :], op0=ALU.mult, op1=ALU.add).then_inc(S["xs_sb"], 1)
            for i in range(NT):
                dve.wait_ge(S["final_ps"], i + 1)
                dve.wait_ge(S["xs_sb"], i + 1)
                dve.scalar_tensor_tensor(out=res[3][:, i, :], in0=bank[:, FINB[i], 0:D], scalar=tanhg[:, 3:4],
                                         in1=xs[:, i, :], op0=ALU.mult, op1=ALU.add).then_inc(S["res3"], 1)


def max_slot(s):
    return 1 if s < UNITS else 0


def ring_items():
    items = []
    for s in range(UNITS + 5):
        for j in range(GH):
            if s < UNITS:
                items += [("score", s, j, 0), ("score", s, j, 1)]
            if j == max_slot(s) and 0 <= s - 1 < UNITS:
                items.append(("max", s - 1))
            if j == 2 and 0 <= s - 4 < UNITS:
                items.append(("out", s - 4))
    return items


RING = ring_items()
PACKING = RING.index(("score", (H - 2) // GH, (H - 2) % GH, 0))
RING_BANK = [n % 2 if n < PACKING else (7, 0, 1)[(n - PACKING) % 3] for n in range(len(RING))]
READ = [sum(it[0] != "max" for it in RING[:n + 1]) for n in range(len(RING))]
MAXED = [READ[RING.index(("score", u, GH - 1, 1))] for u in range(UNITS)]
OUT_ITEM = [READ[RING.index(("out", u))] for u in range(UNITS)]



def kernel(**a):
    import numpy as np
    import concourse.bacc as bacc
    from concourse.bass_utils import run_bass_kernel_spmd as run

    a = {k: np.asarray(v) for k, v in a.items()}
    f32 = np.float32
    tiles = a["x"].reshape(NT, P, D).transpose(1, 0, 2)
    col = lambda n: a[n].reshape(D, 1)
    small = np.concatenate(
        [col("L0_xattn_bq"), col("L0_xattn_bk"), col("L0_xattn_bv"), col("L0_ffn_ln_w"), col("L0_ffn_ln_b"),
         col("L1_xattn_b_Q"), col("L1_xattn_b_K"), col("L1_xattn_b_V"),
         a["L0_ffn_b1s"].reshape(E0 * FC0, P).T, a["L0_ffn_gate_w"].T, a["L1_ffn_router_w"].T], axis=1)
    p = np.arange(P)
    heads = np.arange(H)
    wsel = np.zeros((P, PR0, 3, E0), f32)
    for c in range(PR0):
        for u in range(2):
            wsel[u * CAP0:(u + 1) * CAP0, c, :, 2 * c + u] = 1
    consts = np.concatenate(
        [np.eye(P, dtype=f32), (p[:, None] // DH == heads).astype(f32), (p[:, None] % H == heads).astype(f32),
         np.tile(np.arange(E1, 0, -1, dtype=f32), (P, 1)), wsel.reshape(P, -1),
         (p[:, None] < p[None, :]).astype(f32), np.tile(np.arange(1, CAP0 + 1, dtype=f32), (P, 1)),
         np.ones((P, P), f32)], axis=1)
    selq = np.zeros((P, 3, H, NROW), mybir.dt.np(BF16))
    for n, (i, j) in enumerate(TERMS):
        for h in range(H):
            for d in range(DH):
                selq[h * DH + d, i, h, n * DH + d] = 1
    b2 = np.repeat(a["L0_ffn_b2s"].reshape(PR0, 2, D).transpose(1, 0, 2), CAP0, axis=0)
    arrays = {
        "x": tiles, "small": small, "consts": consts, "selq": selq, "onerows": np.ones((2, H, NB * SK), mybir.dt.np(BF16)),
        "gates": np.tile(np.concatenate([a["g_xattn"], a["g_ffn"]]), (P, 1)),
        "rows": np.stack([a["L0_xattn_bo"], a["L1_xattn_b_O"]])[None],
        "ctxT": a["ctx_1024"].reshape(NB * SK, D).T,
        "w0": np.stack([a[f"L0_xattn_W{n}"].T for n in "qkvo"], axis=1),
        "w1": np.stack([a[f"L1_xattn_W_{n}"] for n in "QKVO"], axis=1),
        "fc1T": a["L0_ffn_fc1s"].transpose(2, 0, 1),
        "fc2": a["L0_ffn_fc2s"].transpose(2, 0, 1).reshape(FC0, P, E0, D).transpose(1, 2, 0, 3),
        "b2": b2,
        "shGU": np.stack([a["L1_ffn_shared_gate_w"].T, a["L1_ffn_shared_up_w"].T], axis=1),
        "shD": a["L1_ffn_shared_down_w"].T.reshape(SFC, P, D).transpose(1, 0, 2),
        "gateup": a["L1_ffn_gate_up_proj"].transpose(1, 0, 2),
        "down": a["L1_ffn_down_proj"].transpose(1, 0, 2),
    }
    nc = bacc.Bacc("TRN2", target_bir_lowering=False, num_devices=1)
    feed, aps = {}, {}
    for name, v in arrays.items():
        feed[f"in_{name}"] = np.ascontiguousarray(v)
        aps[name] = nc.dram_tensor(f"in_{name}", v.shape, mybir.dt.from_np(v.dtype), kind="ExternalInput").ap()
    kscr = nc.dram_tensor("k_parts", (P, 3, NB * SK), BF16).ap()
    out = nc.dram_tensor("out", (P, NT, D), F32, kind="ExternalOutput").ap()
    build(nc, **aps, kscr=kscr, out=out)
    r = run(nc, [feed], core_ids=[0])
    got = r.results[0]["out"]
    return np.ascontiguousarray(np.asarray(got).transpose(1, 0, 2)).reshape(NB, SQ, D)
```

```python
from contextlib import ExitStack

import concourse.bass as bass
from concourse import mybir

P = 128
D = 128
NB = 2
SQ = 256
SK = 512
T = NB * SQ
NT = T // P
KC = SK // P
H = 16
DH = D // H
EPS = 1e-5
SCALE = DH ** -0.5

E0 = 8
CAP0 = T // E0
FF0 = 512
FC0 = FF0 // P
PR0 = E0 * CAP0 // P

E1 = 16
F1 = 128
WIN = 128
LAST = T - WIN
PLACES = T + WIN
WIDE = PLACES + WIN
PC1 = PLACES // P
MORE = T // WIN
SF = 512
SFC = SF // P

TERMS = [(i, j) for i in range(3) for j in range(3)]
NROW = len(TERMS) * DH
MROW = NROW
TERM_END = 64
GH = 4
HPE = 8
NG = H // GH
UNITS = NB * NG

C_VEC = 0
V_BQ, V_BK, V_BV, V_LNW, V_LNB, V_BQ1, V_BK1, V_BV1 = range(8)
C_B1 = 8
C_GATE = C_B1 + E0 * FC0
C_ROUT = C_GATE + E0
C_END = C_ROUT + E1

K_ID = 0
K_HE = K_ID + P
K_HS = K_HE + H
K_RANK = K_HS + H
K_WSEL = K_RANK + E1
K_TRI = K_WSEL + PR0 * 3 * E0
K_IOTA = K_TRI + P
K_ONE = K_IOTA + CAP0
K_END = K_ONE + P

LN_ORDER = [0, 1, 4, 2, 3]


def ln_done(k, i):
    return LN_ORDER.index(k) * NT + i + 1


ALU = mybir.AluOpType
ACT = mybir.ActivationFunctionType
AX_X = mybir.AxisListType.X
F32 = mybir.dt.float32
BF16 = mybir.dt.bfloat16
I32 = mybir.dt.int32


def build(nc, x, small, consts, selq, onerows, gates, rows, ctxT, w0, w1, fc1T, fc2, b2, shGU, shD, gateup, down, kscr, qscr, out):
    with ExitStack() as ctx:
        def sb(name, shape, dt=F32):
            return ctx.enter_context(nc.sbuf_tensor(name, shape, dt))

        def sem(name):
            return ctx.enter_context(nc.semaphore(name))

        bank = ctx.enter_context(nc.psum_tensor("bank", [P, 8, 512], F32))

        x_sb = sb("x_sb", [P, NT, D])
        small_sb = sb("small_sb", [P, C_END])
        const_sb = sb("const_sb", [P, K_END])
        gates_sb = sb("gates_sb", [P, 4])
        rows_sb = sb("rows_sb", [1, 2, D])
        ctxT_sb = sb("ctxT_sb", [D, NB * SK])
        w0_sb = sb("w0_sb", [P, 4, D])
        w1_sb = sb("w1_sb", [P, 4, D])
        fc1T_sb = sb("fc1T_sb", [P, E0, FF0])
        fc2_sb = sb("fc2_sb", [P, E0, FC0, D])
        b2_sb = sb("b2_sb", [P, PR0, D])
        shGU_sb = sb("shGU_sb", [P, 2, SF])
        shD_sb = sb("shD_sb", [P, SFC, D])
        gateup_sb = fc2_sb[:].rearrange("p e f d -> p (e f d)").rearrange("p (e k) -> p e k", e=E1)

        ident = const_sb[:, K_ID:K_ID + P]

        def vec(n):
            return small_sb[:, C_VEC + n:C_VEC + n + 1]

        arena = sb("arena", [P, 6 * NT * SK])

        def at(pos, n, pattern, dt=F32, **k):
            v = arena[:, pos:pos + n]
            return (v.bitcast(dt) if dt is not F32 else v).rearrange(pattern, **k)

        def view(n, pattern, **k):
            return at(n * NT * SK, NT * SK, pattern, **k)

        down_sb = view(0, "p (e d) -> p e d", e=E1)

        res_b = sb("res_b", [P, NT, D])
        res = [res_b, x_sb, res_b, x_sb]
        ln_in = [x_sb, res[0], res[1], res[2]]
        normed = [sb(f"normed{k}", [P, NT, D]) for k in range(2)] * 2
        normedT = [sb(f"normedT{k}", [P, NT, P]) for k in range(2)] * 2
        stats = sb("stats", [P, 5, NT, 6])
        meanvar = sb("meanvar", [P, 5, NT, 2])
        rstd = sb("rstd", [P, 5, NT])
        minus_half = sb("minus_half", [P, NT])
        tanhg = sb("tanhg", [P, 4])
        tri_bf = sb("tri_bf", [P, P], BF16)
        ones_bf = sb("ones_bf", [P, P], BF16)
        ident_bf = sb("ident_bf", [P, P], BF16)
        selq_bf = sb("selq_bf", [P, 3, HPE, NROW], BF16)
        iota_bf = sb("iota_bf", [P, CAP0], BF16)
        zeros_bf = sb("zeros_bf", [P, P], BF16)
        bvcol = sb("bvcol", [P, 2, P])
        bias = sb("bias", [P, 2, D])
        gbias = sb("gbias", [P, 2, D])
        xb_sb = sb("xb", [P, NT, D])

        qpack = fc1T_sb[:].rearrange("p e f -> p (e f)").bitcast(BF16).rearrange("p (h t) -> p h t", h=H)
        kpack = sb("kpack", [P, H, NB * SK], BF16)
        late = kpack[:].rearrange("p h s -> p (h s)").bitcast(F32)

        def late_view(at, n, pattern, dt=F32, **k):
            v = late[:, at:at + n]
            return (v.bitcast(dt) if dt is not F32 else v).rearrange(pattern, **k)

        k0 = sb("k0", [P, NB, SK])
        va0 = sb("va0", [P, NB * KC, H, DH + 1])
        q0T = sb("q0T", [P, NT, P])
        mx0 = sb("mx0", [P, NT, H])
        shifted = view(0, "p (i s) -> p i s", i=NT)
        probs0 = view(1, "p (i s) -> p i s", i=NT)
        probs0T = view(2, "p (i s) -> p i s", i=NT)
        rden0 = sb("rden0", [P, NT, H])
        att = [sb("att", [P, NT, H, DH])] * 2
        attT = [sb("attT", [P, NT, P])] * 2

        ex = sb("ex", [P, NT, E0])
        mxe = sb("mxe", [P, NT])
        sme = sb("sme", [P, NT])
        score = sb("score", [P, NT, E0])
        score_hi = sb("score_hi", [P, NT, E0])
        score3 = sb("score3", [P, NT, 3, E0], BF16)
        scoreT = q0T[0:E0, :, :].rearrange("p i t -> p (i t)")
        work = k0[0:E0, :, :]
        top8 = sb("top8", [E0, 8, 8])
        chosenT = sb("chosenT", [E0, T])
        chosen = sb("chosen", [P, NT, E0], BF16)
        slot0 = sb("slot0", [P, NT, E0], BF16)
        sel0 = at(5 * 2048, 1024, "p (i e s) -> p i e s", BF16, i=NT, e=E0)
        sel0T = view(3, "p (c t) -> p c t", c=PR0)
        yn = at(2 * 2048, 512, "p (i d) -> p i d", i=NT)
        ynr = at(2 * 2048 + 512, 512, "p (i d) -> p i d", i=NT)
        yn3 = at(2 * 2048 + 1024, 768, "p (k i d) -> p k i d", BF16, k=3, i=NT)
        yT = arena[:, 5 * 2048 + 1024:5 * 2048 + 1536]
        keptp = sb("keptp", [P, PR0, 3 * E0])
        kept = sb("kept", [P, PR0])
        b2w = b2_sb
        hid = view(4, "p (c u f s) -> p c u f s", c=PR0, u=2, f=FC0)
        hidg = hid
        moe0 = at(5 * 2048 + 1536, 512, "p (c d) -> p c d", c=PR0)
        xg = sb("xg", [P, NT, D])

        k1 = arena[:, 0:1024]
        k1r = arena[:, 1024:2048]
        k3 = at(2048, 1536, "p (k s) -> p k s", BF16, k=3)
        va1 = sb("va1", [P, NB * KC, H, 32])
        q1 = ctxT_sb[:, 0:T]
        q1r = ctxT_sb[:, T:2 * T]
        q3 = va0[:].rearrange("p c h d -> p (c h d)")[:, 0:768].bitcast(BF16).rearrange("p (k t) -> p k t", k=3)
        mx1 = sb("mx1", [P, NT, H])
        minus_max = sb("minus_max", [P, 2, 2, 2, GH], BF16)
        mrow = sb("mrow", [2 * GH, 2, SQ], BF16)
        probs1 = arena[:, 0:2 * GH * KC * SQ].rearrange("p (n c q) -> p n c q", n=2 * GH, c=KC)
        outT1 = sb("outT1", [P, 2, SQ])
        rden1 = sb("rden1", [P, NT, H])

        va1_flat = va1[:].rearrange("p c h w -> p (c h w)")

        mx16 = sb("mx16", [P, NT])
        eq16 = sb("eq16", [P, NT, E1])
        kmax = sb("kmax", [P, NT])
        sig = sb("sig", [P, 3, NT])
        oh = sb("oh", [P, NT, E1], BF16)
        count = sb("count", [P, E1])
        upto = sb("upto", [P, E1])
        start = sb("start", [P, E1])
        start_moved = sb("start_moved", [P, E1])
        last_start = sb("last_start", [P, E1])
        clipped = sb("clipped", [1, E1])
        placed = sb("placed", [P, NT, E1])
        place = sb("place", [P, NT])
        starts_int = sb("starts_int", [1, E1], I32)
        general_int = sb("general_int", [1, E1 * MORE], I32)
        most = sb("most", [1, 1])
        most_int = sb("most_int", [1, 1], I32)
        zn = va1_flat[:, 0:512].rearrange("p (i d) -> p i d", i=NT)
        znr = va1_flat[:, 512:1024].rearrange("p (i d) -> p i d", i=NT)
        zn3 = va1_flat[:, 1024:1792].bitcast(BF16).rearrange("p (k i d) -> p k i d", k=3, i=NT)
        sel1 = late_view(0, 1280, "p (i s) -> p i s", BF16, i=NT)
        sel1T = at(2 * GH * KC * SQ, PC1 * T, "p (c t) -> p c t", c=PC1)
        zT = late_view(1280, WIDE, "p s -> p s")
        sgate = va1_flat[:, 1792:2816].rearrange("p (k s) -> p k s", k=2)
        shh = late_view(2048, 2048, "p (f t) -> p f t", f=SFC)
        xs = va1_flat[:, 2816:3328].rearrange("p (i d) -> p i d", i=NT)
        gate1 = late_view(4096, WIDE, "p s -> p s")
        hid1 = late_view(4864, WIDE, "p s -> p s")
        moe1T = late_view(5632, PLACES, "p s -> p s")
        moe1 = late_view(6272, PLACES, "p (c d) -> p c d", c=PC1)
        iota_places = late_view(6912, PLACES, "p s -> p s")

        L = {n: sem("load_" + n) for n in ("x", "small", "const", "gates", "rows", "ctx", "selq", "w0", "w1", "fc1", "fc2",
                                           "b2", "sh", "gu", "down")}
        S = {n: sem(n) for n in (
            "half_set", "vchain", "gchain", "tanh_done", "consts_bf", "bvcol_set", "k0_ps", "v0_ps", "k0_sb",
            "va0_sb", "bias0_ps", "bias0_sb", "xb0", "xb1", "nT0_ps", "nT0_sb", "q0_ps", "q0_sb", "sc0_ps",
            "shift0", "probs0_sb", "p0T_ps", "p0T_sb", "pv0_ps", "att0", "attT0_ps", "attT0_sb", "o0_ps", "nT1_ps",
            "nT1_sb", "lg0_ps", "sh0", "ex0", "score_sb", "scT_ps", "chosenT_sb", "chosen_ps", "chosen_sb",
            "cum0_ps", "sel0_sb", "sel0T_ps", "sel0T_sb", "yn_sb", "yn_p1", "yn_r1", "yn_p2", "yn_p3", "score3_sb",
            "yT_ps", "yT_sb", "kept_ps", "kept_sb", "b2w_sb", "fc1_ps", "hid_sb", "hidg_sb", "fc2_ps", "moe0_sb",
            "sc_ps", "xg_sb", "k1_ps", "v1_ps", "bias1_ps", "k1_sb", "va1_zero", "va1_sb", "bias1_sb", "k3_sb",
            "kpack_zero", "qpack_zero", "kpack_in", "nT2_ps", "nT2_sb", "q1_ps", "q1_sb", "q3_sb", "ring_full",
            "ring_free", "minus_max_set", "mrow_ps", "mrow_sb", "mrow_in", "qp_ps", "qpack_sb", "scr_out",
            "qpack_in", "s1_ps", "probs1_sb", "pv1_ps", "outT1_sb", "attT1_ps", "attT1_sb", "o1_ps", "nT3_ps",
            "nT3_sb", "lg1_ps", "mx16_sb", "sig_e", "oh_sb", "cum1_ps", "sel1_sb", "zn_sb", "zn_p1", "zn_r1",
            "zn_p2", "zn_p3", "shg_ps", "shg_sb", "shh_sb", "shd_ps", "xs_sb", "sel1T_ps", "sel1T_sb", "zT_ps",
            "zT_sb", "gu_ps", "gate1_sb", "hid1_sb", "down_ps", "moe1T_sb", "moe1_ps", "moe1_sb",
            "iota_places_set", "count_ps", "starts_set", "general_set", "final_ps", "res3", "sigma_sb", "stored")}
        LN_MV = sem("ln_meanvar")
        LN_RS = sem("ln_rstd")
        RES = sem("residual")
        LN_N = sem("ln_normed")

        PACKB = [6, 2, 3, 4] + [6, 7] * ((HPE - GH) // 2)
        TAILT = [1, 7]
        TAILO = [0, 6]
        SHB = [2, 4, 0, 2]
        SELB = [4, 4, 5, 5, 7]
        FINB = [0, 1, 4, 5]
        SCB = [6, 7, 0, 1]

        block = ctx.enter_context(nc.Block())

        @block.sync
        def _(sp):
            sp.dma_start(x_sb[:], x).then_inc(L["x"], 16)
            sp.dma_start(w0_sb[:], w0).then_inc(L["w0"], 16)
            sp.dma_start(ctxT_sb[:], ctxT).then_inc(L["ctx"], 16)
            sp.dma_start(const_sb[:], consts).then_inc(L["const"], 16)
            sp.dma_start(w1_sb[:], w1).then_inc(L["w1"], 16)
            sp.dma_start(selq_bf[:], selq).then_inc(L["selq"], 16)
            sp.dma_start(fc1T_sb[:], fc1T).then_inc(L["fc1"], 16)
            sp.dma_start(fc2_sb[:], fc2).then_inc(L["fc2"], 16)
            sp.dma_start(shGU_sb[:], shGU).then_inc(L["sh"], 16)
            sp.dma_start(shD_sb[:], shD).then_inc(L["sh"], 16)
            sp.wait_ge(S["kpack_zero"], 1)
            sp.dma_start(kpack[MROW:MROW + 2, :, :], onerows).then_inc(S["kpack_in"], 16)

            sp.wait_ge(S["k3_sb"], 1)
            sp.dma_start(kscr, k3[:]).then_inc(S["scr_out"], 16)
            sp.wait_ge(S["scr_out"], 16)
            for n, (i, j) in enumerate(TERMS):
                sp.dma_start(kpack[n * DH:(n + 1) * DH, :, :],
                             kscr[:, j, :].rearrange("(h d) s -> d h s", d=DH)).then_inc(S["kpack_in"], 16)
            sp.wait_ge(S["fc2_ps"], PR0)
            sp.dma_start(gateup_sb, gateup).then_inc(L["gu"], 16)
            sp.wait_ge(S["q3_sb"], 1)
            sp.dma_start(qscr, q3[HPE * DH:, :, :]).then_inc(S["scr_out"], 16)
            sp.wait_ge(S["scr_out"], 32)
            sp.wait_ge(S["qpack_zero"], 1)
            for n, (i, j) in enumerate(TERMS):
                sp.dma_start(qpack[n * DH:(n + 1) * DH, HPE:, :],
                             qscr[:, i, :].rearrange("(h d) t -> d h t", d=DH)).then_inc(S["qpack_in"], 16)
            for u in range(UNITS):
                b, g = divmod(u, NG)
                sp.wait_ge(S["mrow_sb"], u + 1)
                for part in range(2):
                    sp.dma_start(qpack[MROW + part:MROW + part + 1, g * GH:(g + 1) * GH, b * SQ:(b + 1) * SQ],
                                 mrow[part * GH:(part + 1) * GH, u % 2, :]).then_inc(S["mrow_in"], 16)
            sp.wait_ge(S["pv1_ps"], UNITS)
            sp.dma_start(down_sb, down).then_inc(L["down"], 16)
            for i in range(NT):
                sp.wait_ge(S["res3"], i + 1)
                sp.dma_start(out[:, i, :], res[3][:, i, :]).then_inc(S["stored"], 16)
            sp.wait_ge(S["stored"], 16 * NT)

        @block.gpsimd
        def _(pool):
            pool.dma_start(small_sb[:], small).then_inc(L["small"], 16)
            pool.dma_start(gates_sb[:], gates).then_inc(L["gates"], 16)
            pool.dma_start(rows_sb[:], rows).then_inc(L["rows"], 16)
            pool.dma_start(b2_sb[:], b2).then_inc(L["b2"], 16)
            pool.memset(minus_half[:], -0.5).then_inc(S["half_set"], 1)
            pool.memset(zeros_bf[:], 0.0).then_inc(S["half_set"], 1)
            pool.wait_ge(S["half_set"], 1)

            def ln_rstd(k, i):
                pool.wait_ge(LN_MV, ln_done(k, i))
                pool.tensor_scalar(rstd[:, k, i:i + 1], meanvar[:, k, i, 1:2], EPS, None, ALU.add)\
                    .then_inc(S["gchain"], 1)
                gc[0] += 1
                pool.wait_ge(S["gchain"], gc[0])
                pool.tensor_tensor(rstd[:, k, i:i + 1], rstd[:, k, i:i + 1], minus_half[:, i:i + 1], ALU.pow)\
                    .then_inc(LN_RS, 1)

            gc = [0]

            def link(ins):
                gc[0] += 1
                ins.then_inc(S["gchain"], 1)
                pool.wait_ge(S["gchain"], gc[0])

            def residual_bias(l, src):
                pool.wait_ge(S["tanh_done"], 1)
                pool.wait_ge(S[f"bias{l}_sb"], 1)
                link(pool.tensor_scalar(gbias[:, l, :], bias[:, l, :], tanhg[:, l:l + 1], None, ALU.mult))
                if l:
                    pool.wait_ge(RES, (1 + 1) * NT)
                for i in range(NT):
                    pool.tensor_tensor(xb_sb[:, i, :], src[:, i, :], gbias[:, l, :], ALU.add).then_inc(S[f"xb{l}"], 1)

            for i in range(NT):
                ln_rstd(0, i)
            pool.memset(va1[:], 0.0).then_inc(S["va1_zero"], 1)
            pool.wait_ge(S["va1_zero"], 1)
            pool.memset(va1[:, :, :, DH:DH + 1], 1.0).then_inc(S["va1_zero"], 1)
            residual_bias(0, x_sb)
            pool.wait_ge(S["xb0"], NT)
            pool.memset(late[TERM_END:P, :], 0.0).then_inc(S["kpack_zero"], 1)
            pool.wait_ge(S["kpack_zero"], 1)
            for i in range(NT):
                ln_rstd(1, i)
            for i in range(NT):
                ln_rstd(4, i)
            for i in range(NT):
                pool.wait_ge(LN_RS, ln_done(4, i))
                pool.tensor_scalar(yn[:, i, :], normed[1][:, i, :], meanvar[:, 4, i, 0:1], rstd[:, 4, i:i + 1],
                                   ALU.subtract, ALU.mult).then_inc(S["yn_sb"], 1)
            pool.wait_ge(S["yn_p1"], 1)
            pool.tensor_tensor(ynr[:], yn[:], yn3[:, 0, :, :], ALU.subtract).then_inc(S["yn_r1"], 1)
            pool.wait_ge(S["yn_p2"], 1)
            pool.wait_ge(S["yn_r1"], 1)
            pool.tensor_tensor(yn3[:, 2, :, :], ynr[:], yn3[:, 1, :, :], ALU.subtract).then_inc(S["yn_p3"], 1)
            pool.wait_ge(S["score_sb"], 1)
            link(pool.tensor_copy(score3[:, :, 0, :], score[:]))
            link(pool.tensor_tensor(score_hi[:], score[:], score3[:, :, 0, :], ALU.subtract))
            link(pool.tensor_copy(score3[:, :, 1, :], score_hi[:]))
            pool.tensor_tensor(score3[:, :, 2, :], score_hi[:], score3[:, :, 1, :], ALU.subtract)\
                .then_inc(S["score3_sb"], 1)
            pool.wait_ge(S["k1_sb"], NB)
            link(pool.tensor_copy(k3[:, 0, :], k1[:]))
            link(pool.tensor_tensor(k1r[:], k1[:], k3[:, 0, :], ALU.subtract))
            link(pool.tensor_copy(k3[:, 1, :], k1r[:]))
            pool.tensor_tensor(k3[:, 2, :], k1r[:], k3[:, 1, :], ALU.subtract).then_inc(S["k3_sb"], 1)
            for i in range(NT):
                if i == 0:
                    link(pool.tensor_scalar(xg[:], normed[1][:], tanhg[:, 2:3], None, ALU.mult))
                pool.tensor_tensor(xg[:, i, :], xg[:, i, :], res[0][:, i, :], ALU.add).then_inc(S["xg_sb"], 1)
            pool.wait_ge(S["kept_sb"], 1)
            pool.wait_ge(L["b2"], 16)
            for c in range(PR0):
                pool.tensor_scalar(b2w[:, c, :], b2_sb[:, c, :], kept[:, c:c + 1], None, ALU.mult)\
                    .then_inc(S["b2w_sb"], 1)
            pool.wait_ge(S["fc1_ps"], PR0)
            pool.wait_ge(S["b2w_sb"], PR0)
            pool.memset(fc1T_sb[TERM_END:P, :, :], 0.0).then_inc(S["qpack_zero"], 1)
            pool.wait_ge(S["qpack_zero"], 1)
            for i in range(NT):
                ln_rstd(2, i)
            residual_bias(1, res[1])
            for i in range(NT):
                ln_rstd(3, i)
            pool.wait_ge(S["s1_ps"], UNITS * GH)
            pool.iota(iota_places, [[1, PLACES]], base=0, channel_multiplier=0,
                      allow_small_or_imprecise_dtypes=True).then_inc(S["iota_places_set"], 1)
            pool.memset(zT[:, PLACES:WIDE], 0.0).then_inc(S["iota_places_set"], 1)
            pool.wait_ge(S["sigma_sb"], 1)
            for i in range(NT):
                pool.tensor_scalar(zn[:, i, :], normed[3][:, i, :], sig[:, 2, i:i + 1], None, ALU.mult)\
                    .then_inc(S["zn_sb"], 1)
            pool.wait_ge(S["zn_p1"], 1)
            pool.tensor_tensor(znr[:], zn[:], zn3[:, 0, :, :], ALU.subtract).then_inc(S["zn_r1"], 1)
            pool.wait_ge(S["zn_p2"], 1)
            pool.tensor_tensor(zn3[:, 2, :, :], znr[:], zn3[:, 1, :, :], ALU.subtract).then_inc(S["zn_p3"], 1)

        @block.tensor
        def _(pe):
            def mm(o, lhsT, rhs, start=True, stop=True, **k):
                return pe.matmul(o, lhsT, rhs, start=start, stop=stop, **k)

            pe.wait_ge(L["ctx"], 16)
            pe.wait_ge(L["w0"], 16)
            for b in range(NB):
                mm(bank[:, b, :], w0_sb[:, 1, :], ctxT_sb[:, b * SK:(b + 1) * SK]).then_inc(S["k0_ps"], 1)

            def transpose(o, src, n=P):
                return pe.transpose(o, src, ident[0:n, 0:n])

            pe.wait_ge(L["const"], 16)
            for i in range(NT):
                pe.wait_ge(LN_N, 0 * NT + i + 1)
                transpose(bank[:, 4 + i, 0:P], normed[0][:, i, :]).then_inc(S["nT0_ps"], 1)
            for i in range(NT):
                pe.wait_ge(S["nT0_sb"], i + 1)
                if i >= 2:
                    pe.wait_ge(S["q0_sb"], i - 1)
                mm(bank[:, 2 + i % 2, 0:P], w0_sb[:, 0, :], normedT[0][:, i, :]).then_inc(S["q0_ps"], 1)
            pe.wait_ge(S["k0_sb"], NB)
            for i in range(NT):
                pe.wait_ge(S["q0_sb"], i + 1)
                mm(bank[:, 4 + i, :], q0T[:, i, :], k0[:, i // 2, :]).then_inc(S["sc0_ps"], 1)
            pe.wait_ge(S["bvcol_set"], 2)
            pe.wait_ge(L["rows"], 16)
            mm(bank[:, 0, 0:D], bvcol[:, 0, :], w0_sb[:, 3, :], stop=False)
            mm(bank[:, 0, 0:D], const_sb[0:1, K_ONE:K_ONE + P], rows_sb[0:1, 0, :], start=False).then_inc(S["bias0_ps"], 1)
            for c in range(NB * KC):
                mm(bank[:, 2 + c // KC, (c % KC) * P:(c % KC + 1) * P], ctxT_sb[:, c * P:(c + 1) * P],
                   w0_sb[:, 2, :]).then_inc(S["v0_ps"], 1)

            def probs0_turned(i):
                pe.wait_ge(S["probs0_sb"], i + 1)
                if i == 0:
                    pe.wait_ge(S["bias0_sb"], 1)
                if i >= 2:
                    pe.wait_ge(S["va0_sb"], KC * (i - 1))
                for c in range(KC):
                    ins = transpose(bank[:, i, c * P:(c + 1) * P], probs0[:, i, c * P:(c + 1) * P])
                ins.then_inc(S["p0T_ps"], 1)

            def weighted0(i):
                pe.wait_ge(S["p0T_sb"], i + 1)
                pe.wait_ge(S["va0_sb"], KC * (i // 2 + 1))
                for c in range(KC):
                    ins = mm(bank[:, 4 + i, 0:H * (DH + 1)], probs0T[:, i, c * P:(c + 1) * P],
                             va0[:, (i // 2) * KC + c, :, :], start=c == 0, stop=c == KC - 1)
                ins.then_inc(S["pv0_ps"], 1)

            def attention0_turned(i):
                pe.wait_ge(S["att0"], i + 1)
                transpose(bank[:, i, 0:P], att[0][:, i, :, :]).then_inc(S["attT0_ps"], 1)

            def project0(i):
                pe.wait_ge(S["attT0_sb"], i + 1)
                mm(bank[:, 4 + i, 0:D], attT[0][:, i, :], w0_sb[:, 3, :]).then_inc(S["o0_ps"], 1)

            probs0_turned(0)
            probs0_turned(1)
            weighted0(0)
            probs0_turned(2)
            weighted0(1)
            probs0_turned(3)
            weighted0(2)
            attention0_turned(0)
            attention0_turned(1)
            weighted0(3)
            project0(0)
            attention0_turned(2)
            project0(1)
            attention0_turned(3)
            project0(2)
            project0(3)
            for i in range(NT):
                pe.wait_ge(LN_N, 1 * NT + i + 1)
                transpose(bank[:, i, 0:P], normed[1][:, i, :]).then_inc(S["nT1_ps"], 1)
            pe.wait_ge(L["small"], 16)
            for i in range(NT):
                pe.wait_ge(S["nT1_sb"], i + 1)
                mm(bank[:, 4, i * E0:(i + 1) * E0], normedT[1][:, i, :], small_sb[:, C_GATE:C_GATE + E0])\
                    .then_inc(S["lg0_ps"], 1)
            pe.wait_ge(S["score_sb"], 1)
            for i in range(NT):
                ins = transpose(bank[0:E0, 5, i * P:(i + 1) * P], score[:, i, :])
            ins.then_inc(S["scT_ps"], 1)
            pe.wait_ge(S["nT1_sb"], NT)
            pe.wait_ge(L["w1"], 16)
            for b in range(NB):
                mm(bank[:, b, :], w1_sb[:, 1, :], ctxT_sb[:, b * SK:(b + 1) * SK]).then_inc(S["k1_ps"], 1)
            for c in range(NB * KC):
                mm(bank[:, 2 + c // KC, (c % KC) * P:(c % KC + 1) * P], ctxT_sb[:, c * P:(c + 1) * P],
                   w1_sb[:, 2, :]).then_inc(S["v1_ps"], 1)
            mm(bank[:, 6, 0:D], bvcol[:, 1, :], w1_sb[:, 3, :], stop=False)
            mm(bank[:, 6, 0:D], const_sb[0:1, K_ONE:K_ONE + P], rows_sb[0:1, 1, :], start=False).then_inc(S["bias1_ps"], 1)
            pe.wait_ge(S["chosenT_sb"], 1)
            pe.wait_ge(S["bias1_sb"], 1)
            for i in range(NT):
                ins = transpose(bank[:, 6, i * E0:(i + 1) * E0], chosenT[:, i * P:(i + 1) * P], E0)
            ins.then_inc(S["chosen_ps"], 1)

            def count_before(pb, mask, n):
                for i in range(NT):
                    for k in range(i):
                        mm(bank[:, pb, i * n:(i + 1) * n], ones_bf[:], mask[:, k, :], start=k == 0, stop=False)
                    ins = mm(bank[:, pb, i * n:(i + 1) * n], tri_bf[:], mask[:, i, :], start=i == 0)
                return ins

            pe.wait_ge(S["consts_bf"], 4)
            pe.wait_ge(S["chosen_sb"], 1)
            count_before(7, chosen, E0).then_inc(S["cum0_ps"], 1)
            pe.wait_ge(S["yn_p1"], 1)
            pe.wait_ge(S["yn_p2"], 1)
            pe.wait_ge(S["yn_p3"], 1)
            for i in range(NT):
                pe.wait_ge(S["sel0_sb"], i + 1)
                for part in range(3):
                    ins = mm(bank[:, 4, :], yn3[:, part, i, :], sel0[:, i, :, :],
                             start=i == 0 and part == 0, stop=i == NT - 1 and part == 2)
            ins.then_inc(S["yT_ps"], 1)
            pe.wait_ge(S["score3_sb"], 1)
            for c in range(PR0):
                for i in range(NT):
                    ins = mm(bank[:, 5, c * 3 * E0:(c + 1) * 3 * E0], sel0[:, i, 2 * c:2 * c + 2, :],
                             score3[:, i, :, :], start=i == 0, stop=i == NT - 1)
            ins.then_inc(S["kept_ps"], 1)
            pe.wait_ge(S["k1_sb"], NB)
            pe.wait_ge(S["va1_sb"], NB * KC)
            for i in range(NT):
                for c in range(PR0):
                    ins = pe.transpose(bank[:, c, 0:T // 2].bitcast(BF16)[:, i * P:(i + 1) * P],
                                       sel0[:, i, 2 * c:2 * c + 2, :], ident_bf[:])
                ins.then_inc(S["sel0T_ps"], 1)
            pe.wait_ge(S["yT_sb"], 1)
            pe.wait_ge(L["fc1"], 16)
            for c in range(PR0):
                if c == 2:
                    pe.wait_ge(S["sel0T_sb"], PR0)
                for e in (2 * c, 2 * c + 1):
                    for f in range(FC0):
                        o = (e % 2 * FC0 + f) * CAP0
                        ins = mm(bank[:, SCB[c], o:o + CAP0], fc1T_sb[:, e, f * P:(f + 1) * P],
                                 yT[:, e * CAP0:(e + 1) * CAP0])
                ins.then_inc(S["fc1_ps"], 1)
            pe.wait_ge(L["fc2"], 16)
            for c in range(PR0):
                pe.wait_ge(S["hidg_sb"], c + 1)
                if c == 3:
                    pe.wait_ge(S["kept_sb"], 1)
                for f in range(FC0):
                    for u in range(2):
                        ins = mm(bank[u * CAP0:(u + 1) * CAP0, 2 + c, 0:D], hidg[:, c, u, f, :],
                                 fc2_sb[:, 2 * c + u, f, :], start=f == 0, stop=f == FC0 - 1)
                ins.then_inc(S["fc2_ps"], 1)
            pe.wait_ge(S["moe0_sb"], PR0)
            for i in range(NT):
                for c in range(PR0):
                    ins = mm(bank[:, SCB[i], 0:D], sel0T[:, c, i * P:(i + 1) * P], moe0[:, c, :],
                             start=c == 0, stop=c == PR0 - 1)
                ins.then_inc(S["sc_ps"], 1)
            for i in range(NT):
                pe.wait_ge(LN_N, 2 * NT + i + 1)
                transpose(bank[:, 2 + i, 0:P], normed[2][:, i, :]).then_inc(S["nT2_ps"], 1)
            for i in range(NT):
                pe.wait_ge(S["nT2_sb"], i + 1)
                mm(bank[:, SCB[i], 0:P], w1_sb[:, 0, :], normedT[2][:, i, :]).then_inc(S["q1_ps"], 1)

            pe.wait_ge(S["q1_sb"], NT)
            pe.wait_ge(S["q3_sb"], 1)
            pe.wait_ge(L["selq"], 16)
            ring = [0]

            def next_ring():
                n = ring[0]
                ring[0] += 1
                before = [k for k in range(n) if RING_BANK[k] == RING_BANK[n]]
                if not before:
                    if RING_BANK[n] == PACKB[HPE - 1]:
                        pe.wait_ge(S["qpack_sb"], HPE)
                elif RING[before[-1]][0] == "max":
                    pe.wait_ge(S["mrow_sb"], RING[before[-1]][1] + 1)
                else:
                    pe.wait_ge(S["ring_free"], READ[before[-1]])
                return RING_BANK[n]

            def pack_q(h):
                if h >= GH:
                    pe.wait_ge(S["qpack_sb"], h - 1)
                for part in range(3):
                    ins = mm(bank[0:NROW, PACKB[h], :], selq_bf[:, part, h, :], q3[:, part, :],
                             start=part == 0, stop=part == 2)
                ins.then_inc(S["qp_ps"], 1)

            def raw_scores(u, j, qt):
                b, g = divmod(u, NG)
                h = g * GH + j
                t0 = b * SQ + qt * P
                r = next_ring()
                mm(bank[:, r, :], qpack[:, h, t0:t0 + P], kpack[:, h, b * SK:(b + 1) * SK])\
                    .then_inc(S["ring_full"], 1)

            def max_rows(u):
                r = next_ring()
                pe.wait_ge(S["minus_max_set"], u + 1)
                for qt in range(2):
                    ins = pe.transpose(bank[0:2 * GH, r, :].bitcast(BF16)[:, qt * P:(qt + 1) * P],
                                       minus_max[:, u % 2, qt, :, :], ident_bf[:])
                ins.then_inc(S["mrow_ps"], 1)

            def scores(u, j):
                b, g = divmod(u, NG)
                h = g * GH + j
                n = u * GH + j
                if n >= 2:
                    pe.wait_ge(S["probs1_sb"], n - 1)
                if j == 0:
                    pe.wait_ge(S["mrow_in"], 32 * (u + 1))
                for kc in range(KC):
                    s0 = b * SK + kc * P
                    ins = mm(bank[:, 2 + 2 * (n % 2) + kc // 2, (kc % 2) * SQ:(kc % 2 + 1) * SQ],
                             kpack[:, h, s0:s0 + P], qpack[:, h, b * SQ:(b + 1) * SQ])
                ins.then_inc(S["s1_ps"], 1)

            def weighted(u, kc):
                b, g = divmod(u, NG)
                if kc == 0:
                    pe.wait_ge(S["probs1_sb"], (u + 1) * GH)
                    if u >= 1:
                        pe.wait_ge(S["outT1_sb"], u)
                    else:
                        pe.wait_ge(S["qpack_sb"], HPE)
                for j in range(GH):
                    ins = mm(bank[32 * j:32 * j + 32, 6, 0:SQ], va1[:, b * KC + kc, g * GH + j, :],
                             probs1[:, (u % 2) * GH + j, kc, :], start=kc == 0, stop=kc == KC - 1)
                if kc == KC - 1:
                    ins.then_inc(S["pv1_ps"], 1)

            def out_rows(u):
                pe.wait_ge(S["outT1_sb"], u + 1)
                r = next_ring()
                for qt in range(2):
                    ins = transpose(bank[:, r, qt * P:(qt + 1) * P], outT1[:, u % 2, qt * P:(qt + 1) * P])
                ins.then_inc(S["ring_full"], 1)

            pack_q(0)
            pack_q(1)
            pe.wait_ge(S["kpack_in"], 16 * (len(TERMS) + 1))
            for s in range(UNITS + 5):
                for j in range(GH):
                    if s * GH + j < HPE:
                        pe.wait_ge(S["qpack_sb"], s * GH + j + 1)
                    elif s * GH + j == HPE:
                        pe.wait_ge(S["qpack_in"], 16 * len(TERMS))
                    if s < UNITS:
                        raw_scores(s, j, 0)
                    if 0 <= s - 2 < UNITS:
                        scores(s - 2, j)
                    if s < UNITS:
                        raw_scores(s, j, 1)
                    if j == max_slot(s) and 0 <= s - 1 < UNITS:
                        max_rows(s - 1)
                    if j == 2 and 0 <= s - 4 < UNITS:
                        out_rows(s - 4)
                    if s * GH + j + 2 < HPE:
                        pack_q(s * GH + j + 2)
                    if 0 <= s - 3 < UNITS:
                        for kc in ((), (0, 1), (2,), (3,))[j]:
                            weighted(s - 3, kc)
                    if (s, j) == FIRST_ATT:
                        pe.wait_ge(S["ring_free"], READ[SPARE_FROM])
                        for i in range(2):
                            transpose(bank[:, 1, i * P:(i + 1) * P], att[1][:, i, :, :]).then_inc(S["attT1_ps"], 1)
                    if (s, j) == FIRST_OUT:
                        pe.wait_ge(S["attT1_sb"], 2)
                        for i in range(2):
                            mm(bank[:, 1, (2 + i) * P:(3 + i) * P], attT[1][:, i, :], w1_sb[:, 3, :]).then_inc(S["o1_ps"], 1)
                    if (s, j) == FIRST_NORM:
                        for i in range(2):
                            pe.wait_ge(LN_N, 3 * NT + i + 1)
                            transpose(bank[:, 1, i * P:(i + 1) * P], normed[3][:, i, :]).then_inc(S["nT3_ps"], 1)
            pe.wait_ge(S["ring_free"], READ[-1])
            pe.wait_ge(S["nT3_sb"], 2)
            for i in (2, 3):
                transpose(bank[:, TAILT[i - 2], 0:P], att[1][:, i, :, :]).then_inc(S["attT1_ps"], 1)
            for i in (2, 3):
                pe.wait_ge(S["attT1_sb"], i + 1)
                mm(bank[:, TAILO[i - 2], 0:D], attT[1][:, i, :], w1_sb[:, 3, :]).then_inc(S["o1_ps"], 1)

            def shared_gate_up(f, k, tokens):
                return mm(bank[:, SHB[f] + k, tokens], shGU_sb[:, k, f * P:(f + 1) * P],
                          normedT[3][:].rearrange("p i t -> p (i t)")[:, tokens])

            pe.wait_ge(L["sh"], 32)
            pe.wait_ge(S["probs1_sb"], UNITS * GH)
            for f in range(2):
                for k in range(2):
                    shared_gate_up(f, k, slice(0, SQ))
            for i in (2, 3):
                pe.wait_ge(LN_N, 3 * NT + i + 1)
                transpose(bank[:, TAILT[i - 2], 0:P], normed[3][:, i, :]).then_inc(S["nT3_ps"], 1)
            for i in range(NT):
                pe.wait_ge(S["nT3_sb"], i + 1)
                mm(bank[:, 6, i * E1:(i + 1) * E1], normedT[3][:, i, :], small_sb[:, C_ROUT:C_ROUT + E1])\
                    .then_inc(S["lg1_ps"], 1)
            pe.wait_ge(L["sh"], 32)
            first = []

            def load_starts(n):
                pe.wait_ge(S["starts_set"], 1)
                for e in range(len(first), min(len(first) + n, E1)):
                    first.append(pe.value_load(starts_int[0:1, e:e + 1], min_val=0, max_val=PLACES))

            for f in range(SFC):
                if f == 3:
                    pe.wait_ge(S["shh_sb"], 1)
                for k in range(2):
                    ins = shared_gate_up(f, k, slice(SQ if f < 2 else 0, T))
                    if (f, k) == (0, 0):
                        pe.wait_ge(S["oh_sb"], 1)
                        for i in range(NT):
                            cnt = mm(bank[:, 6, NT * E1:(NT + 1) * E1], ones_bf[:], oh[:, i, :],
                                     start=i == 0, stop=i == NT - 1)
                        cnt.then_inc(S["count_ps"], 1)
                        count_before(7, oh, E1).then_inc(S["cum1_ps"], 1)
                ins.then_inc(S["shg_ps"], 1)
                if f:
                    load_starts((1, 2, 4)[f - 1])

            def no_window(at_bank):
                for w, n in ((0, T), (1, WIDE - T)):
                    mm(bank[:, at_bank + w, 0:n], zeros_bf[:], selq_bf[:].rearrange("p k h r -> p (k h r)")[:, 0:n])

            pe.wait_ge(S["shh_sb"], 2)
            for i in range(NT):
                pe.wait_ge(S["sel1_sb"], i + 1)
                for c in range(PC1):
                    ins = pe.transpose(bank[:, SELB[c], :].bitcast(BF16)[:, (c % 2) * T + i * P:(c % 2) * T + (i + 1) * P],
                                       sel1[:, i, c * P:(c + 1) * P], ident_bf[:])
                ins.then_inc(S["sel1T_ps"], 1)
            pe.wait_ge(S["shh_sb"], SFC)
            no_window(0)
            no_window(2)
            pe.wait_ge(S["zn_p1"], 1)
            pe.wait_ge(S["zn_p2"], 1)
            pe.wait_ge(S["zn_p3"], 1)
            for w, n in ((0, T), (1, PLACES - T)):
                if w:
                    load_starts(5)
                    pe.wait_ge(S["sel1T_sb"], 1)
                for i in range(NT):
                    for part in range(3):
                        ins = mm(bank[:, 6 + w, 0:n], zn3[:, part, i, :], sel1[:, i, w * T:w * T + n],
                                 start=i == 0 and part == 0, stop=i == NT - 1 and part == 2)
                ins.then_inc(S["zT_ps"], 1)

            def shared_down(i):
                for f in range(SFC):
                    ins = mm(bank[:, 6, i * P:(i + 1) * P], shh[:, f, i * P:(i + 1) * P], shD_sb[:, f, :],
                             start=f == 0, stop=f == SFC - 1)
                return ins

            load_starts(1)
            pe.wait_ge(L["gu"], 16)
            pe.wait_ge(S["zT_sb"], 2)
            pe.wait_ge(S["iota_places_set"], 2)
            gate_ps, up_ps, down_ps = (bank[:, b:b + 2, :].rearrange("p b n -> p (b n)") for b in (0, 2, 4))

            def gate_up(e, at):
                for k, o in ((0, gate_ps), (1, up_ps)):
                    ins = mm(o[:, bass.ds(at, WIN)], gateup_sb[:, e, k * F1:(k + 1) * F1], zT[:, bass.ds(at, WIN)])
                return ins

            def project(e, at):
                return mm(down_ps[:, bass.ds(at, WIN)], down_sb[:, e, :], hid1[:, bass.ds(at, WIN)])

            def general(one):
                for e in range(E1):
                    for k in range(MORE):
                        n = e * MORE + k
                        one(e, pe.value_load(general_int[0:1, n:n + 1], min_val=0, max_val=PLACES))

            for e in range(E1 - 1):
                gate_up(e, first[e])
                if e % 4 == 3:
                    load_starts(1)
            pe.wait_ge(S["general_set"], 1)
            large = pe.value_load(most_int[0:1, 0:1], min_val=0, max_val=T)
            with pe.If(large > WIN):
                general(gate_up)
            gate_up(E1 - 1, first[E1 - 1]).then_inc(S["gu_ps"], 1)
            pe.wait_ge(L["sh"], 32)
            pe.wait_ge(S["sel1T_sb"], PC1)
            no_window(4)
            shared_down(0)
            shared_down(1)
            pe.wait_ge(L["down"], 16)
            pe.wait_ge(S["hid1_sb"], 1)
            for e in range(E1 - 1):
                project(e, first[e])
            with pe.If(large > WIN):
                general(project)
            project(E1 - 1, first[E1 - 1]).then_inc(S["down_ps"], 1)
            shared_down(2)
            pe.wait_ge(S["moe1T_sb"], 1)
            for c in range(PC1):
                ins = transpose(bank[:, 2 + c // KC, (c % KC) * P:(c % KC + 1) * P], moe1T[:, c * P:(c + 1) * P])
            ins.then_inc(S["moe1_ps"], 1)
            shared_down(3).then_inc(S["shd_ps"], 1)
            pe.wait_ge(S["moe1_sb"], 1)
            for i in range(NT):
                for c in range(PC1):
                    ins = mm(bank[:, FINB[i], 0:D], sel1T[:, c, i * P:(i + 1) * P], moe1[:, c, :],
                             start=c == 0, stop=c == PC1 - 1)
                ins.then_inc(S["final_ps"], 1)

        @block.scalar
        def _(act):
            act.wait_ge(L["gates"], 16)
            act.activation(tanhg[:], gates_sb[:], ACT.Tanh).then_inc(S["tanh_done"], 1)

            def copies(ps, sbs, dst, src):
                for i in range(NT):
                    act.wait_ge(S[ps], i + 1)
                    act.copy(dst(i), src(i)).then_inc(S[sbs], 1)

            act.wait_ge(L["small"], 16)
            copies("nT0_ps", "nT0_sb", lambda i: normedT[0][:, i, :], lambda i: bank[:, 4 + i, 0:P])
            for i in range(NT):
                act.wait_ge(S["q0_ps"], i + 1)
                act.activation(q0T[:, i, :], bank[:, 2 + i % 2, 0:P], ACT.Identity, bias=vec(V_BQ)).then_inc(S["q0_sb"], 1)
            for i in range(NT):
                act.wait_ge(S["shift0"], i + 1)
                act.activation(probs0[:, i, :], shifted[:, i, :], ACT.Exp, scale=SCALE).then_inc(S["probs0_sb"], 1)
                if i == 0:
                    act.wait_ge(S["bias0_ps"], 1)
                    act.copy(bias[:, 0, :], bank[:, 0, 0:D]).then_inc(S["bias0_sb"], 1)
                else:
                    act.wait_ge(S["p0T_ps"], i)
                    act.copy(probs0T[:, i - 1, :], bank[:, i - 1, :]).then_inc(S["p0T_sb"], 1)
            act.wait_ge(S["p0T_ps"], NT)
            act.copy(probs0T[:, NT - 1, :], bank[:, NT - 1, :]).then_inc(S["p0T_sb"], 1)
            copies("attT0_ps", "attT0_sb", lambda i: attT[0][:, i, :], lambda i: bank[:, i, 0:P])
            copies("nT1_ps", "nT1_sb", lambda i: normedT[1][:, i, :], lambda i: bank[:, i, 0:P])
            act.wait_ge(S["sh0"], 1)
            act.activation(ex[:], ex[:], ACT.Exp).then_inc(S["ex0"], 1)
            for b in range(NB):
                act.wait_ge(S["k1_ps"], b + 1)
                act.activation(k1[:, b * SK:(b + 1) * SK], bank[:, b, :], ACT.Identity, bias=vec(V_BK1))\
                    .then_inc(S["k1_sb"], 1)
            act.wait_ge(S["va1_zero"], 2)
            for c in range(NB * KC):
                act.wait_ge(S["v1_ps"], KC * (c // KC + 1))
                act.copy(va1[:, c, :, 0:DH], bank[:, 2 + c // KC, (c % KC) * P:(c % KC + 1) * P]
                         .rearrange("p (h d) -> p h d", d=DH)).then_inc(S["va1_sb"], 1)
            act.wait_ge(S["bias1_ps"], 1)
            act.copy(bias[:, 1, :], bank[:, 6, 0:D]).then_inc(S["bias1_sb"], 1)
            act.wait_ge(S["yn_sb"], NT)
            act.copy(yn3[:, 0, :, :], yn[:]).then_inc(S["yn_p1"], 1)
            act.wait_ge(S["yn_r1"], 1)
            act.copy(yn3[:, 1, :, :], ynr[:]).then_inc(S["yn_p2"], 1)
            act.wait_ge(S["sel0T_ps"], NT)
            for c in range(PR0):
                act.copy(sel0T[:, c, :], bank[:, c, 0:T // 2].bitcast(BF16)).then_inc(S["sel0T_sb"], 1)
            for c in range(PR0):
                act.wait_ge(S["hid_sb"], c + 1)
                act.activation(hidg[:, c, :, :, :], hid[:, c, :, :, :], ACT.Gelu_apprx_tanh).then_inc(S["hidg_sb"], 1)
            copies("nT2_ps", "nT2_sb", lambda i: normedT[2][:, i, :], lambda i: bank[:, 2 + i, 0:P])
            for i in range(NT):
                act.wait_ge(S["q1_ps"], i + 1)
                act.activation(q1[:, i * P:(i + 1) * P], bank[:, SCB[i], 0:P], ACT.Identity, bias=vec(V_BQ1))\
                    .then_inc(S["q1_sb"], 1)
            act.wait_ge(S["qpack_zero"], 1)

            def pack(h):
                act.wait_ge(S["qp_ps"], h + 1)
                act.copy(qpack[0:NROW, h, :], bank[0:NROW, PACKB[h], :]).then_inc(S["qpack_sb"], 1)

            act.activation(sig[:, 0, :], gates_sb[:], ACT.Exp)
            pack(0)
            pack(1)
            for s in range(UNITS + 5):
                for j in range(GH):
                    if j == 0 and 0 <= s - 4 < UNITS:
                        u = s - 4
                        act.wait_ge(S["pv1_ps"], u + 1)
                        if u >= 2:
                            act.wait_ge(S["ring_full"], OUT_ITEM[u - 2])
                        act.copy(outT1[:, u % 2, :], bank[:, 6, 0:SQ]).then_inc(S["outT1_sb"], 1)
                    if 0 <= s - 2 < UNITS:
                        n = (s - 2) * GH + j
                        act.wait_ge(S["s1_ps"], n + 1)
                        if s - 2 >= 2:
                            act.wait_ge(S["pv1_ps"], s - 3)
                        act.activation(probs1[:, n % (2 * GH), :, :],
                                       bank[:, 2 + 2 * (n % 2):4 + 2 * (n % 2), :], ACT.Exp, scale=SCALE)\
                            .then_inc(S["probs1_sb"], 1)
                    if j == max_slot(s) and 0 <= s - 1 < UNITS:
                        u = s - 1
                        act.wait_ge(S["mrow_ps"], u + 1)
                        if u >= 2:
                            act.wait_ge(S["mrow_in"], 32 * (u - 1))
                        r = RING_BANK[RING.index(("max", u))]
                        act.copy(mrow[:, u % 2, :], bank[0:2 * GH, r, :].bitcast(BF16)[:, 0:SQ])\
                            .then_inc(S["mrow_sb"], 1)
                    if s * GH + j + 2 < HPE:
                        pack(s * GH + j + 2)
                    if (s, j) == FIRST_ATT:
                        act.wait_ge(S["attT1_ps"], 2)
                        act.copy(attT[1][:, 0:2, :].rearrange("p i t -> p (i t)"), bank[:, 1, 0:SQ])\
                            .then_inc(S["attT1_sb"], 2)
                    if (s, j) == FIRST_NORM:
                        act.wait_ge(S["nT3_ps"], 2)
                        act.copy(normedT[3][:, 0:2, :].rearrange("p i t -> p (i t)"), bank[:, 1, 0:SQ])\
                            .then_inc(S["nT3_sb"], 2)
            for i in (2, 3):
                act.wait_ge(S["attT1_ps"], i + 1)
                act.copy(attT[1][:, i, :], bank[:, TAILT[i - 2], 0:P]).then_inc(S["attT1_sb"], 1)
            for i in (2, 3):
                act.wait_ge(S["nT3_ps"], i + 1)
                act.copy(normedT[3][:, i, :], bank[:, TAILT[i - 2], 0:P]).then_inc(S["nT3_sb"], 1)
            act.wait_ge(S["mx16_sb"], 1)
            act.activation(sig[:, 0, :], mx16[:], ACT.Exp, scale=-1.0).then_inc(S["sig_e"], 1)
            for f in range(SFC):
                act.wait_ge(S["shg_ps"], f + 1)
                if f >= 2:
                    act.wait_ge(S["shh_sb"], f - 1)
                act.activation(sgate[:, f % 2, :], bank[:, SHB[f], :], ACT.Silu).then_inc(S["shg_sb"], 1)
                if f == 1:
                    act.wait_ge(S["zn_sb"], NT)
                    act.copy(zn3[:, 0, :, :], zn[:]).then_inc(S["zn_p1"], 1)
                if f == 2:
                    act.wait_ge(S["zn_r1"], 1)
                    act.copy(zn3[:, 1, :, :], znr[:]).then_inc(S["zn_p2"], 1)
            act.wait_ge(S["sel1T_ps"], NT)
            for c in reversed(range(PC1)):
                act.copy(sel1T[:, c, :], bank[:, SELB[c], :].bitcast(BF16)[:, (c % 2) * T:(c % 2 + 1) * T])\
                    .then_inc(S["sel1T_sb"], 1)
            for w, n in ((0, T), (1, PLACES - T)):
                act.wait_ge(S["zT_ps"], w + 1)
                act.copy(zT[:, w * T:w * T + n], bank[:, 6 + w, 0:n]).then_inc(S["zT_sb"], 1)
            act.wait_ge(S["gu_ps"], 1)
            act.activation(gate1, bank[:, 0:2, :].rearrange("p b n -> p (b n)")[:, 0:WIDE], ACT.Silu)\
                .then_inc(S["gate1_sb"], 1)
            act.wait_ge(S["down_ps"], 1)
            act.copy(moe1T, bank[:, 4:6, :].rearrange("p b n -> p (b n)")[:, 0:PLACES]).then_inc(S["moe1T_sb"], 1)
            act.wait_ge(S["moe1_ps"], 1)
            act.copy(moe1, bank[:, 2:4, :].rearrange("p b n -> p (b n)")[:, 0:PLACES]).then_inc(S["moe1_sb"], 1)

        @block.vector
        def _(dve):
            chain = [0]

            def link(ins):
                chain[0] += 1
                ins.then_inc(S["vchain"], 1)
                dve.wait_ge(S["vchain"], chain[0])

            def ln_stats(k, i, src):
                link(dve.bn_stats(stats[:, k, i, :], src))
                dve.bn_aggr(meanvar[:, k, i, :], stats[:, k, i, :]).then_inc(LN_MV, 1)

            def ln_apply(k, i):
                dve.wait_ge(LN_RS, ln_done(k, i))
                dve.tensor_scalar(normed[k][:, i, :], ln_in[k][:, i, :], meanvar[:, k, i, 0:1], rstd[:, k, i:i + 1],
                                  ALU.subtract, ALU.mult).then_inc(LN_N, 1)

            dve.wait_ge(L["x"], 16)
            for i in range(NT):
                ln_stats(0, i, x_sb[:, i, :])
            dve.wait_ge(L["small"], 16)
            for l, v in ((0, V_BV), (1, V_BV1)):
                dve.tensor_copy(bvcol[:, l, :], vec(v).to_broadcast([P, P])).then_inc(S["bvcol_set"], 1)
            for i in range(NT):
                ln_apply(0, i)
            dve.wait_ge(L["const"], 16)
            he = const_sb[:, K_HE:K_HE + H]
            hs = const_sb[:, K_HS:K_HS + H]
            for c in range(NB * KC):
                dve.tensor_copy(va0[:, c, :, DH:DH + 1], hs.unsqueeze(2))
            for b in range(NB):
                dve.wait_ge(S["k0_ps"], b + 1)
                dve.scalar_tensor_tensor(
                    out=k0[:, b, :].rearrange("p (j h) -> p j h", h=H),
                    in0=bank[:, b, :].rearrange("p (j h) -> p j h", h=H), scalar=vec(V_BK),
                    in1=he.unsqueeze(1).to_broadcast([P, SK // H, H]), op0=ALU.add, op1=ALU.mult)\
                    .then_inc(S["k0_sb"], 1)

            def masked_v(b):
                dve.wait_ge(S["v0_ps"], (b + 1) * KC)
                for c in range(b * KC, (b + 1) * KC):
                    dve.tensor_tensor(va0[:, c, :, 0:DH],
                                      bank[:, 2 + b, (c % KC) * P:(c % KC + 1) * P].rearrange("p (h d) -> p h d", d=DH),
                                      hs.unsqueeze(2).to_broadcast([P, H, DH]), ALU.mult).then_inc(S["va0_sb"], 1)

            for i in range(NT):
                dve.wait_ge(S["sc0_ps"], i + 1)
                s_v = bank[:, 4 + i, :].rearrange("p (j h) -> p j h", h=H)
                link(dve.tensor_reduce(mx0[:, i, :], bank[:, 4 + i, :].rearrange("p (j h) -> p h j", h=H), AX_X, ALU.max))
                dve.tensor_tensor(shifted[:, i, :].rearrange("p (j h) -> p j h", h=H), s_v,
                                  mx0[:, i, :].unsqueeze(1).to_broadcast([P, SK // H, H]), ALU.subtract)\
                    .then_inc(S["shift0"], 1)
                if i >= 2:
                    masked_v(i - 2)
            dve.tensor_copy(tri_bf[:], const_sb[:, K_TRI:K_TRI + P]).then_inc(S["consts_bf"], 1)
            dve.tensor_copy(ones_bf[:], const_sb[:, K_ONE:K_ONE + P]).then_inc(S["consts_bf"], 1)
            dve.tensor_copy(ident_bf[:], ident).then_inc(S["consts_bf"], 1)
            dve.tensor_copy(iota_bf[:], const_sb[:, K_IOTA:K_IOTA + CAP0]).then_inc(S["consts_bf"], 1)
            for i in range(NT):
                dve.wait_ge(S["pv0_ps"], i + 1)
                pv = bank[:, 4 + i, 0:H * (DH + 1)].rearrange("p (h d) -> p h d", d=DH + 1)
                link(dve.reciprocal(rden0[:, i, :].unsqueeze(2), pv[:, :, DH:DH + 1]))
                dve.tensor_tensor(att[0][:, i, :, :], pv[:, :, 0:DH],
                                  rden0[:, i, :].unsqueeze(2).to_broadcast([P, H, DH]), ALU.mult).then_inc(S["att0"], 1)
            for i in range(NT):
                dve.wait_ge(S["o0_ps"], i + 1)
                dve.wait_ge(S["xb0"], i + 1)
                dve.scalar_tensor_tensor(out=res[0][:, i, :], in0=bank[:, 4 + i, 0:D], scalar=tanhg[:, 0:1],
                                         in1=xb_sb[:, i, :], op0=ALU.mult, op1=ALU.add).then_inc(RES, 1)
                dve.wait_ge(RES, 0 * NT + i + 1)
                ln_stats(1, i, res[0][:, i, :])
            for i in range(NT):
                ln_apply(1, i)
            for i in range(NT):
                dve.wait_ge(LN_N, 1 * NT + i + 1)
                ln_stats(4, i, normed[1][:, i, :])
            dve.wait_ge(S["lg0_ps"], NT)
            lg = bank[:, 4, 0:NT * E0].rearrange("p (i e) -> p i e", e=E0)
            link(dve.tensor_reduce(mxe[:], lg, AX_X, ALU.max))
            dve.tensor_tensor(ex[:], lg, mxe[:].unsqueeze(2).to_broadcast([P, NT, E0]), ALU.subtract).then_inc(S["sh0"], 1)
            dve.wait_ge(S["ex0"], 1)
            link(dve.tensor_reduce(sme[:], ex[:], AX_X, ALU.add))
            link(dve.reciprocal(sme[:], sme[:]))
            dve.tensor_tensor(score[:], ex[:], sme[:].unsqueeze(2).to_broadcast([P, NT, E0]), ALU.mult)\
                .then_inc(S["score_sb"], 1)
            dve.wait_ge(S["scT_ps"], 1)
            link(dve.tensor_copy(scoreT, bank[0:E0, 5, :]))
            src = scoreT
            for r in range(CAP0 // 8):
                link(dve.max(top8[:, r, :], src))
                link(dve.match_replace(work[:, r % 2, :], top8[:, r, :], src, -1.0))
                src = work[:, r % 2, :]
            dve.tensor_scalar(chosenT[:], src, 0.0, None, ALU.is_lt).then_inc(S["chosenT_sb"], 1)
            dve.wait_ge(S["chosen_ps"], 1)
            dve.tensor_copy(chosen[:], bank[:, 6, 0:NT * E0].rearrange("p (i e) -> p i e", e=E0))\
                .then_inc(S["chosen_sb"], 1)
            dve.wait_ge(S["chosen_sb"], 1)
            dve.wait_ge(S["cum0_ps"], 1)
            link(dve.scalar_tensor_tensor(out=slot0[:], in0=bank[:, 7, 0:NT * E0].rearrange("p (i e) -> p i e", e=E0),
                                          scalar=1.0, in1=chosen[:], op0=ALU.add, op1=ALU.mult))
            for i in range(NT):
                dve.tensor_tensor(sel0[:, i, :, :], iota_bf[:].unsqueeze(1).to_broadcast([P, E0, CAP0]),
                                  slot0[:, i, :].unsqueeze(2).to_broadcast([P, E0, CAP0]), ALU.is_equal)\
                    .then_inc(S["sel0_sb"], 1)
            dve.wait_ge(S["yT_ps"], 1)
            dve.tensor_scalar(yT[:], bank[:, 4, :], vec(V_LNW), vec(V_LNB), ALU.mult, ALU.add).then_inc(S["yT_sb"], 1)
            dve.wait_ge(S["kept_ps"], 1)
            link(dve.tensor_tensor(keptp[:], bank[:, 5, 0:PR0 * 3 * E0].rearrange("p (c k) -> p c k", k=3 * E0),
                                   const_sb[:, K_WSEL:K_WSEL + PR0 * 3 * E0].rearrange("p (c k) -> p c k", k=3 * E0),
                                   ALU.mult))
            dve.tensor_reduce(kept[:], keptp[:], AX_X, ALU.add).then_inc(S["kept_sb"], 1)
            for c in range(PR0):
                dve.wait_ge(S["fc1_ps"], c + 1)
                dve.tensor_tensor(
                    hid[:, c, :, :, :].rearrange("p u f s -> p (u f) s"),
                    bank[:, SCB[c], :].rearrange("p (k s) -> p k s", s=CAP0),
                    small_sb[:, C_B1 + 2 * FC0 * c:C_B1 + 2 * FC0 * (c + 1)].unsqueeze(2)
                    .to_broadcast([P, 2 * FC0, CAP0]), ALU.add).then_inc(S["hid_sb"], 1)
            for c in range(PR0):
                dve.wait_ge(S["fc2_ps"], c + 1)
                dve.wait_ge(S["b2w_sb"], c + 1)
                dve.scalar_tensor_tensor(out=moe0[:, c, :], in0=bank[:, 2 + c, 0:D], scalar=kept[:, c:c + 1],
                                         in1=b2w[:, c, :], op0=ALU.mult, op1=ALU.add).then_inc(S["moe0_sb"], 1)
            for i in range(NT):
                dve.wait_ge(S["sc_ps"], i + 1)
                dve.wait_ge(S["xg_sb"], i + 1)
                dve.scalar_tensor_tensor(out=res[1][:, i, :], in0=bank[:, SCB[i], 0:D], scalar=tanhg[:, 2:3],
                                         in1=xg[:, i, :], op0=ALU.mult, op1=ALU.add).then_inc(RES, 1)
                dve.wait_ge(RES, 1 * NT + i + 1)
                ln_stats(2, i, res[1][:, i, :])
            for i in range(NT):
                ln_apply(2, i)
            dve.wait_ge(S["q1_sb"], NT)
            link(dve.tensor_copy(q3[:, 0, :], q1[:]))
            link(dve.tensor_tensor(q1r[:], q1[:], q3[:, 0, :], ALU.subtract))
            link(dve.tensor_copy(q3[:, 1, :], q1r[:]))
            dve.tensor_tensor(q3[:, 2, :], q1r[:], q3[:, 1, :], ALU.subtract).then_inc(S["q3_sb"], 1)

            def residual3(i):
                dve.wait_ge(S["o1_ps"], max(i + 1, 2))
                dve.wait_ge(S["xb1"], i + 1)
                o = bank[:, 1, (2 + i) * P:(3 + i) * P] if i < 2 else bank[:, TAILO[i - 2], 0:D]
                dve.scalar_tensor_tensor(out=res[2][:, i, :], in0=o, scalar=tanhg[:, 1:2],
                                         in1=xb_sb[:, i, :], op0=ALU.mult, op1=ALU.add).then_inc(RES, 1)
                dve.wait_ge(RES, 2 * NT + i + 1)
                ln_stats(3, i, res[2][:, i, :])

            high_at = {}

            def unit_max(u):
                b, g = divmod(u, NG)
                return mx1[:, b * 2:b * 2 + 2, g * GH:(g + 1) * GH]

            def max_high(u):
                dve.wait_ge(S["ring_free"], MAXED[u])
                if u >= 2:
                    dve.wait_ge(S["mrow_ps"], u - 1)
                dve.tensor_scalar(minus_max[:, u % 2, :, 0, :], unit_max(u), -1.0, None, ALU.mult).then_inc(S["vchain"], 1)
                chain[0] += 1
                high_at[u] = chain[0]

            def max_low(u):
                dve.wait_ge(S["vchain"], high_at[u])
                dve.scalar_tensor_tensor(out=minus_max[:, u % 2, :, 1, :], in0=unit_max(u), scalar=-1.0,
                                         in1=minus_max[:, u % 2, :, 0, :], op0=ALU.mult, op1=ALU.subtract)\
                    .then_inc(S["minus_max_set"], 1)

            for n, item in enumerate(RING):
                if item[0] == "max":
                    continue
                dve.wait_ge(S["ring_full"], READ[n])
                r = RING_BANK[n]
                if item[0] == "score":
                    _, u, j, qt = item
                    b, g = divmod(u, NG)
                    dve.tensor_reduce(mx1[:, b * 2 + qt, g * GH + j:g * GH + j + 1], bank[:, r, :], AX_X, ALU.max)\
                        .then_inc(S["ring_free"], 1)
                    if j == 0 and u >= 1:
                        (max_low if qt else max_high)(u - 1)
                    if (u, j, qt) == (UNITS - 1, GH - 1, 1):
                        max_high(u)
                        max_low(u)
                else:
                    u = item[1]
                    b, g = divmod(u, NG)
                    o = bank[:, r, 0:2 * P].rearrange("p (t h d) -> p t h d", t=2, d=32)
                    rd = rden1[:, b * 2:b * 2 + 2, g * GH:(g + 1) * GH]
                    link(dve.reciprocal(rd.unsqueeze(3), o[:, :, :, DH:DH + 1]))
                    dve.tensor_tensor(att[1][:, b * 2:b * 2 + 2, g * GH:(g + 1) * GH, :], o[:, :, :, 0:DH],
                                      rd.unsqueeze(3).to_broadcast([P, 2, GH, DH]), ALU.mult)\
                        .then_inc(S["ring_free"], 1)
                    if u == NG:
                        for i in range(2):
                            residual3(i)
                    if u == NG + 1:
                        for i in range(2):
                            ln_apply(3, i)
            for i in (2, 3):
                residual3(i)
            for i in (2, 3):
                ln_apply(3, i)
            dve.wait_ge(S["lg1_ps"], NT)
            lg1 = bank[:, 6, 0:NT * E1].rearrange("p (i e) -> p i e", e=E1)
            rank = const_sb[:, K_RANK:K_RANK + E1].unsqueeze(1).to_broadcast([P, NT, E1])
            dve.tensor_reduce(mx16[:], lg1, AX_X, ALU.max).then_inc(S["mx16_sb"], 1)
            dve.wait_ge(S["mx16_sb"], 1)
            link(dve.tensor_tensor(eq16[:], lg1, mx16[:].unsqueeze(2).to_broadcast([P, NT, E1]), ALU.is_equal))
            link(dve.tensor_tensor(eq16[:], eq16[:], rank, ALU.mult))
            link(dve.tensor_reduce(kmax[:], eq16[:], AX_X, ALU.max))
            dve.tensor_tensor(oh[:], eq16[:], kmax[:].unsqueeze(2).to_broadcast([P, NT, E1]), ALU.is_equal)\
                .then_inc(S["oh_sb"], 1)
            dve.wait_ge(S["sig_e"], 1)
            link(dve.tensor_scalar(sig[:, 1, :], sig[:, 0, :], 1.0, None, ALU.add))
            dve.reciprocal(sig[:, 2, :], sig[:, 1, :]).then_inc(S["sigma_sb"], 1)

            def shared_hidden(f):
                dve.wait_ge(S["shg_sb"], f + 1)
                dve.tensor_tensor(shh[:, f, :], bank[:, SHB[f] + 1, :], sgate[:, f % 2, :], ALU.mult)\
                    .then_inc(S["shh_sb"], 1)

            dve.wait_ge(S["count_ps"], 1)
            link(dve.tensor_copy(count[:], bank[:, 6, NT * E1:(NT + 1) * E1]))
            link(dve.tensor_tensor_scan(upto[:], const_sb[:, K_ONE:K_ONE + E1], count[:], 0.0, ALU.mult, ALU.add))
            link(dve.tensor_tensor(start[:], upto[:], count[:], ALU.subtract))
            link(dve.tensor_scalar(start_moved[:], start[:], float(LAST), float(WIN), ALU.is_gt, ALU.mult))
            link(dve.tensor_tensor(start[:], start[:], start_moved[:], ALU.add))
            dve.tensor_copy(starts_int[:], start[0:1, :]).then_inc(S["starts_set"], 1)
            dve.wait_ge(S["cum1_ps"], 1)
            link(dve.tensor_tensor(placed[:], bank[:, 7, 0:NT * E1].rearrange("p (i e) -> p i e", e=E1),
                                   start[:].unsqueeze(1).to_broadcast([P, NT, E1]), ALU.add))
            link(dve.tensor_tensor(placed[:], placed[:], oh[:], ALU.mult))
            link(dve.tensor_reduce(place[:], placed[:], AX_X, ALU.add))
            shared_hidden(0)
            dve.wait_ge(S["iota_places_set"], 1)
            for i in range(NT):
                dve.tensor_scalar(sel1[:, i, :], iota_places, place[:, i:i + 1], None, ALU.is_equal)\
                    .then_inc(S["sel1_sb"], 1)
            shared_hidden(1)
            shared_hidden(2)
            shared_hidden(3)
            link(dve.tensor_tensor(last_start[:], start[:], count[:], ALU.add))
            link(dve.tensor_scalar(last_start[:], last_start[:], float(-WIN), None, ALU.add))
            for k in range(MORE):
                link(dve.scalar_tensor_tensor(out=clipped[:], in0=start[0:1, :], scalar=float(k * WIN),
                                              in1=last_start[0:1, :], op0=ALU.add, op1=ALU.min))
                link(dve.tensor_tensor(general_int[0:1, k:E1 * MORE:MORE], clipped[:], start[0:1, :], ALU.max))
            link(dve.tensor_reduce(most[:], count[0:1, :], AX_X, ALU.max))
            dve.tensor_copy(most_int[:], most[:]).then_inc(S["general_set"], 1)
            dve.wait_ge(S["gate1_sb"], 1)
            dve.tensor_tensor(hid1, bank[:, 2:4, :].rearrange("p b n -> p (b n)")[:, 0:WIDE], gate1, ALU.mult)\
                .then_inc(S["hid1_sb"], 1)
            dve.wait_ge(S["shd_ps"], 1)
            for i in range(NT):
                dve.scalar_tensor_tensor(out=xs[:, i, :], in0=bank[:, 6, i * P:(i + 1) * P], scalar=tanhg[:, 3:4],
                                         in1=res[2][:, i, :], op0=ALU.mult, op1=ALU.add).then_inc(S["xs_sb"], 1)
            for i in range(NT):
                dve.wait_ge(S["final_ps"], i + 1)
                dve.wait_ge(S["xs_sb"], i + 1)
                dve.scalar_tensor_tensor(out=res[3][:, i, :], in0=bank[:, FINB[i], 0:D], scalar=tanhg[:, 3:4],
                                         in1=xs[:, i, :], op0=ALU.mult, op1=ALU.add).then_inc(S["res3"], 1)


def max_slot(s):
    return 1 if s < UNITS else 0


def ring_items():
    items = []
    for s in range(UNITS + 5):
        for j in range(GH):
            if s < UNITS:
                items += [("score", s, j, 0), ("score", s, j, 1)]
            if j == max_slot(s) and 0 <= s - 1 < UNITS:
                items.append(("max", s - 1))
            if j == 2 and 0 <= s - 4 < UNITS:
                items.append(("out", s - 4))
    return items


RING = ring_items()
PACKING = RING.index(("score", (HPE - 2) // GH, (HPE - 2) % GH, 0))
RING_BANK = [n % 2 if n < PACKING else (7, 0, 1)[(n - PACKING) % 3] for n in range(len(RING))]
LAST_SCORE = RING.index(("score", UNITS - 1, GH - 1, 1))
SPARE_FROM = max(n for n in range(LAST_SCORE + 1) if RING_BANK[n] == 1)
RING_BANK[LAST_SCORE + 1:] = [(7, 0)[n % 2] for n in range(len(RING) - LAST_SCORE - 1)]
FIRST_ATT, FIRST_OUT, FIRST_NORM = (UNITS, 1), (UNITS, 3), (UNITS + 1, 3)
READ = [sum(it[0] != "max" for it in RING[:n + 1]) for n in range(len(RING))]
MAXED = [READ[RING.index(("score", u, GH - 1, 1))] for u in range(UNITS)]
OUT_ITEM = [READ[RING.index(("out", u))] for u in range(UNITS)]



def kernel(**a):
    import numpy as np
    import concourse.bacc as bacc
    from concourse.bass_utils import run_bass_kernel_spmd as run

    a = {k: np.asarray(v) for k, v in a.items()}
    f32 = np.float32
    tiles = a["x"].reshape(NT, P, D).transpose(1, 0, 2)
    col = lambda n: a[n].reshape(D, 1)
    small = np.concatenate(
        [col("L0_xattn_bq"), col("L0_xattn_bk"), col("L0_xattn_bv"), col("L0_ffn_ln_w"), col("L0_ffn_ln_b"),
         col("L1_xattn_b_Q"), col("L1_xattn_b_K"), col("L1_xattn_b_V"),
         a["L0_ffn_b1s"].reshape(E0 * FC0, P).T, a["L0_ffn_gate_w"].T, a["L1_ffn_router_w"].T], axis=1)
    p = np.arange(P)
    heads = np.arange(H)
    wsel = np.zeros((P, PR0, 3, E0), f32)
    for c in range(PR0):
        for u in range(2):
            wsel[u * CAP0:(u + 1) * CAP0, c, :, 2 * c + u] = 1
    consts = np.concatenate(
        [np.eye(P, dtype=f32), (p[:, None] // DH == heads).astype(f32), (p[:, None] % H == heads).astype(f32),
         np.tile(np.arange(E1, 0, -1, dtype=f32), (P, 1)), wsel.reshape(P, -1),
         (p[:, None] < p[None, :]).astype(f32), np.tile(np.arange(1, CAP0 + 1, dtype=f32), (P, 1)),
         np.ones((P, P), f32)], axis=1)
    selq = np.zeros((P, 3, HPE, NROW), mybir.dt.np(BF16))
    for n, (i, j) in enumerate(TERMS):
        for h in range(HPE):
            for d in range(DH):
                selq[h * DH + d, i, h, n * DH + d] = 1
    b2 = np.repeat(a["L0_ffn_b2s"].reshape(PR0, 2, D).transpose(1, 0, 2), CAP0, axis=0)
    arrays = {
        "x": tiles, "small": small, "consts": consts, "selq": selq, "onerows": np.ones((2, H, NB * SK), mybir.dt.np(BF16)),
        "gates": np.tile(np.concatenate([a["g_xattn"], a["g_ffn"]]), (P, 1)),
        "rows": np.stack([a["L0_xattn_bo"], a["L1_xattn_b_O"]])[None],
        "ctxT": a["ctx_1024"].reshape(NB * SK, D).T,
        "w0": np.stack([a[f"L0_xattn_W{n}"].T for n in "qkvo"], axis=1),
        "w1": np.stack([a[f"L1_xattn_W_{n}"] for n in "QKVO"], axis=1),
        "fc1T": a["L0_ffn_fc1s"].transpose(2, 0, 1),
        "fc2": a["L0_ffn_fc2s"].transpose(2, 0, 1).reshape(FC0, P, E0, D).transpose(1, 2, 0, 3),
        "b2": b2,
        "shGU": np.stack([a["L1_ffn_shared_gate_w"].T, a["L1_ffn_shared_up_w"].T], axis=1),
        "shD": a["L1_ffn_shared_down_w"].T.reshape(SFC, P, D).transpose(1, 0, 2),
        "gateup": a["L1_ffn_gate_up_proj"].transpose(1, 0, 2),
        "down": a["L1_ffn_down_proj"].transpose(1, 0, 2),
    }
    nc = bacc.Bacc("TRN2", target_bir_lowering=False, num_devices=1)
    feed, aps = {}, {}
    for name, v in arrays.items():
        feed[f"in_{name}"] = np.ascontiguousarray(v)
        aps[name] = nc.dram_tensor(f"in_{name}", v.shape, mybir.dt.from_np(v.dtype), kind="ExternalInput").ap()
    kscr = nc.dram_tensor("k_parts", (P, 3, NB * SK), BF16).ap()
    qscr = nc.dram_tensor("q_parts", ((H - HPE) * DH, 3, T), BF16).ap()
    out = nc.dram_tensor("out", (P, NT, D), F32, kind="ExternalOutput").ap()
    build(nc, **aps, kscr=kscr, qscr=qscr, out=out)
    r = run(nc, [feed], core_ids=[0])
    got = r.results[0]["out"]
    return np.ascontiguousarray(np.asarray(got).transpose(1, 0, 2)).reshape(NB, SQ, D)
```
